# Optimizing a Trainium2 kernel written in Bass

```python
import numpy as np
import jax
import jax.numpy as jnp

def _softmax(x, axis=-1):
    return jax.nn.softmax(x, axis=axis)

def _gelu(x):
    return jax.nn.gelu(x, approximate=True)

def _silu(x):
    return jax.nn.silu(x)

def _sigmoid(x):
    return jax.nn.sigmoid(x)

def _layernorm(x, axis=-1, eps=1e-05):
    m = jnp.mean(x, axis=axis, keepdims=True)
    v = jnp.var(x, axis=axis, keepdims=True)
    return (x - m) / jnp.sqrt(v + eps)

def _scatter_add(tgt, idx, src, axis=0):
    return tgt.at[idx].add(src)

def _segment_sum(src, seg, n):
    return jax.ops.segment_sum(src, seg, n)
kernel_name = 'mk_xattn_ffn_d4_seqx_r8_e48c22'

def setup_inputs(seed: int=0):
    np.random.seed(seed)
    _w = jnp.asarray

    def _rec_inputs():
        import jax
        import jax.numpy as jnp
        _rk = jax.random.key(seed)
        x = -0.0002928 + 1 * jax.random.normal(jax.random.fold_in(_rk, 1), (128, 64, 128), jnp.float32)
        _lenS = 64 - jax.random.randint(jax.random.fold_in(_rk, 7), (128,), 0, max(1, 64 // 4) + 1, jnp.int32)
        _lenS2 = 64 - jax.random.randint(jax.random.fold_in(_rk, 8), (128,), 0, max(1, 64 // 4) + 1, jnp.int32)
        _ctx_1024P = jax.random.normal(jax.random.fold_in(_rk, 11), (128, 16, 128), jnp.float32)
        _ctx_1024c = jax.random.dirichlet(jax.random.fold_in(_rk, 511), 0.3 * jnp.ones((16,), jnp.float32), (128, 64))
        _ctx_1024t = jnp.einsum('bsk,bkd->bsd', _ctx_1024c, _ctx_1024P)
        _ctx_1024t = _ctx_1024t * jax.lax.rsqrt(jnp.mean(jnp.square(_ctx_1024t)) + 1e-12) * 0.953939
        ctx_1024 = -1.39393e-06 + 0.999914 * (_ctx_1024t + 0.3 * jax.random.normal(jax.random.fold_in(_rk, 611), (128, 64, 128), jnp.float32))
        _validS = jnp.arange(64)[None, :] < _lenS[:, None]
        _validS2 = jnp.arange(64)[None, :] < _lenS2[:, None]
        _causal = jnp.tril(jnp.ones((64, 64), dtype=bool))
        mask_Bx1xSxS2_ff0 = jnp.where(jnp.ones((128, 1, 64, 64), dtype=bool), 0.0, -1000000000.0).astype(jnp.float32)
        mask_SxS2_bk1 = jnp.broadcast_to(_validS2[0:1, :], (64, 64))
        return (x, ctx_1024, mask_Bx1xSxS2_ff0, mask_SxS2_bk1)
    x, ctx_1024, mask_Bx1xSxS2_ff0, mask_SxS2_bk1 = _rec_inputs()

    def _L0_xattn_setup():
        import jax, jax.numpy as jnp
        import numpy as np
        D_MODEL = 128
        N_HEADS = 16
        D_K = D_MODEL // N_HEADS
        key = jax.random.key(seed)
        ks = jax.random.split(key, 7)
        B, L = (1, 512)
        query = jax.random.normal(ks[0], (B, L, D_MODEL), dtype=jnp.float32)
        key_t = jax.random.normal(ks[1], (B, L, D_MODEL), dtype=jnp.float32)
        value = jax.random.normal(ks[2], (B, L, D_MODEL), dtype=jnp.float32)
        scale = 1.0 / np.sqrt(D_MODEL)
        w_q = jax.random.normal(ks[3], (D_MODEL, D_MODEL), dtype=jnp.float32) * scale
        w_k = jax.random.normal(ks[4], (D_MODEL, D_MODEL), dtype=jnp.float32) * scale
        w_v = jax.random.normal(ks[5], (D_MODEL, D_MODEL), dtype=jnp.float32) * scale
        w_o = jax.random.normal(ks[6], (D_MODEL, D_MODEL), dtype=jnp.float32) * scale
        return {'query': query, 'key': key_t, 'value': value, 'w_q': w_q, 'w_k': w_k, 'w_v': w_v, 'w_o': w_o}
    _L0_xattn_all = _L0_xattn_setup()
    _L0_xattn_in = {k: v for k, v in _L0_xattn_all.items() if k in ('w_q', 'w_k', 'w_v', 'w_o')}
    del _L0_xattn_all

    def _L0_ffn_setup():
        import jax, jax.numpy as jnp
        import numpy as np
        B, C, D, O = (4, 512, 128, 128)
        PROJ = 32
        RANKS = [1, 2, 4, 8]
        E = len(RANKS)
        CLAMP_MAX = float(np.log(1.0 / 0.01))

        def _l2norm(v, axis):
            return v / jnp.maximum(jnp.linalg.norm(v, axis=axis, keepdims=True), 1e-12)
        key = jax.random.key(seed)
        ks = jax.random.split(key, 16)
        inp = {'x': jax.random.normal(ks[0], (B, C, D), dtype=jnp.float32), 'W': jax.random.normal(ks[1], (O, D), dtype=jnp.float32) / np.sqrt(D), 'Wp': jax.random.normal(ks[2], (PROJ, D), dtype=jnp.float32) / np.sqrt(D), 'bp': jnp.zeros((PROJ,), dtype=jnp.float32), 'sim': jax.random.normal(ks[3], (PROJ, E), dtype=jnp.float32) * 0.01, 'temp': jnp.full((1,), np.log(1.0 / 0.5), dtype=jnp.float32)}
        for i, r in enumerate(RANKS):
            inp[f'Wd{i}'] = jax.random.normal(ks[4 + 2 * i], (r, D), dtype=jnp.float32) / r
            inp[f'Wu{i}'] = jax.random.normal(ks[5 + 2 * i], (O, r), dtype=jnp.float32) * 0.01
        return inp
    _L0_ffn_all = _L0_ffn_setup()
    _L0_ffn_in = {k: v for k, v in _L0_ffn_all.items() if k in ('W', 'Wp', 'bp', 'sim', 'temp', 'Wd0', 'Wu0', 'Wd1', 'Wu1', 'Wd2', 'Wu2', 'Wd3', 'Wu3')}
    del _L0_ffn_all

    def _L1_xattn_setup():
        import jax, jax.numpy as jnp
        import numpy as np
        EMBED_PHI = 128
        EMBED_F = 128
        HIDDEN_F = 128
        N_HEADS = 16
        B, S = (2, 256)
        key = jax.random.key(seed)
        ks = jax.random.split(key, 9)
        sphi = 1.0 / np.sqrt(EMBED_PHI)
        sf = 1.0 / np.sqrt(EMBED_F)
        sh = 1.0 / np.sqrt(HIDDEN_F)
        return {'q': jax.random.normal(ks[0], (B, S, EMBED_PHI), jnp.float32), 'k': jax.random.normal(ks[1], (B, S, EMBED_PHI), jnp.float32), 'v': jax.random.normal(ks[2], (B, S, EMBED_F), jnp.float32), 'Wq': jax.random.normal(ks[3], (HIDDEN_F, EMBED_PHI), jnp.float32) * sphi, 'Wk': jax.random.normal(ks[4], (HIDDEN_F, EMBED_PHI), jnp.float32) * sphi, 'Wv': jax.random.normal(ks[5], (HIDDEN_F, EMBED_F), jnp.float32) * sf, 'bv': jax.random.normal(ks[6], (HIDDEN_F,), jnp.float32) * sf, 'Wo': jax.random.normal(ks[7], (EMBED_F, HIDDEN_F), jnp.float32) * sh, 'bo': jax.random.normal(ks[8], (EMBED_F,), jnp.float32) * sh}
    _L1_xattn_all = _L1_xattn_setup()
    _L1_xattn_in = {k: v for k, v in _L1_xattn_all.items() if k in ('Wq', 'Wk', 'Wv', 'bv', 'Wo', 'bo')}
    del _L1_xattn_all

    def _L1_ffn_setup():
        import jax, jax.numpy as jnp
        import numpy as np
        N_EXPERTS = 16
        TOP_K = 4
        HIDDEN = 128
        INTER = 64
        B, S = (2, 128)
        key = jax.random.key(seed)
        k1, k2, k3, k4, k5 = jax.random.split(key, 5)
        return {'hidden_states': jax.random.normal(k1, (B, S, HIDDEN), dtype=jnp.float32), 'gate_w': jax.random.normal(k2, (N_EXPERTS, HIDDEN), dtype=jnp.float32) * 0.02, 'w1': jax.random.normal(k3, (N_EXPERTS, HIDDEN, INTER), dtype=jnp.float32) * 0.02, 'w3': jax.random.normal(k4, (N_EXPERTS, HIDDEN, INTER), dtype=jnp.float32) * 0.02, 'w2': jax.random.normal(k5, (N_EXPERTS, INTER, HIDDEN), dtype=jnp.float32) * 0.02}
    _L1_ffn_all = _L1_ffn_setup()
    _L1_ffn_in = {k: v for k, v in _L1_ffn_all.items() if k in ('gate_w', 'w1', 'w3', 'w2')}
    del _L1_ffn_all

    def _L2_xattn_setup():
        import jax, jax.numpy as jnp
        import numpy as np
        HIDDEN = 128
        HEADS = 16
        N, T1, T2 = (2, 256, 256)

        def _split_heads(x):
            n, t, e = x.shape
            return x.reshape(n, t, HEADS, e // HEADS).transpose(0, 2, 1, 3)
        key = jax.random.key(seed)
        k1, k2, k3, k4 = jax.random.split(key, 4)
        q = jax.random.normal(k1, (N, T1, HIDDEN), dtype=jnp.float32)
        encoder_k = jax.random.normal(k2, (N, T2, HIDDEN), dtype=jnp.float32)
        encoder_v = jax.random.normal(k3, (N, T2, HIDDEN), dtype=jnp.float32)
        encoder_attention_mask = jnp.zeros((N, 1, T2, T2), dtype=jnp.float32)
        wo_w = jax.random.normal(k4, (HIDDEN, HIDDEN), dtype=jnp.float32) * (1.0 / np.sqrt(HIDDEN))
        wo_b = jnp.zeros((HIDDEN,), dtype=jnp.float32)
        return {'q': q, 'encoder_k': encoder_k, 'encoder_v': encoder_v, 'encoder_attention_mask': encoder_attention_mask, 'wo_w': wo_w, 'wo_b': wo_b}
    _L2_xattn_all = _L2_xattn_setup()
    _L2_xattn_in = {k: v for k, v in _L2_xattn_all.items() if k in ('wo_w', 'wo_b')}
    del _L2_xattn_all

    def _L2_ffn_setup():
        import jax, jax.numpy as jnp
        import numpy as np
        DIM = 128

        def _reference_tuple_inner(x, W_r, W_k, W_v, mu_r, mu_k):
            B, T, C = x.shape
            x_prev = jnp.concatenate([jnp.zeros((B, 1, C), x.dtype), x[:, :-1, :]], axis=1)
            xr = mu_r * x + (1.0 - mu_r) * x_prev
            xk = mu_k * x + (1.0 - mu_k) * x_prev
            r = jax.nn.sigmoid(jnp.einsum('btc,dc->btd', xr, W_r))
            k = jnp.einsum('btc,dc->btd', xk, W_k)
            k_act = jnp.square(jax.nn.relu(k))
            out = r * jnp.einsum('btc,dc->btd', k_act, W_v)
            new_state = x[:, -1, :]
            return (out, new_state)
        key = jax.random.key(seed)
        ks = jax.random.split(key, 6)
        B, T, C = (8, 256, DIM)
        x = jax.random.normal(ks[0], (B, T, C), dtype=jnp.float32)
        s = 1.0 / np.sqrt(C)
        W_r = jax.random.uniform(ks[1], (C, C), jnp.float32, -s, s)
        W_k = jax.random.uniform(ks[2], (C, C), jnp.float32, -s, s)
        W_v = jax.random.uniform(ks[3], (C, C), jnp.float32, -s, s)
        mu_r = jax.random.uniform(ks[4], (C,), jnp.float32)
        mu_k = jax.random.uniform(ks[5], (C,), jnp.float32)
        return {'x': x, 'W_r': W_r, 'W_k': W_k, 'W_v': W_v, 'mu_r': mu_r, 'mu_k': mu_k}
    _L2_ffn_all = _L2_ffn_setup()
    _L2_ffn_in = {k: v for k, v in _L2_ffn_all.items() if k in ('W_r', 'W_k', 'W_v', 'mu_r', 'mu_k')}
    del _L2_ffn_all

    def _L3_xattn_setup():
        import jax, jax.numpy as jnp
        import numpy as np
        D = 128
        H = 16
        HD = D // H
        SCALE = 1.0 / np.sqrt(HD)

        def _split_heads(x):
            B, S, _ = x.shape
            return x.reshape(B, S, H, HD).transpose(0, 2, 1, 3)
        key = jax.random.key(seed)
        ks = jax.random.split(key, 12)
        B, S = (4, 256)
        inp = {'queries': jax.random.normal(ks[0], (B, S, D), jnp.float32), 'keys': jax.random.normal(ks[1], (B, S, D), jnp.float32), 'values': jax.random.normal(ks[2], (B, S, D), jnp.float32), 'mask': jax.random.randint(ks[3], (S, S), 0, 2).astype(bool), 'Wq': jax.random.normal(ks[4], (D, D), jnp.float32) * 0.02, 'bq': jax.random.normal(ks[5], (D,), jnp.float32) * 0.02, 'Wk': jax.random.normal(ks[6], (D, D), jnp.float32) * 0.02, 'bk': jax.random.normal(ks[7], (D,), jnp.float32) * 0.02, 'Wv': jax.random.normal(ks[8], (D, D), jnp.float32) * 0.02, 'bv': jax.random.normal(ks[9], (D,), jnp.float32) * 0.02, 'Wo': jax.random.normal(ks[10], (D, D), jnp.float32) * 0.02, 'bo': jax.random.normal(ks[11], (D,), jnp.float32) * 0.02}
        return inp
    _L3_xattn_all = _L3_xattn_setup()
    _L3_xattn_in = {k: v for k, v in _L3_xattn_all.items() if k in ('Wq', 'bq', 'Wk', 'bk', 'Wv', 'bv', 'Wo', 'bo')}
    del _L3_xattn_all

    def _L3_ffn_setup():
        import jax, jax.numpy as jnp
        import numpy as np
        DIM = 128
        DEPTH = 2
        HEADS = 8
        DIM_HEAD = 64
        WINDOW = 64
        INNER = HEADS * DIM_HEAD
        HID = int(DIM * 4 * 2 / 3)
        B, N = (2, 1024)
        QK_SCALE = 8.0

        def shift_token(t):
            t1, t2 = jnp.split(t, 2, axis=-1)
            t2 = jnp.pad(t2, ((0, 0), (1, 0), (0, 0)))[:, :-1]
            return jnp.concatenate([t1, t2], axis=-1)

        def l2norm(t):
            return t / jnp.clip(jnp.linalg.norm(t, axis=-1, keepdims=True), 1e-12)

        def rotate_half(x):
            x1, x2 = jnp.split(x, 2, axis=-1)
            return jnp.concatenate([-x2, x1], axis=-1)

        def rotary_xpos(q, k):
            n = q.shape[-2]
            half_idx = jnp.arange(0, DIM_HEAD, 2, dtype=jnp.float32)
            inv_freq = 1.0 / 10000.0 ** (half_idx / DIM_HEAD)
            t = jnp.arange(n, dtype=jnp.float32)
            freqs = t[:, None] * inv_freq[None, :]
            freqs = jnp.concatenate([freqs, freqs], axis=-1)
            base = (half_idx + 0.4 * DIM_HEAD) / (1.4 * DIM_HEAD)
            power = (t - n // 2) / float(WINDOW // 2)
            scale = base[None, :] ** power[:, None]
            scale = jnp.concatenate([scale, scale], axis=-1)
            cos, sin = (jnp.cos(freqs), jnp.sin(freqs))
            q = q * cos * scale + rotate_half(q) * sin * scale
            k = k * cos / scale + rotate_half(k) * sin / scale
            return (q, k)

        def local_attention(q, k, v):
            b, h, n, d = q.shape
            w = n // WINDOW
            bq = q.reshape(b, h, w, WINDOW, d) * QK_SCALE
            bk = k.reshape(b, h, w, WINDOW, d)
            bv = v.reshape(b, h, w, WINDOW, d)

            def look_around(t):
                p = jnp.pad(t, ((0, 0), (0, 0), (1, 0), (0, 0), (0, 0)))
                return jnp.concatenate([p[:, :, :w], p[:, :, 1:]], axis=3)
            bk, bv = (look_around(bk), look_around(bv))
            bt = jnp.arange(n).reshape(w, WINDOW)
            btp = jnp.pad(bt, ((1, 0), (0, 0)), constant_values=-1)
            btk = jnp.concatenate([btp[:w], btp[1:]], axis=1)
            sim = jnp.einsum('bhwid,bhwjd->bhwij', bq, bk)
            i = bt[:, :, None]
            j = btk[:, None, :]
            mask = (i < j) | (i > j + WINDOW) | (j == -1)
            sim = jnp.where(mask, -jnp.finfo(sim.dtype).max, sim)
            attn = jax.nn.softmax(sim, axis=-1)
            out = jnp.einsum('bhwij,bhwjd->bhwid', attn, bv)
            return out.reshape(b, h, n, d)

        def _layer(x, wqkv, qs, ksc, wo, lg, lb, w1, b1, w2, b2):
            b, n, _ = x.shape
            h = shift_token(x)
            qkv = h @ wqkv
            q, k, v = jnp.split(qkv, 3, axis=-1)
            to_heads = lambda t: t.reshape(b, n, HEADS, DIM_HEAD).transpose(0, 2, 1, 3)
            q, k, v = (to_heads(q), to_heads(k), to_heads(v))
            q = l2norm(q) * qs
            k = l2norm(k) * ksc
            q, k = rotary_xpos(q, k)
            o = local_attention(q, k, v)
            o = o.transpose(0, 2, 1, 3).reshape(b, n, INNER)
            x = x + o @ wo
            h = shift_token(x)
            mu = h.mean(-1, keepdims=True)
            var = h.var(-1, keepdims=True)
            h = (h - mu) / jnp.sqrt(var + 1e-05) * lg + lb
            h = h @ w1 + b1
            a, g = jnp.split(h, 2, axis=-1)
            h = a * jax.nn.gelu(g, approximate=False)
            x = x + h @ w2 + b2
            return x
        key = jax.random.key(seed)
        ks = jax.random.split(key, 6)
        return {'x': jax.random.normal(ks[0], (B, N, DIM), jnp.float32), 'wqkv': jax.random.normal(ks[1], (DEPTH, DIM, 3 * INNER), jnp.float32) * 0.02, 'q_scale': jnp.ones((DEPTH, DIM_HEAD), jnp.float32), 'k_scale': jnp.ones((DEPTH, DIM_HEAD), jnp.float32), 'wo': jax.random.normal(ks[2], (DEPTH, INNER, DIM), jnp.float32) * 0.02, 'ln_g': jnp.ones((DEPTH, DIM), jnp.float32), 'ln_b': jnp.zeros((DEPTH, DIM), jnp.float32), 'w1': jax.random.normal(ks[3], (DEPTH, DIM, 2 * HID), jnp.float32) * 0.02, 'b1': jnp.zeros((DEPTH, 2 * HID), jnp.float32), 'w2': jax.random.normal(ks[4], (DEPTH, HID, DIM), jnp.float32) * 0.02, 'b2': jnp.zeros((DEPTH, DIM), jnp.float32)}
    _L3_ffn_all = _L3_ffn_setup()
    _L3_ffn_in = {k: v for k, v in _L3_ffn_all.items() if k in ('wqkv', 'q_scale', 'k_scale', 'wo', 'ln_g', 'ln_b', 'w1', 'b1', 'w2', 'b2')}
    del _L3_ffn_all
    return {'x': x, 'ctx_1024': ctx_1024, 'mask_Bx1xSxS2_ff0': mask_Bx1xSxS2_ff0, 'mask_SxS2_bk1': mask_SxS2_bk1, 'L0_xattn_w_q': _L0_xattn_in['w_q'], 'L0_xattn_w_k': _L0_xattn_in['w_k'], 'L0_xattn_w_v': _L0_xattn_in['w_v'], 'L0_xattn_w_o': _L0_xattn_in['w_o'], 'L0_ffn_W': _L0_ffn_in['W'], 'L0_ffn_Wp': _L0_ffn_in['Wp'], 'L0_ffn_bp': _L0_ffn_in['bp'], 'L0_ffn_sim': _L0_ffn_in['sim'], 'L0_ffn_temp': _L0_ffn_in['temp'], 'L0_ffn_Wd0': _L0_ffn_in['Wd0'], 'L0_ffn_Wu0': _L0_ffn_in['Wu0'], 'L0_ffn_Wd1': _L0_ffn_in['Wd1'], 'L0_ffn_Wu1': _L0_ffn_in['Wu1'], 'L0_ffn_Wd2': _L0_ffn_in['Wd2'], 'L0_ffn_Wu2': _L0_ffn_in['Wu2'], 'L0_ffn_Wd3': _L0_ffn_in['Wd3'], 'L0_ffn_Wu3': _L0_ffn_in['Wu3'], 'L1_xattn_Wq': _L1_xattn_in['Wq'], 'L1_xattn_Wk': _L1_xattn_in['Wk'], 'L1_xattn_Wv': _L1_xattn_in['Wv'], 'L1_xattn_bv': _L1_xattn_in['bv'], 'L1_xattn_Wo': _L1_xattn_in['Wo'], 'L1_xattn_bo': _L1_xattn_in['bo'], 'L1_ffn_gate_w': _L1_ffn_in['gate_w'], 'L1_ffn_w1': _L1_ffn_in['w1'], 'L1_ffn_w3': _L1_ffn_in['w3'], 'L1_ffn_w2': _L1_ffn_in['w2'], 'L2_xattn_wo_w': _L2_xattn_in['wo_w'], 'L2_xattn_wo_b': _L2_xattn_in['wo_b'], 'L2_ffn_W_r': _L2_ffn_in['W_r'], 'L2_ffn_W_k': _L2_ffn_in['W_k'], 'L2_ffn_W_v': _L2_ffn_in['W_v'], 'L2_ffn_mu_r': _L2_ffn_in['mu_r'], 'L2_ffn_mu_k': _L2_ffn_in['mu_k'], 'L3_xattn_Wq': _L3_xattn_in['Wq'], 'L3_xattn_bq': _L3_xattn_in['bq'], 'L3_xattn_Wk': _L3_xattn_in['Wk'], 'L3_xattn_bk': _L3_xattn_in['bk'], 'L3_xattn_Wv': _L3_xattn_in['Wv'], 'L3_xattn_bv': _L3_xattn_in['bv'], 'L3_xattn_Wo': _L3_xattn_in['Wo'], 'L3_xattn_bo': _L3_xattn_in['bo'], 'L3_ffn_wqkv': _L3_ffn_in['wqkv'], 'L3_ffn_q_scale': _L3_ffn_in['q_scale'], 'L3_ffn_k_scale': _L3_ffn_in['k_scale'], 'L3_ffn_wo': _L3_ffn_in['wo'], 'L3_ffn_ln_g': _L3_ffn_in['ln_g'], 'L3_ffn_ln_b': _L3_ffn_in['ln_b'], 'L3_ffn_w1': _L3_ffn_in['w1'], 'L3_ffn_b1': _L3_ffn_in['b1'], 'L3_ffn_w2': _L3_ffn_in['w2'], 'L3_ffn_b2': _L3_ffn_in['b2']}

def reference(x, ctx_1024, mask_Bx1xSxS2_ff0, mask_SxS2_bk1, L0_xattn_w_q, L0_xattn_w_k, L0_xattn_w_v, L0_xattn_w_o, L0_ffn_W, L0_ffn_Wp, L0_ffn_bp, L0_ffn_sim, L0_ffn_temp, L0_ffn_Wd0, L0_ffn_Wu0, L0_ffn_Wd1, L0_ffn_Wu1, L0_ffn_Wd2, L0_ffn_Wu2, L0_ffn_Wd3, L0_ffn_Wu3, L1_xattn_Wq, L1_xattn_Wk, L1_xattn_Wv, L1_xattn_bv, L1_xattn_Wo, L1_xattn_bo, L1_ffn_gate_w, L1_ffn_w1, L1_ffn_w3, L1_ffn_w2, L2_xattn_wo_w, L2_xattn_wo_b, L2_ffn_W_r, L2_ffn_W_k, L2_ffn_W_v, L2_ffn_mu_r, L2_ffn_mu_k, L3_xattn_Wq, L3_xattn_bq, L3_xattn_Wk, L3_xattn_bk, L3_xattn_Wv, L3_xattn_bv, L3_xattn_Wo, L3_xattn_bo, L3_ffn_wqkv, L3_ffn_q_scale, L3_ffn_k_scale, L3_ffn_wo, L3_ffn_ln_g, L3_ffn_ln_b, L3_ffn_w1, L3_ffn_b1, L3_ffn_w2, L3_ffn_b2):
    import jax
    import jax.numpy as jnp

    def _L0_xattn_ref(query, key, value, w_q, w_k, w_v, w_o):
        import jax, jax.numpy as jnp
        import numpy as np
        D_MODEL = 128
        N_HEADS = 16
        D_K = D_MODEL // N_HEADS
        B, L, _ = query.shape
        Q = (query @ w_q.T).reshape(B, L, N_HEADS, D_K).transpose(0, 2, 1, 3)
        K = (key @ w_k.T).reshape(B, L, N_HEADS, D_K).transpose(0, 2, 1, 3)
        V = (value @ w_v.T).reshape(B, L, N_HEADS, D_K).transpose(0, 2, 1, 3)
        scores = jnp.einsum('bhqd,bhkd->bhqk', Q, K) / jnp.sqrt(jnp.float32(D_K))
        attn = jax.nn.softmax(scores, axis=-1)
        out = jnp.einsum('bhqk,bhkd->bhqd', attn, V)
        out = out.transpose(0, 2, 1, 3).reshape(B, L, D_MODEL)
        return out @ w_o.T

    def _L0_ffn_ref(x, W, Wp, bp, sim, temp, Wd0, Wu0, Wd1, Wu1, Wd2, Wu2, Wd3, Wu3):
        import jax, jax.numpy as jnp
        import numpy as np
        B, C, D, O = (4, 512, 128, 128)
        PROJ = 32
        RANKS = [1, 2, 4, 8]
        E = len(RANKS)
        CLAMP_MAX = float(np.log(1.0 / 0.01))

        def _l2norm(v, axis):
            return v / jnp.maximum(jnp.linalg.norm(v, axis=axis, keepdims=True), 1e-12)
        base = jnp.einsum('bcd,od->bco', x, W)
        xf = x.reshape(-1, x.shape[-1])
        proj = _l2norm(xf @ Wp.T + bp, axis=1)
        simn = _l2norm(sim, axis=0)
        scale = jnp.exp(jnp.minimum(temp, CLAMP_MAX))
        logits = proj @ simn * scale
        lw = jax.nn.softmax(logits, axis=1)
        top1 = jnp.argmax(lw, axis=1)
        ret = jnp.where(jnp.arange(E)[None, :] == top1[:, None], lw, 0.0)
        ret = ret.reshape(x.shape[0], x.shape[1], E)
        downs = (Wd0, Wd1, Wd2, Wd3)
        ups = (Wu0, Wu1, Wu2, Wu3)
        l = jnp.stack([jnp.einsum('bcr,or->bco', jnp.einsum('bcd,rd->bcr', x, d), u) for d, u in zip(downs, ups)], axis=2)
        res = jnp.sum(ret[..., None] * l, axis=2)
        return base + res

    def _L1_xattn_ref(q, k, v, Wq, Wk, Wv, bv, Wo, bo):
        import jax, jax.numpy as jnp
        import numpy as np
        EMBED_PHI = 128
        EMBED_F = 128
        HIDDEN_F = 128
        N_HEADS = 16
        B, S = (2, 256)
        Bq, Sq, _ = q.shape
        hd = HIDDEN_F // N_HEADS
        scale = 1.0 / np.sqrt(hd)
        qh = (q @ Wq.T).reshape(Bq, Sq, N_HEADS, hd).transpose(0, 2, 1, 3)
        kh = (k @ Wk.T).reshape(Bq, Sq, N_HEADS, hd).transpose(0, 2, 1, 3)
        vh = (v @ Wv.T + bv).reshape(Bq, Sq, N_HEADS, hd).transpose(0, 2, 1, 3)
        scores = jnp.einsum('bhsd,bhtd->bhst', qh, kh) * scale
        mask = jnp.triu(jnp.ones((Sq, Sq), dtype=bool), k=0).at[0, 0].set(False)
        scores = jnp.where(mask, -jnp.inf, scores)
        probs = jax.nn.softmax(scores, axis=-1)
        out = jnp.einsum('bhst,bhtd->bhsd', probs, vh)
        out = out.transpose(0, 2, 1, 3).reshape(Bq, Sq, HIDDEN_F)
        return out @ Wo.T + bo

    def _L1_ffn_ref(hidden_states, gate_w, w1, w3, w2):
        import jax, jax.numpy as jnp
        import numpy as np
        N_EXPERTS = 16
        TOP_K = 4
        HIDDEN = 128
        INTER = 64
        B, S = (2, 128)
        'DeepseekV3 MoE adapter forward: router -> sparse scores -> expert GLU MLP -> combine.'
        b, s, h = hidden_states.shape
        x = hidden_states.reshape(-1, h)
        logits = jnp.einsum('th,eh->te', x, gate_w)
        probs = jax.nn.softmax(logits, axis=-1)
        topk_w, topk_idx = jax.lax.top_k(probs, TOP_K)
        topk_w = topk_w / jnp.sum(topk_w, axis=-1, keepdims=True)
        one_hot = (topk_idx[..., None] == jnp.arange(N_EXPERTS)).astype(topk_w.dtype)
        scores = jnp.einsum('tk,tke->te', topk_w, one_hot)
        g = jnp.einsum('th,ehi->tei', x, w1)
        u = jnp.einsum('th,ehi->tei', x, w3)
        act = jax.nn.silu(g) * u
        expert_out = jnp.einsum('tei,eih->teh', act, w2)
        out = jnp.einsum('teh,te->th', expert_out, scores)
        return out.reshape(b, s, h)

    def _L2_xattn_ref(q, encoder_k, encoder_v, encoder_attention_mask, wo_w, wo_b):
        import jax, jax.numpy as jnp
        import numpy as np
        HIDDEN = 128
        HEADS = 16
        N, T1, T2 = (2, 256, 256)

        def _split_heads(x):
            n, t, e = x.shape
            return x.reshape(n, t, HEADS, e // HEADS).transpose(0, 2, 1, 3)
        qh = _split_heads(q)
        kh = _split_heads(encoder_k)
        vh = _split_heads(encoder_v)
        scores = jnp.einsum('bhqd,bhkd->bhqk', qh, kh) + encoder_attention_mask
        weights = jax.nn.softmax(scores, axis=-1)
        ctx = jnp.einsum('bhqk,bhkd->bhqd', weights, vh)
        ctx = ctx.transpose(0, 2, 1, 3).reshape(q.shape[0], q.shape[1], -1)
        return jax.nn.relu(ctx @ wo_w.T + wo_b)

    def _L2_ffn_ref(x, W_r, W_k, W_v, mu_r, mu_k):
        import jax, jax.numpy as jnp
        import numpy as np
        DIM = 128

        def _reference_tuple_inner(x, W_r, W_k, W_v, mu_r, mu_k):
            B, T, C = x.shape
            x_prev = jnp.concatenate([jnp.zeros((B, 1, C), x.dtype), x[:, :-1, :]], axis=1)
            xr = mu_r * x + (1.0 - mu_r) * x_prev
            xk = mu_k * x + (1.0 - mu_k) * x_prev
            r = jax.nn.sigmoid(jnp.einsum('btc,dc->btd', xr, W_r))
            k = jnp.einsum('btc,dc->btd', xk, W_k)
            k_act = jnp.square(jax.nn.relu(k))
            out = r * jnp.einsum('btc,dc->btd', k_act, W_v)
            new_state = x[:, -1, :]
            return (out, new_state)
        return _reference_tuple_inner(x, W_r, W_k, W_v, mu_r, mu_k)[0]

    def _L3_xattn_ref(queries, keys, values, mask, Wq, bq, Wk, bk, Wv, bv, Wo, bo):
        import jax, jax.numpy as jnp
        import numpy as np
        D = 128
        H = 16
        HD = D // H
        SCALE = 1.0 / np.sqrt(HD)

        def _split_heads(x):
            B, S, _ = x.shape
            return x.reshape(B, S, H, HD).transpose(0, 2, 1, 3)
        q = _split_heads(queries @ Wq + bq)
        k = _split_heads(keys @ Wk + bk)
        v = _split_heads(values @ Wv + bv)
        scores = jnp.einsum('bhqd,bhkd->bhqk', q, k) * SCALE
        neg = jnp.finfo(scores.dtype).min
        scores = jnp.where(mask[None, None, :, :], scores, neg)
        probs = jax.nn.softmax(scores, axis=-1)
        ctx = jnp.einsum('bhqk,bhkd->bhqd', probs, v)
        B, _, Sq, _ = ctx.shape
        combined = ctx.transpose(0, 2, 1, 3).reshape(B, Sq, D)
        return combined @ Wo + bo

    def _L3_ffn_ref(x, wqkv, q_scale, k_scale, wo, ln_g, ln_b, w1, b1, w2, b2):
        import jax, jax.numpy as jnp
        import numpy as np
        DIM = 128
        DEPTH = 2
        HEADS = 8
        DIM_HEAD = 64
        WINDOW = 64
        INNER = HEADS * DIM_HEAD
        HID = int(DIM * 4 * 2 / 3)
        B, N = (2, 1024)
        QK_SCALE = 8.0

        def shift_token(t):
            t1, t2 = jnp.split(t, 2, axis=-1)
            t2 = jnp.pad(t2, ((0, 0), (1, 0), (0, 0)))[:, :-1]
            return jnp.concatenate([t1, t2], axis=-1)

        def l2norm(t):
            return t / jnp.clip(jnp.linalg.norm(t, axis=-1, keepdims=True), 1e-12)

        def rotate_half(x):
            x1, x2 = jnp.split(x, 2, axis=-1)
            return jnp.concatenate([-x2, x1], axis=-1)

        def rotary_xpos(q, k):
            n = q.shape[-2]
            half_idx = jnp.arange(0, DIM_HEAD, 2, dtype=jnp.float32)
            inv_freq = 1.0 / 10000.0 ** (half_idx / DIM_HEAD)
            t = jnp.arange(n, dtype=jnp.float32)
            freqs = t[:, None] * inv_freq[None, :]
            freqs = jnp.concatenate([freqs, freqs], axis=-1)
            base = (half_idx + 0.4 * DIM_HEAD) / (1.4 * DIM_HEAD)
            power = (t - n // 2) / float(WINDOW // 2)
            scale = base[None, :] ** power[:, None]
            scale = jnp.concatenate([scale, scale], axis=-1)
            cos, sin = (jnp.cos(freqs), jnp.sin(freqs))
            q = q * cos * scale + rotate_half(q) * sin * scale
            k = k * cos / scale + rotate_half(k) * sin / scale
            return (q, k)

        def local_attention(q, k, v):
            b, h, n, d = q.shape
            w = n // WINDOW
            bq = q.reshape(b, h, w, WINDOW, d) * QK_SCALE
            bk = k.reshape(b, h, w, WINDOW, d)
            bv = v.reshape(b, h, w, WINDOW, d)

            def look_around(t):
                p = jnp.pad(t, ((0, 0), (0, 0), (1, 0), (0, 0), (0, 0)))
                return jnp.concatenate([p[:, :, :w], p[:, :, 1:]], axis=3)
            bk, bv = (look_around(bk), look_around(bv))
            bt = jnp.arange(n).reshape(w, WINDOW)
            btp = jnp.pad(bt, ((1, 0), (0, 0)), constant_values=-1)
            btk = jnp.concatenate([btp[:w], btp[1:]], axis=1)
            sim = jnp.einsum('bhwid,bhwjd->bhwij', bq, bk)
            i = bt[:, :, None]
            j = btk[:, None, :]
            mask = (i < j) | (i > j + WINDOW) | (j == -1)
            sim = jnp.where(mask, -jnp.finfo(sim.dtype).max, sim)
            attn = jax.nn.softmax(sim, axis=-1)
            out = jnp.einsum('bhwij,bhwjd->bhwid', attn, bv)
            return out.reshape(b, h, n, d)

        def _layer(x, wqkv, qs, ksc, wo, lg, lb, w1, b1, w2, b2):
            b, n, _ = x.shape
            h = shift_token(x)
            qkv = h @ wqkv
            q, k, v = jnp.split(qkv, 3, axis=-1)
            to_heads = lambda t: t.reshape(b, n, HEADS, DIM_HEAD).transpose(0, 2, 1, 3)
            q, k, v = (to_heads(q), to_heads(k), to_heads(v))
            q = l2norm(q) * qs
            k = l2norm(k) * ksc
            q, k = rotary_xpos(q, k)
            o = local_attention(q, k, v)
            o = o.transpose(0, 2, 1, 3).reshape(b, n, INNER)
            x = x + o @ wo
            h = shift_token(x)
            mu = h.mean(-1, keepdims=True)
            var = h.var(-1, keepdims=True)
            h = (h - mu) / jnp.sqrt(var + 1e-05) * lg + lb
            h = h @ w1 + b1
            a, g = jnp.split(h, 2, axis=-1)
            h = a * jax.nn.gelu(g, approximate=False)
            x = x + h @ w2 + b2
            return x
        for l in range(DEPTH):
            x = _layer(x, wqkv[l], q_scale[l], k_scale[l], wo[l], ln_g[l], ln_b[l], w1[l], b1[l], w2[l], b2[l])
        return x
    x = x + _L0_xattn_ref(_layernorm(x, axis=-1), ctx_1024, ctx_1024, L0_xattn_w_q, L0_xattn_w_k, L0_xattn_w_v, L0_xattn_w_o)
    x = x + _L0_ffn_ref(_layernorm(x, axis=-1), L0_ffn_W, L0_ffn_Wp, L0_ffn_bp, L0_ffn_sim, L0_ffn_temp, L0_ffn_Wd0, L0_ffn_Wu0, L0_ffn_Wd1, L0_ffn_Wu1, L0_ffn_Wd2, L0_ffn_Wu2, L0_ffn_Wd3, L0_ffn_Wu3)
    x = x + _L1_xattn_ref(_layernorm(x, axis=-1), ctx_1024, ctx_1024, L1_xattn_Wq, L1_xattn_Wk, L1_xattn_Wv, L1_xattn_bv, L1_xattn_Wo, L1_xattn_bo)
    x = x + _L1_ffn_ref(_layernorm(x, axis=-1), L1_ffn_gate_w, L1_ffn_w1, L1_ffn_w3, L1_ffn_w2)
    x = x + _L2_xattn_ref(_layernorm(x, axis=-1), ctx_1024, ctx_1024, mask_Bx1xSxS2_ff0, L2_xattn_wo_w, L2_xattn_wo_b)
    x = x + _L2_ffn_ref(_layernorm(x, axis=-1), L2_ffn_W_r, L2_ffn_W_k, L2_ffn_W_v, L2_ffn_mu_r, L2_ffn_mu_k)
    x = x + _L3_xattn_ref(_layernorm(x, axis=-1), ctx_1024, ctx_1024, mask_SxS2_bk1, L3_xattn_Wq, L3_xattn_bq, L3_xattn_Wk, L3_xattn_bk, L3_xattn_Wv, L3_xattn_bv, L3_xattn_Wo, L3_xattn_bo)
    x = x + _L3_ffn_ref(_layernorm(x, axis=-1), L3_ffn_wqkv, L3_ffn_q_scale, L3_ffn_k_scale, L3_ffn_wo, L3_ffn_ln_g, L3_ffn_ln_b, L3_ffn_w1, L3_ffn_b1, L3_ffn_w2, L3_ffn_b2)
    return x

_drawn_inputs = setup_inputs


def setup_inputs(seed=0):
    import zlib

    import numpy as np

    out = dict(_drawn_inputs(seed))
    spreads = {'L0_ffn_bp': (0.0, 0.8),
     'L2_xattn_wo_b': (0.0, 0.1),
     'L3_ffn_q_scale': (1.0, 0.6),
     'L3_ffn_k_scale': (1.0, 0.6),
     'L3_ffn_ln_g': (1.0, 0.6),
     'L3_ffn_ln_b': (0.0, 0.8),
     'L3_ffn_b1': (0.0, 0.8),
     'L3_ffn_b2': (0.0, 0.8)}
    factors = {'L0_ffn_Wp': 3.505,
     'L0_ffn_sim': 3.395,
     'L0_ffn_Wd0': 3.941,
     'L0_ffn_Wu0': 3.8,
     'L0_ffn_Wd1': 6.331,
     'L0_ffn_Wu1': 6.392,
     'L0_ffn_Wd2': 8.0,
     'L0_ffn_Wu2': 8.0,
     'L0_ffn_Wd3': 8.0,
     'L0_ffn_Wu3': 8.0,
     'L1_ffn_gate_w': 8.0,
     'L1_ffn_w1': 8.0,
     'L1_ffn_w3': 8.0,
     'L1_ffn_w2': 8.0,
     'L2_ffn_W_r': 4.752,
     'L2_ffn_mu_r': 8.0,
     'L3_xattn_Wq': 8.0,
     'L3_xattn_bq': 8.0,
     'L3_xattn_Wk': 8.0,
     'L3_xattn_bk': 64.0,
     'L3_xattn_Wv': 3.788,
     'L3_xattn_bv': 8.0,
     'L3_xattn_Wo': 3.751,
     'L3_xattn_bo': 4.627,
     'L3_ffn_w1': 8.0,
     'L3_ffn_w2': 8.0}
    for name, (base, spread) in spreads.items():
        noise = np.random.default_rng([zlib.crc32(name.encode()), seed]).standard_normal(out[name].shape)
        drawn = base * np.exp(spread * noise) if base else spread * noise
        out[name] = jnp.asarray(drawn.astype(out[name].dtype))
    for name, factor in factors.items():
        out[name] = (out[name] * factor).astype(out[name].dtype)
    return out
```

```python
from contextlib import ExitStack

import numpy as np
import concourse.bass as bass
from concourse import mybir

F32 = mybir.dt.float32
ACT = mybir.ActivationFunctionType
ALU = mybir.AluOpType
AX = mybir.AxisListType.X

P = 128
S = 64
NSEQ = 128
TILES = NSEQ * S // P
GT = 4
GROUPS = TILES // GT
GTOK = GT * P
GSEQ = GTOK // S
HEADS = 16
HD = P // HEADS
PAIRS = HEADS // 2
VC = HD + 1
LN_EPS = 1e-5
PROJ, RANKS = 32, (1, 2, 4, 8)
NLR, RSUM = len(RANKS), sum(RANKS)
ROUTE = PROJ + NLR + RSUM
LOG_SCALE = 20
EXPERTS, INTER, TOPK = 16, 64, 4
EC = EXPERTS * INTER // P
LHEADS, LD, LPAIRS = 8, 64, 4
INNER = LHEADS * LD
HALF = LD // 2
DEPTH = 2
HID = 341
HC = [(c * P, min(P, HID - c * P)) for c in range((HID + P - 1) // P)]
GROUP_SIGNALS = """
a_in_psum added blended bn_done c_loaded chain damped exp_ready expo_ready g_in_psum gated
gates_in_psum gates_ready gates_t_ready gelu_done hidden_in_psum k_copied k_in_psum k_placed
kt_ready l_newton l_root l_squared ln_ready logit_ready lv_in_psum m_loaded mask_added max_ready
mixed newton norm_ready norms o_ready ot_in_psum ot_ready picked products pt_high pt_low q_copied
q_in_psum qk_in_psum qk_turned qt_ready r0_ready rec_ready relu_done rk_in_psum root_steps rotated
route_in_psum router_copied scored shift_loaded shifted sig silu_done squared stored summed
sums_ready times_up top_ready turned unit unparked v_copied v_done v_even v_in_psum v_odd var_ready
weighted x_loaded x_norm_ready xt_in_psum xt_ready y_done y_ready""".split()
NEG = -(2.0 ** 100)


class Signal:

    def __init__(self, sem):
        self.sem, self.base, self.per, self.ahead = sem, 0, 0, 0

    def opens(self, per, ahead=0):
        self.per, self.ahead = per, ahead

    def closes(self, groups):
        self.base += self.per * groups + self.ahead
        self.per = self.ahead = 0

    def at(self, g, k):
        return g * self.per + (self.base + k)


def build_program(nc, w, x_in, ctx_t, mask_l2, mask_l3, out):
    with ExitStack() as ctx:
        def sb(name, shape, dt=F32):
            return ctx.enter_context(nc.sbuf_tensor(name, shape, dt))

        signals = {}

        def signal(name, per=0, ahead=0):
            if name not in signals:
                assert per == 0 or name in GROUP_SIGNALS, name
                signals[name] = Signal(ctx.enter_context(nc.semaphore(name)))
            signals[name].opens(per, ahead)
            return signals[name]

        def close_stage(groups=GROUPS):
            for s in signals.values():
                s.closes(groups)

        for n in GROUP_SIGNALS:
            signal(n).base = 1

        x = sb("x", [P, TILES, P])
        ident = sb("ident", [P, P])
        ones = sb("ones", [P, P])
        attn_w = {n: sb("w_" + n, [P, P]) for n in (
            "L0_q", "L0_k", "L0_v", "L0_o", "L1_q", "L1_k", "L1_v", "L1_o", "L2_o",
            "L3_q", "L3_k", "L3_v", "L3_o")}
        row_bias = {n: sb("b_" + n, [P, P]) for n in ("L1_v", "L1_o", "L2_o", "L3_v", "L3_o")}
        col_bias = {n: sb("b_" + n, [P, 1]) for n in ("L3_q", "L3_k")}
        mask_l1_sb = sb("mask_l1_sb", [P, S])
        mask_l3_sb = sb("mask_l3_sb", [P, S])
        mask_l3_in = sb("mask_l3_in", [P, S], mybir.dt.uint8)

        xi = [sb(f"xi{i}", [P, GT, P]) for i in range(2)]
        ci = [sb(f"ci{i}", [P, GSEQ, 2, S]) for i in range(2)]
        kblk = [sb(f"kblk{i}", [P, HEADS, GTOK]) for i in range(2)]
        q_t = [sb(f"q_t{i}", [P, GTOK]) for i in range(2)]
        k_t = sb("k_t", [P, GTOK])
        v2 = [sb(f"v2{i}", [P, GSEQ, PAIRS, 2, VC]) for i in range(2)]
        x_norm = sb("x_norm", [P, GT, P])
        x_norm_t = sb("x_norm_t", [P, GTOK])
        bn = sb("bn", [P, GT, 6])
        mean = sb("mean", [P, GT])
        mean_gap = sb("mean_gap", [P, GT])
        dev = sb("dev", [P, GT])
        var_eps = sb("var_eps", [P, GT])
        var_log = sb("var_log", [P, GT])
        r0 = sb("r0", [P, GT])
        r_sq = sb("r_sq", [P, GT])
        rstd = sb("rstd", [P, GT])
        probs = [sb(f"probs{i}", [P, HEADS, S]) for i in range(2)]
        row_max = [sb(f"row_max{i}", [P, HEADS]) for i in range(2)]
        mask2 = [sb(f"mask2{i}", [P, GT, S]) for i in range(2)]
        probs_t = sb("probs_t", [P, PAIRS, P])
        wide = [t[:, :, :].rearrange("p a b -> p (a b)")[:, i * GTOK:(i + 1) * GTOK]
                for t in (*probs, probs_t) for i in range(2)]
        hi = [t[:, :, :, :].rearrange("p b j k -> p (b j k)")[:, 0:GTOK].rearrange("p (u c) -> p u c", u=GT)
              for t in ci]
        rec = sb("rec", [P, PAIRS, 2])
        o = sb("o", [P, HEADS, HD])
        o_t = sb("o_t", [P, P])

        w_low = {"W": sb("w_low", [P, P]), "Wp": sb("w_low_p", [PROJ, P]), "sim": sb("w_sim", [PROJ, NLR]),
                 "bp": sb("w_bp", [PROJ, 1]), "temp": sb("w_temp", [P, 1])}
        w_route = sb("w_route", [P, ROUTE])
        b_route = sb("b_route", [P, ROUTE])
        w_up = sb("w_up", [P, P])
        w_gate = sb("w_gate", [P, EXPERTS])
        w_1 = sb("w_1", [P, EXPERTS, INTER])
        w_3 = sb("w_3", [P, EXPERTS, INTER])
        w_2 = sb("w_2", [P, EC, P])
        pick_expert = sb("pick_expert", [P, EC, P])
        w_mix = {n: sb("w_mix_" + n, [P, P]) for n in "rkv"}
        mu = {n: sb("mu_" + n, [P, 1]) for n in "rk"}
        one_less_mu = {n: sb("one_less_mu_" + n, [P, 1]) for n in "rk"}
        w_qkv = [sb(f"w_qkv{l}", [P, 3 * INNER]) for l in range(DEPTH)]
        w_lo = [sb(f"w_lo{l}", [P, LPAIRS, P]) for l in range(DEPTH)]
        rot_base = sb("rot_base", [P, 4, LD])
        rot = [sb(f"rot{l}", [P, 4, LD]) for l in range(DEPTH)]
        rot_scale = sb("rot_scale", [P, DEPTH, 2, LD])
        w_up1 = [sb(f"w_up1{l}", [P, 2 * HID]) for l in range(DEPTH)]
        b_up1 = [sb(f"b_up1{l}", [P, 2 * len(HC)]) for l in range(DEPTH)]
        w_dn = [sb(f"w_dn{l}", [P, len(HC), P]) for l in range(DEPTH)]
        b_dn = [sb(f"b_dn{l}", [P, P]) for l in range(DEPTH)]
        ln_gb = [sb(f"ln_gb{l}", [P, 2]) for l in range(DEPTH)]
        causal = sb("causal", [P, S])
        gates = sb("gates", [P, GT, P])
        gates_t = [k_t, x_norm_t]
        route = sb("route", [P, GT, ROUTE])
        small = {n: sb("small_" + n, [P, GT, 16]) for n in "abcdefgh"}
        tiny = {n: sb("tiny_" + n, [P, GT]) for n in "abcdef"}
        top8 = sb("top8", [P, GT, 8])

        ps_scores = [ctx.enter_context(nc.psum_tensor(f"ps_s{i}", [P, 2, 512], F32)) for i in range(2)]
        ps_pt = [ctx.enter_context(nc.psum_tensor(f"ps_pt{i}", [P, 512], F32)) for i in range(2)]
        ps_o = ctx.enter_context(nc.psum_tensor("ps_o", [P, 512], F32))
        ps_pj = ctx.enter_context(nc.psum_tensor("ps_pj", [P, 512], F32))

        loaded = signal("loaded")
        zeroed = signal("zeroed")
        marked = signal("marked")
        drawn = signal("drawn")
        loads = [(x[:, :, :], x_in), (mask_l3_in[0:S, :], mask_l3), (mask_l3_in[S:P, :], mask_l3)]
        loads += [(attn_w[n][:, :], w[n]) for n in attn_w]
        loads += [(row_bias[n][0:1, :], w["b" + n]) for n in row_bias]
        loads += [(col_bias[n][:, :], w["b" + n]) for n in col_bias]

        loads += [(w_low[n][:, :], w["low_" + n]) for n in ("W", "Wp", "sim", "bp", "temp")]
        loads += [(w_route[:, 0:PROJ], w["low_WpT"]), (w_route[:, PROJ + NLR:ROUTE], w["low_Wd"]),
                  (w_up[0:RSUM, :], w["low_Wu"]), (w_gate[:, :], w["moe_gate"]), (w_1[:, :, :], w["moe_1"]),
                  (w_3[:, :, :], w["moe_3"]), (w_2[:, :, :], w["moe_2"])]
        loads += [(w_mix[n][:, :], w["mix_" + n]) for n in "rkv"]
        loads += [(mu[n][:, :], w["mu_" + n]) for n in "rk"]

        loads += [(rot_base[:, :, :], w["rot"]), (rot_scale[:, :, :, :], w["rot_scale"])]
        for l in range(DEPTH):
            loads += [(w_qkv[l][:, :], w["wqkv"][l]), (w_lo[l][:, :, :], w["lo"][l]), (w_up1[l][:, :], w["up1"][l]),
                      (b_up1[l][:, :], w["b_up1"][l]), (w_dn[l][:, :, :], w["dn"][l]),
                      (b_dn[l][0:1, :], w["b_dn"][l]), (ln_gb[l][:, :], w["ln"][l])]

        with nc.Block() as block:
            @block.sync
            def _(sp):
                sp.wait_ge(zeroed.sem, 8 + DEPTH)
                for dst, src in loads:
                    sp.dma_start(dst, src).then_inc(loaded.sem, 16)
                sp.wait_ge(loaded.sem, 16 * len(loads))

            @block.vector
            def _(dve):
                for n in row_bias:
                    dve.memset(row_bias[n][:, :], 0.0).then_inc(zeroed.sem, 1)
                dve.memset(ones[:, :], 1.0).then_inc(zeroed.sem, 1)
                dve.memset(w_up[:, :], 0.0).then_inc(zeroed.sem, 1)
                dve.memset(gates[:, :, :], 0.0).then_inc(zeroed.sem, 1)
                for l in range(DEPTH):
                    dve.memset(b_dn[l][:, :], 0.0).then_inc(zeroed.sem, 1)
                for i in range(2):
                    dve.memset(kblk[i][:, :, :], 0.0).then_inc(zeroed.sem, 1)
                    dve.memset(v2[i][:, :, :, :, :], 0.0).then_inc(zeroed.sem, 1)
                dve.wait_ge(zeroed.sem, 12 + DEPTH)
                for i in range(2):
                    for j in range(2):
                        dve.memset(v2[i][j * S:(j + 1) * S, :, :, j, HD:VC], 1.0).then_inc(marked.sem, 1)
                dve.wait_ge(loaded.sem, 16 * len(loads))
                dve.tensor_scalar(mask_l3_sb[:, :], mask_l3_in[:, :], -NEG, NEG, ALU.mult, ALU.add)\
                   .then_inc(marked.sem, 1)

            @block.gpsimd
            def _(pool):
                for n in GROUP_SIGNALS:
                    pool.sem_inc(signals[n].sem, 1)
                pool.memset(ident[:, :], 0.0).then_inc(drawn.sem, 1)
                pool.wait_ge(drawn.sem, 1)
                pool.affine_select(out=ident[:, :], in_=ident[:, :], compare_op=ALU.not_equal, fill=1.0,
                                   base=0, pattern=[[-1, P]], channel_multiplier=1).then_inc(drawn.sem, 1)
                pool.wait_ge(drawn.sem, 2)
                pool.memset(mask_l1_sb[:, :], 0.0).then_inc(drawn.sem, 1)
                for b in range(2):
                    rows = mask_l1_sb[b * S:(b + 1) * S, :]
                    pool.wait_ge(drawn.sem, 3 + 2 * b)
                    pool.affine_select(out=rows, in_=rows, compare_op=ALU.is_gt, fill=NEG,
                                       base=0, pattern=[[-1, S]], channel_multiplier=1)\
                        .then_inc(drawn.sem, 1)
                    pool.wait_ge(drawn.sem, 4 + 2 * b)
                    pool.memset(rows[0:1, 0:1], 0.0).then_inc(drawn.sem, 1)
                pool.wait_ge(drawn.sem, 7)
                pool.memset(causal[:, :], 0.0).then_inc(drawn.sem, 1)
                for b in range(2):
                    rows = causal[b * S:(b + 1) * S, :]
                    pool.wait_ge(drawn.sem, 8 + b)
                    pool.affine_select(out=rows, in_=rows, compare_op=ALU.is_ge, fill=NEG,
                                       base=0, pattern=[[-1, S]], channel_multiplier=1)\
                        .then_inc(drawn.sem, 1)
                pool.wait_ge(drawn.sem, 10)
                pool.memset(pick_expert[:, :, :], 0.0).then_inc(drawn.sem, 1)
                pool.wait_ge(drawn.sem, 11)
                picks = pick_expert[:, :, :].rearrange("p c (j i) -> p c j i", j=2)
                pool.affine_select(out=picks, in_=picks, compare_op=ALU.not_equal, fill=1.0, base=0,
                                   pattern=[[-2, EC], [-1, 2], [0, INTER]], channel_multiplier=1)\
                    .then_inc(drawn.sem, 1)

        sp_turn = signal("sp_turn")
        dve_turn = signal("dve_turn")
        x_loaded = signal("x_loaded")
        stored = signal("stored")
        bn_done = signal("bn_done")
        var_ready = signal("var_ready")
        ln_ready = signal("ln_ready")
        r0_ready = signal("r0_ready")
        newton = signal("newton")
        x_norm_ready = signal("x_norm_ready")
        xt_in_psum = signal("xt_in_psum")
        xt_ready = signal("xt_ready")
        added = signal("added")

        def open_front(added_per, norm=True):
            for s, per in ((x_loaded, 16), (stored, 16), (xt_in_psum, 1), (xt_ready, 1), (added, added_per)):
                s.opens(per)
            if norm:
                for s, per in ((bn_done, GT + 6), (var_ready, 1), (ln_ready, 1), (r0_ready, 1), (newton, 4),
                               (x_norm_ready, GT)):
                    s.opens(per)

        def norm_stats(dve, g, par, src=xi):
            dve.wait_ge(x_loaded.sem, x_loaded.at(g, 16))
            for u in range(GT):
                dve.bn_stats(bn[:, u, :], src[par][:, u, :]).then_inc(bn_done.sem, 1)
            dve.wait_ge(bn_done.sem, bn_done.at(g, GT))
            dve.tensor_tensor(mean[:, :], bn[:, :, 1], bn[:, :, 4], ALU.add).then_inc(bn_done.sem, 1)
            dve.tensor_tensor(mean_gap[:, :], bn[:, :, 1], bn[:, :, 4], ALU.subtract)\
               .then_inc(bn_done.sem, 1)
            dve.tensor_tensor(dev[:, :], bn[:, :, 2], bn[:, :, 5], ALU.add).then_inc(bn_done.sem, 1)
            dve.wait_ge(bn_done.sem, bn_done.at(g, GT + 3))
            dve.tensor_scalar(mean[:, :], mean[:, :], 0.5, None, ALU.mult).then_inc(bn_done.sem, 1)
            dve.tensor_tensor(mean_gap[:, :], mean_gap[:, :], mean_gap[:, :], ALU.mult)\
               .then_inc(bn_done.sem, 1)
            dve.tensor_scalar(dev[:, :], dev[:, :], 1.0 / P, LN_EPS, ALU.mult, ALU.add)\
               .then_inc(bn_done.sem, 1)
            dve.wait_ge(bn_done.sem, bn_done.at(g, GT + 6))
            dve.scalar_tensor_tensor(out=var_eps[:, :], in0=mean_gap[:, :], scalar=0.25,
                                     in1=dev[:, :], op0=ALU.mult, op1=ALU.add)\
               .then_inc(var_ready.sem, 1)

        def normalise(dve, g, par, src=xi):
            dve.wait_ge(r0_ready.sem, r0_ready.at(g, 1))
            dve.tensor_tensor(r_sq[:, :], r0[:, :], r0[:, :], ALU.mult).then_inc(newton.sem, 1)
            dve.wait_ge(newton.sem, newton.at(g, 1))
            dve.tensor_tensor(r_sq[:, :], r_sq[:, :], var_eps[:, :], ALU.mult).then_inc(newton.sem, 1)
            dve.wait_ge(newton.sem, newton.at(g, 2))
            dve.tensor_scalar(r_sq[:, :], r_sq[:, :], -0.5, 1.5, ALU.mult, ALU.add)\
               .then_inc(newton.sem, 1)
            dve.wait_ge(newton.sem, newton.at(g, 3))
            dve.tensor_tensor(rstd[:, :], r0[:, :], r_sq[:, :], ALU.mult).then_inc(newton.sem, 1)
            dve.wait_ge(newton.sem, newton.at(g, 4))
            dve.wait_ge(xt_in_psum.sem, xt_in_psum.at(g, 0))
            for u in range(GT):
                dve.tensor_scalar(x_norm[:, u, :], src[par][:, u, :], mean[:, u:u + 1],
                                  rstd[:, u:u + 1], ALU.subtract, ALU.mult)\
                   .then_inc(x_norm_ready.sem, 1)

        def root(act, g):
            act.wait_ge(var_ready.sem, var_ready.at(g, 1))
            act.activation(var_log[:, :], var_eps[:, :], ACT.Ln).then_inc(ln_ready.sem, 1)
            act.wait_ge(ln_ready.sem, ln_ready.at(g, 1))
            act.wait_ge(newton.sem, newton.at(g, 0))
            act.activation(r0[:, :], var_log[:, :], ACT.Exp, scale=-0.5).then_inc(r0_ready.sem, 1)

        def transpose_x(pe, g):
            pe.wait_ge(x_norm_ready.sem, x_norm_ready.at(g, GT))
            for u in range(GT):
                last = pe.transpose(ps_pj[:, u * P:(u + 1) * P], x_norm[:, u, :], ident[:, :])
            last.then_inc(xt_in_psum.sem, 1)

        def cross_attention(name, scale, mask=None, mask_per_seq=None, project=True, relu=False):
            wq, wk, wv, wo = (attn_w.get(f"{name}_{n}", ident) for n in "qkvo")
            bv, bo = row_bias.get(name + "_v"), row_bias.get(name + "_o")
            bq, bk = col_bias.get(name + "_q"), col_bias.get(name + "_k")
            masked = mask is not None or mask_per_seq is not None

            open_front(GT)
            c_loaded = signal("c_loaded", 32)
            m_loaded = signal("m_loaded", 16 if mask_per_seq is not None else 0)
            k_placed = signal("k_placed", 16 * HEADS)
            k_in_psum = signal("k_in_psum", 1 if project else 0)
            kt_ready = signal("kt_ready", 1 if project else 0)
            v_in_psum = signal("v_in_psum", 2)
            v_even = signal("v_even", 2)
            v_odd = signal("v_odd", 2)
            q_in_psum = signal("q_in_psum", 1 if project else 0)
            qt_ready = signal("qt_ready", 1 if project else 0)
            scored = signal("scored", GT)
            max_ready = signal("max_ready", GT)
            mask_added = signal("mask_added", GT if masked else 0)
            shifted = signal("shifted", GT)
            exp_ready = signal("exp_ready", GT)
            turned = signal("turned", 2 * GT, 2)
            pt_low = signal("pt_low", GT)
            pt_high = signal("pt_high", GT)
            summed = signal("summed", GT)
            rec_ready = signal("rec_ready", 2 * GT)
            o_ready = signal("o_ready", 2 * GT)
            ot_in_psum = signal("ot_in_psum", GT)
            ot_ready = signal("ot_ready", GT)
            y_ready = signal("y_ready", GT)

            q_src = q_t
            q_signal = qt_ready if project else xt_ready

            with nc.Block() as block:
                @block.sync
                def _(sp):
                    def load(g, par, wait_store):
                        if wait_store:
                            sp.wait_ge(stored.sem, stored.at(g - 1, 0))
                            sp.sem_inc(sp_turn.sem, 1)
                        sp.dma_start(xi[par][:, :, :], x[:, bass.ds(g * GT, GT), :]).then_inc(x_loaded.sem, 16)
                        if wait_store:
                            sp.wait_ge(v_in_psum.sem, v_in_psum.at(g - 1, 0))
                            sp.sem_inc(sp_turn.sem, 1)
                            if not project:
                                sp.wait_ge(k_placed.sem, k_placed.at(g - 1, 0))
                                sp.sem_inc(sp_turn.sem, 1)
                            if mask_per_seq is not None:
                                sp.wait_ge(mask_added.sem, mask_added.at(g - 1, 0))
                                sp.sem_inc(sp_turn.sem, 1)
                                sp.wait_ge(bn_done.sem, bn_done.at(g - 1, 1))
                            sp.sem_inc(sp_turn.sem, 1)
                        src = ctx_t[:, bass.ds(g * GTOK, GTOK)].rearrange("p (b k) -> p b k", k=S)
                        for j in range(2):
                            sp.dma_start(ci[par][:, :, j, :], src).then_inc(c_loaded.sem, 16)
                        if mask_per_seq is not None:
                            sp.dma_start(mask2[par][:, :, :], mask_per_seq[:, bass.ds(g * GT, GT), :])\
                              .then_inc(m_loaded.sem, 16)

                    def place_keys(g, par, wait_scores):
                        if project:
                            sp.wait_ge(kt_ready.sem, kt_ready.at(g, 1))
                        else:
                            sp.wait_ge(c_loaded.sem, c_loaded.at(g, 32))
                        sp.sem_inc(sp_turn.sem, 1)
                        if wait_scores:
                            sp.wait_ge(scored.sem, scored.at(g - 1, 1))
                        sp.sem_inc(sp_turn.sem, 1)
                        src = k_t[:, :] if project else ci[par][:, :, 0, :]
                        for h in range(HEADS):
                            rows = slice(h * HD, (h + 1) * HD)
                            dst = kblk[par][rows, h, :]
                            if not project:
                                dst = dst.rearrange("p (b k) -> p b k", k=S)
                            sp.dma_start(dst, src[rows]).then_inc(k_placed.sem, 16)

                    def body(g, par, ahead=True):
                        if ahead:
                            load(g + 1, 1 - par, True)
                            place_keys(g + 1, 1 - par, True)
                        sp.wait_ge(added.sem, added.at(g, GT))
                        sp.sem_inc(sp_turn.sem, 1)
                        sp.dma_start(x[:, bass.ds(g * GT, GT), :], xi[par][:, :, :]).then_inc(stored.sem, 16)

                    load(0, 0, False)
                    place_keys(0, 0, False)
                    with sp.Fori(0, GROUPS - 2, 2) as g:
                        body(g, 0)
                        body(g + 1, 1)
                    body(GROUPS - 2, 0)
                    body(GROUPS - 1, 1, ahead=False)
                    sp.wait_ge(stored.sem, stored.at(GROUPS, 0))

                @block.vector
                def _(dve):
                    def values_even(g, par, wait_use):
                        if wait_use:
                            dve.wait_ge(summed.sem, summed.at(g - 1, 0))
                        for c in range(2):
                            dve.wait_ge(v_in_psum.sem, v_in_psum.at(g, c + 1))
                            src = ps_pj[0:S, :].rearrange("p (b r j d) -> p b r j d", b=4, r=PAIRS, j=2)
                            dve.tensor_copy(v2[par][0:S, 4 * c:4 * c + 4, :, 0, 0:HD], src[:, :, :, 0, :])\
                               .then_inc(v_even.sem, 1)

                    def softmax(g, u, par):
                        s = u % 2
                        scores = ps_scores[s][:, :, :].rearrange("p a (h k) -> p (a h) k", k=S)
                        dve.wait_ge(scored.sem, scored.at(g, u + 1))
                        dve.wait_ge(turned.sem, turned.at(g, 2 * u))
                        if masked:
                            if mask_per_seq is not None:
                                m = mask2[par][:, u, :]
                            else:
                                m = mask[:, :]
                            m = m.unsqueeze(1).broadcast_to([P, HEADS, S])
                            dve.tensor_tensor(probs[s][:, :, :], scores, m, ALU.add).then_inc(mask_added.sem, 1)
                            scores = probs[s][:, :, :]
                            dve.wait_ge(mask_added.sem, mask_added.at(g, u + 1))
                        dve.tensor_reduce(row_max[s][:, :], scores, AX, ALU.max).then_inc(max_ready.sem, 1)
                        dve.wait_ge(max_ready.sem, max_ready.at(g, u + 1))
                        dve.tensor_tensor(probs[s][:, :, :], scores,
                                          row_max[s][:, :].unsqueeze(2).broadcast_to([P, HEADS, S]),
                                          ALU.subtract).then_inc(shifted.sem, 1)

                    def turn_high(g, u):
                        dve.wait_ge(turned.sem, turned.at(g, 2 + 2 * u + 2))
                        dve.wait_ge(summed.sem, summed.at(g, u))
                        dve.tensor_copy(probs_t[:, 4:8, :], ps_pt[1][:, :].rearrange("p (r t) -> p r t", r=4))\
                           .then_inc(pt_high.sem, 1)

                    def divide(g, u):
                        dve.wait_ge(summed.sem, summed.at(g, u + 1))
                        dve.wait_ge(ot_in_psum.sem, ot_in_psum.at(g, u))
                        acc = ps_o[:, 0:PAIRS * 2 * 2 * VC].rearrange("p (r b j c) -> p r b j c", b=2, j=2, c=VC)
                        for b in range(2):
                            rows = slice(b * S, (b + 1) * S)
                            dve.reciprocal(rec[rows, :, :], acc[rows, :, b, :, HD]).then_inc(rec_ready.sem, 1)
                        for b in range(2):
                            rows = slice(b * S, (b + 1) * S)
                            dve.wait_ge(rec_ready.sem, rec_ready.at(g, 2 * u + b + 1))
                            dve.tensor_tensor(o[rows, :, :].rearrange("p (r j) d -> p r j d", j=2),
                                              acc[rows, :, b, :, 0:HD],
                                              rec[rows, :, :].unsqueeze(3).broadcast_to([S, PAIRS, 2, HD]),
                                              ALU.mult).then_inc(o_ready.sem, 1)

                    def add_residual(g, u, par):
                        dve.wait_ge(y_ready.sem, y_ready.at(g, u + 1))
                        y = ps_pt[1][:, 0:P]
                        xu = xi[par][:, u, :]
                        if relu:
                            dve.scalar_tensor_tensor(out=xu, in0=y, scalar=0.0, in1=xu, op0=ALU.max,
                                                     op1=ALU.add).then_inc(added.sem, 1)
                        else:
                            dve.tensor_tensor(xu, y, xu, ALU.add).then_inc(added.sem, 1)

                    def body(g, par, ahead=True):
                        nxt, other = g + 1, 1 - par
                        if ahead:
                            if mask_per_seq is not None:
                                dve.wait_ge(m_loaded.sem, m_loaded.at(nxt, 16))
                            norm_stats(dve, nxt, other)
                        turn_high(g, 0)
                        softmax(g, 1, par)
                        divide(g, 0)
                        if ahead:
                            normalise(dve, nxt, other)
                            values_even(nxt, other, True)
                        for u in (1, 2):
                            turn_high(g, u)
                            softmax(g, u + 1, par)
                            add_residual(g, u - 1, par)
                            divide(g, u)
                        turn_high(g, 3)
                        divide(g, 3)
                        if ahead:
                            softmax(nxt, 0, other)
                        add_residual(g, 2, par)
                        add_residual(g, 3, par)

                    if mask_per_seq is not None:
                        dve.wait_ge(m_loaded.sem, m_loaded.at(0, 16))
                    norm_stats(dve, 0, 0)
                    normalise(dve, 0, 0)
                    values_even(0, 0, False)
                    softmax(0, 0, 0)
                    with dve.Fori(0, GROUPS - 2, 2) as g:
                        body(g, 0)
                        body(g + 1, 1)
                    body(GROUPS - 2, 0)
                    body(GROUPS - 1, 1, ahead=False)

                @block.scalar
                def _(act):
                    def keys(g):
                        if not project:
                            return
                        act.wait_ge(k_in_psum.sem, k_in_psum.at(g, 1))
                        act.wait_ge(k_placed.sem, k_placed.at(g, 0))
                        if bk is None:
                            act.activation(k_t[:, :], ps_pj[:, :], ACT.Copy).then_inc(kt_ready.sem, 1)
                        else:
                            act.activation(k_t[:, :], ps_pj[:, :], ACT.Identity, bias=bk[:, 0:1])\
                               .then_inc(kt_ready.sem, 1)

                    def values_odd(g, par, wait_use):
                        if wait_use:
                            act.wait_ge(summed.sem, summed.at(g - 1, 0))
                        for c in range(2):
                            act.wait_ge(v_in_psum.sem, v_in_psum.at(g, c + 1))
                            src = ps_pj[S:P, :].rearrange("p (b r j d) -> p b r j d", b=4, r=PAIRS, j=2)
                            act.activation(v2[par][S:P, 4 * c:4 * c + 4, :, 1, 0:HD], src[:, :, :, 1, :], ACT.Copy)\
                               .then_inc(v_odd.sem, 1)

                    def x_transposed(g, par, wait_use):
                        act.wait_ge(xt_in_psum.sem, xt_in_psum.at(g, 1))
                        if project:
                            act.wait_ge(q_in_psum.sem, q_in_psum.at(g, 0))
                            act.activation(x_norm_t[:, :], ps_pj[:, :], ACT.Copy).then_inc(xt_ready.sem, 1)
                        else:
                            if wait_use:
                                act.wait_ge(scored.sem, scored.at(g - 1, 0))
                            act.activation(q_t[par][:, :], ps_pj[:, :], ACT.Copy).then_inc(xt_ready.sem, 1)

                    def queries(g, par, wait_use):
                        if not project:
                            return
                        act.wait_ge(q_in_psum.sem, q_in_psum.at(g, 1))
                        if wait_use:
                            act.wait_ge(scored.sem, scored.at(g - 1, 0))
                        if bq is None:
                            act.activation(q_t[par][:, :], ps_pj[:, :], ACT.Copy).then_inc(qt_ready.sem, 1)
                        else:
                            act.activation(q_t[par][:, :], ps_pj[:, :], ACT.Identity, bias=bq[:, 0:1])\
                               .then_inc(qt_ready.sem, 1)

                    def exponentials(g, u):
                        act.wait_ge(shifted.sem, shifted.at(g, u + 1))
                        p = probs[u % 2][:, :, :]
                        act.activation(p, p, ACT.Exp, scale=scale).then_inc(exp_ready.sem, 1)

                    def turn_low(g, u):
                        act.wait_ge(turned.sem, turned.at(g, 2 + 2 * u + 1))
                        act.wait_ge(summed.sem, summed.at(g, u))
                        act.activation(probs_t[:, 0:4, :], ps_pt[0][:, :].rearrange("p (r t) -> p r t", r=4),
                                       ACT.Copy).then_inc(pt_low.sem, 1)

                    def o_transposed(g, u):
                        act.wait_ge(ot_in_psum.sem, ot_in_psum.at(g, u + 1))
                        act.wait_ge(y_ready.sem, y_ready.at(g, u))
                        act.activation(o_t[:, :], ps_pt[0][:, 0:P], ACT.Copy).then_inc(ot_ready.sem, 1)

                    def body(g, par, ahead=True):
                        nxt, other = g + 1, 1 - par
                        if ahead:
                            root(act, nxt)
                        turn_low(g, 0)
                        exponentials(g, 1)
                        if ahead:
                            keys(nxt)
                            values_odd(nxt, other, True)
                        turn_low(g, 1)
                        exponentials(g, 2)
                        o_transposed(g, 0)
                        if ahead:
                            x_transposed(nxt, other, True)
                        turn_low(g, 2)
                        if ahead:
                            queries(nxt, other, True)
                        exponentials(g, 3)
                        o_transposed(g, 1)
                        turn_low(g, 3)
                        o_transposed(g, 2)
                        if ahead:
                            o_transposed(g, 3)
                            exponentials(nxt, 0)
                        else:
                            o_transposed(g, 3)

                    root(act, 0)
                    keys(0)
                    values_odd(0, 0, False)
                    x_transposed(0, 0, False)
                    queries(0, 0, False)
                    exponentials(0, 0)
                    with act.Fori(0, GROUPS - 2, 2) as g:
                        body(g, 0)
                        body(g + 1, 1)
                    body(GROUPS - 2, 0)
                    body(GROUPS - 1, 1, ahead=False)

                @block.tensor
                def _(pe):
                    pe.sem_inc(turned.sem, 2)

                    def project_kv(g, par):
                        pe.wait_ge(c_loaded.sem, c_loaded.at(g, 32))
                        pe.wait_ge(q_signal.sem, q_signal.at(g, 0))
                        if project:
                            pe.matmul(ps_pj[:, :], wk[:, :], ci[par][:, :, 0, :], start=True, stop=True)\
                              .then_inc(k_in_psum.sem, 1)
                        for c in range(2):
                            if c == 0 and project:
                                pe.wait_ge(kt_ready.sem, kt_ready.at(g, 1))
                            if c == 1:
                                pe.wait_ge(v_even.sem, v_even.at(g, 1))
                                pe.wait_ge(v_odd.sem, v_odd.at(g, 1))
                            for b in range(4):
                                seq = 4 * c + b
                                twice = ci[par][:, seq, :, :].rearrange("p j k -> p (j k)")
                                dst = ps_pj[:, b * P:(b + 1) * P]
                                last = pe.matmul(dst, twice, wv[:, :], start=True, stop=bv is None)
                                if bv is not None:
                                    last = pe.matmul(dst, ones[:, :], bv[:, :], start=False, stop=True)
                            last.then_inc(v_in_psum.sem, 1)

                    def free_bank(g):
                        pe.wait_ge(v_even.sem, v_even.at(g, 2))
                        pe.wait_ge(v_odd.sem, v_odd.at(g, 2))

                    def project_q(g):
                        if not project:
                            return
                        pe.wait_ge(xt_ready.sem, xt_ready.at(g, 1))
                        pe.matmul(ps_pj[:, :], wq[:, :], x_norm_t[:, :], start=True, stop=True)\
                          .then_inc(q_in_psum.sem, 1)

                    def scores(g, u, par, reuse):
                        if u == 0:
                            pe.wait_ge(q_signal.sem, q_signal.at(g, 1))
                            pe.wait_ge(k_placed.sem, k_placed.at(g, 16 * HEADS))
                        if reuse:
                            free = mask_added if masked else shifted
                            pe.wait_ge(free.sem, free.at(g, u - 1))
                        for half in range(2):
                            for b in range(2):
                                tok = slice((2 * u + b) * S, (2 * u + b + 1) * S)
                                last = pe.matmul(
                                    ps_scores[u % 2][b * S:(b + 1) * S, half, :], q_src[par][:, tok],
                                    kblk[par][:, half * 8:half * 8 + 8, tok], start=True, stop=True)
                        last.then_inc(scored.sem, 1)

                    def transpose_probs(g, u):
                        pe.wait_ge(exp_ready.sem, exp_ready.at(g, u + 1))
                        flat = probs[u % 2][:, :, :].rearrange("p h k -> p (h k)")
                        for c in range(2):
                            free = pt_high if c else pt_low
                            pe.wait_ge(free.sem, free.at(g, u))
                            done = added if c else ot_ready
                            pe.wait_ge(done.sem, done.at(g, max(u - 1, 0)))
                            for r in range(4):
                                last = pe.transpose(ps_pt[c][:, r * P:(r + 1) * P],
                                                    flat[:, (4 * c + r) * P:(4 * c + r + 1) * P], ident[:, :])
                            last.then_inc(turned.sem, 1)

                    def weigh_values(g, u, par):
                        pe.wait_ge(pt_low.sem, pt_low.at(g, u + 1))
                        pe.wait_ge(pt_high.sem, pt_high.at(g, u + 1))
                        if u == 0:
                            pe.wait_ge(v_even.sem, v_even.at(g, 2))
                            pe.wait_ge(v_odd.sem, v_odd.at(g, 2))
                        pe.wait_ge(o_ready.sem, o_ready.at(g, 2 * u))
                        for r in range(PAIRS):
                            n = 4 * VC
                            last = pe.matmul(ps_o[:, r * n:(r + 1) * n], probs_t[:, r, :],
                                             v2[par][:, 2 * u:2 * u + 2, r, :, :], start=True, stop=True)
                        last.then_inc(summed.sem, 1)

                    def project_o(g, u, last_turned):
                        pe.wait_ge(o_ready.sem, o_ready.at(g, 2 * u + 2))
                        pe.wait_ge(pt_low.sem, pt_low.at(g, last_turned + 1))
                        pe.transpose(ps_pt[0][:, 0:P], o[:, :, :].rearrange("p h d -> p (h d)"), ident[:, :])\
                          .then_inc(ot_in_psum.sem, 1)
                        pe.wait_ge(ot_ready.sem, ot_ready.at(g, u + 1))
                        pe.wait_ge(pt_high.sem, pt_high.at(g, last_turned + 1))
                        pe.wait_ge(added.sem, added.at(g, u))
                        y = ps_pt[1][:, 0:P]
                        last = pe.matmul(y, o_t[:, :], wo[:, :], start=True, stop=bo is None)
                        if bo is not None:
                            last = pe.matmul(y, ones[:, :], bo[:, :], start=False, stop=True)
                        last.then_inc(y_ready.sem, 1)

                    def body(g, par, ahead=True):
                        nxt, other = g + 1, 1 - par
                        transpose_probs(g, 0)
                        scores(g, 2, par, True)
                        weigh_values(g, 0, par)
                        if ahead:
                            project_kv(nxt, other)
                        transpose_probs(g, 1)
                        scores(g, 3, par, True)
                        project_o(g, 0, 1)
                        weigh_values(g, 1, par)
                        if ahead:
                            free_bank(nxt)
                            transpose_x(pe, nxt)
                        transpose_probs(g, 2)
                        if ahead:
                            project_q(nxt)
                            scores(nxt, 0, other, True)
                        project_o(g, 1, 2)
                        weigh_values(g, 2, par)
                        transpose_probs(g, 3)
                        if ahead:
                            scores(nxt, 1, other, True)
                        project_o(g, 2, 3)
                        weigh_values(g, 3, par)
                        project_o(g, 3, 3)

                    project_kv(0, 0)
                    free_bank(0)
                    transpose_x(pe, 0)
                    project_q(0)
                    scores(0, 0, 0, False)
                    scores(0, 1, 0, False)
                    with pe.Fori(0, GROUPS - 2, 2) as g:
                        body(g, 0)
                        body(g + 1, 1)
                    body(GROUPS - 2, 0)
                    body(GROUPS - 1, 1, ahead=False)

            close_stage()

        def move_windows(sp, added_per):
            def load(g, par):
                sp.dma_start(xi[par][:, :, :], x[:, bass.ds(g * GT, GT), :]).then_inc(x_loaded.sem, 16)

            def body(g, par, ahead=True):
                if ahead:
                    sp.wait_ge(stored.sem, stored.at(g, 0))
                    sp.sem_inc(sp_turn.sem, 1)
                    sp.wait_ge(bn_done.sem, bn_done.at(g, 1))
                    sp.sem_inc(sp_turn.sem, 1)
                    load(g + 1, 1 - par)
                sp.wait_ge(added.sem, added.at(g, added_per))
                sp.sem_inc(sp_turn.sem, 1)
                sp.dma_start(x[:, bass.ds(g * GT, GT), :], xi[par][:, :, :]).then_inc(stored.sem, 16)

            load(0, 0)
            with sp.Fori(0, GROUPS - 2, 2) as g:
                body(g, 0)
                body(g + 1, 1)
            body(GROUPS - 2, 0)
            body(GROUPS - 1, 1, ahead=False)
            sp.wait_ge(stored.sem, stored.at(GROUPS, 0))

        def run_groups(eng, body):
            with eng.Fori(0, GROUPS - 2, 2) as g:
                body(g, 0, True)
                body(g + 1, 1, True)
            body(GROUPS - 2, 0, True)
            body(GROUPS - 1, 1, False)

        class Steps:

            def __init__(self, eng, sig, g, k=0):
                self.eng, self.sig, self.g, self.k = eng, sig, g, k

            def __call__(self, ins):
                self.k += 1
                ins.then_inc(self.sig.sem, 1)
                self.eng.wait_ge(self.sig.sem, self.sig.at(self.g, self.k))

        def copy_x_transposed(act, g, par, used, used_value):
            act.wait_ge(xt_in_psum.sem, xt_in_psum.at(g, 1))
            if used is not None:
                act.wait_ge(used.sem, used_value)
            act.activation(q_t[par][:, :], ps_pj[:, :], ACT.Copy).then_inc(xt_ready.sem, 1)

        def prepare_low_rank():
            prep = signal("prep_dve")
            prep_pe, prep_act = signal("prep_pe"), signal("prep_act")
            sim, sq, nrm = w_low["sim"], small["a"][:, 0, 0:NLR], small["b"][:, 0, 0:NLR]
            root_, work = small["c"][:, 0, 0:NLR], small["d"][:, 0, 0:NLR]
            temp = w_low["temp"]
            with nc.Block() as block:
                @block.vector
                def _(dve):
                    step = Steps(dve, prep, 0)
                    step(dve.tensor_tensor(sq[0:PROJ, :], sim[:, :], sim[:, :], ALU.mult))
                    step(dve.tensor_scalar(temp[:, :], temp[:, :], float(np.log(100.0)), None, ALU.min))
                    step(dve.memset(route[0:PROJ, 0:3, 0:P // 4], 0.0))
                    step(dve.memset(wide[0][:, 0:P], 0.0))
                    step(dve.tensor_scalar(wide[0][0:PROJ, 0:P], ones[0:PROJ, :], w_low["bp"][:, 0:1], None, ALU.mult))
                    dve.wait_ge(prep_pe.sem, 1)
                    step(dve.tensor_scalar(nrm, ps_pj[:, 0:NLR], 1e-24, float(2 ** LOG_SCALE), ALU.max, ALU.mult))
                    dve.wait_ge(prep_act.sem, 3)
                    step(dve.tensor_tensor(work, root_, root_, ALU.mult))
                    step(dve.tensor_tensor(work, work, nrm, ALU.mult))
                    step(dve.tensor_scalar(work, work, -0.5, 1.5, ALU.mult, ALU.add))
                    step(dve.tensor_tensor(root_, root_, work, ALU.mult))
                    step(dve.tensor_scalar(root_, root_, float(2 ** LOG_SCALE), None, ALU.mult))
                    step(dve.tensor_scalar(root_, root_, temp[:, 0:1], None, ALU.mult))
                    step(dve.tensor_tensor(sim[:, :], sim[:, :], root_[0:PROJ, :], ALU.mult))
                    dve.wait_ge(prep_pe.sem, 3)
                    step(dve.tensor_copy(w_route[:, PROJ:PROJ + NLR], ps_pj[:, 0:NLR]))
                    step(dve.tensor_copy(b_route[:, 0:PROJ + NLR], ps_o[:, 0:PROJ + NLR]))
                    step(dve.memset(b_route[:, PROJ + NLR:ROUTE], 0.0))

                @block.scalar
                def _(act):
                    act.wait_ge(prep.sem, prep.at(0, 2))
                    act.activation(temp[:, :], temp[:, :], ACT.Exp).then_inc(prep_act.sem, 1)
                    act.wait_ge(prep.sem, prep.at(0, 6))
                    act.activation(work, nrm, ACT.Ln).then_inc(prep_act.sem, 1)
                    act.wait_ge(prep_act.sem, 2)
                    act.activation(root_, work, ACT.Exp, scale=-0.5).then_inc(prep_act.sem, 1)

                @block.tensor
                def _(pe):
                    pe.wait_ge(prep.sem, prep.at(0, 5))
                    pe.matmul(ps_pj[:, 0:NLR], ones[0:PROJ, :], sq[0:PROJ, :], start=True, stop=True)\
                      .then_inc(prep_pe.sem, 1)
                    pe.wait_ge(prep.sem, prep.at(0, 13))
                    pe.matmul(ps_pj[:, 0:NLR], w_low["Wp"][:, :], sim[:, :], start=True, stop=True)\
                      .then_inc(prep_pe.sem, 1)
                    pe.matmul(ps_o[:, 0:PROJ], wide[0][0:PROJ, 0:P], ident[0:PROJ, 0:PROJ], start=True, stop=True)
                    pe.matmul(ps_o[:, PROJ:PROJ + NLR], wide[0][0:PROJ, 0:P], sim[:, :], start=True, stop=True)\
                      .then_inc(prep_pe.sem, 1)

        def low_rank_experts():
            open_front(1)
            route_in_psum = signal("route_in_psum", 1)
            chain = signal("chain", 25)
            norm_ready = signal("norm_ready", 1)
            root_steps = signal("root_steps", 2)
            logit_ready = signal("logit_ready", 1)
            expo_ready = signal("expo_ready", 1)
            gates_ready = signal("gates_ready", NLR)
            gates_in_psum = signal("gates_in_psum", 1)
            gates_t_ready = signal("gates_t_ready", 1)
            y_done = signal("y_done", 1)

            with nc.Block() as block:
                @block.sync
                def _(sp):
                    move_windows(sp, 1)

                @block.tensor
                def _(pe):
                    def route_and_base(g, par):
                        pe.wait_ge(xt_ready.sem, xt_ready.at(g, 1))
                        pe.wait_ge(chain.sem, chain.at(g, 0))
                        for u in range(GT):
                            last = pe.matmul(ps_pt[0][:, u * ROUTE:(u + 1) * ROUTE],
                                             q_t[par][:, u * P:(u + 1) * P], w_route[:, :],
                                             start=True, stop=True)
                        last.then_inc(route_in_psum.sem, 1)
                        pe.wait_ge(added.sem, added.at(g, 0))
                        for u in range(GT):
                            pe.matmul(ps_o[:, u * P:(u + 1) * P], q_t[par][:, u * P:(u + 1) * P],
                                      w_low["W"][:, :], start=u == 0, stop=False, skip_group_check=True)

                    def up(g):
                        pe.wait_ge(gates_ready.sem, gates_ready.at(g, NLR))
                        pe.wait_ge(gates_t_ready.sem, gates_t_ready.at(g, 0))
                        for u in range(GT):
                            last = pe.transpose(ps_pt[1][:, u * P:(u + 1) * P], gates[:, u, :], ident[:, :])
                        last.then_inc(gates_in_psum.sem, 1)
                        pe.wait_ge(gates_t_ready.sem, gates_t_ready.at(g, 1))
                        for u in range(GT):
                            last = pe.matmul(ps_o[:, u * P:(u + 1) * P], gates_t[0][:, u * P:(u + 1) * P],
                                             w_up[:, :], start=False, stop=True, skip_group_check=True)
                        last.then_inc(y_done.sem, 1)

                    def body(g, par, ahead):
                        route_and_base(g, par)
                        if ahead:
                            pe.wait_ge(xt_ready.sem, xt_ready.at(g, 1))
                            transpose_x(pe, g + 1)
                        up(g)

                    transpose_x(pe, 0)
                    run_groups(pe, body)

                @block.scalar
                def _(act):
                    def body(g, par, ahead):
                        act.wait_ge(norm_ready.sem, norm_ready.at(g, 1))
                        act.activation(tiny["b"][:, :], tiny["a"][:, :], ACT.Ln).then_inc(root_steps.sem, 1)
                        act.wait_ge(root_steps.sem, root_steps.at(g, 1))
                        act.activation(tiny["c"][:, :], tiny["b"][:, :], ACT.Exp, scale=-0.5)\
                           .then_inc(root_steps.sem, 1)
                        if ahead:
                            root(act, g + 1)
                        act.wait_ge(logit_ready.sem, logit_ready.at(g, 1))
                        act.activation(small["b"][:, :, 0:NLR], small["a"][:, :, 0:NLR], ACT.Exp)\
                           .then_inc(expo_ready.sem, 1)
                        if ahead:
                            copy_x_transposed(act, g + 1, 1 - par, y_done, y_done.at(g, 0))
                        act.wait_ge(gates_in_psum.sem, gates_in_psum.at(g, 1))
                        act.wait_ge(y_done.sem, y_done.at(g, 0))
                        act.activation(gates_t[0][:, :], ps_pt[1][:, :], ACT.Copy).then_inc(gates_t_ready.sem, 1)

                    root(act, 0)
                    copy_x_transposed(act, 0, 0, None, 0)
                    run_groups(act, body)

                @block.vector
                def _(dve):
                    def col(t, i):
                        return small[t][:, :, i]

                    def body(g, par, ahead):
                        step = Steps(dve, chain, g)
                        if ahead:
                            norm_stats(dve, g + 1, 1 - par)
                        dve.wait_ge(route_in_psum.sem, route_in_psum.at(g, 1))
                        rs = route[:, :, :]
                        step(dve.tensor_tensor(rs, ps_pt[0][:, 0:GT * ROUTE].rearrange("p (u c) -> p u c", u=GT),
                                               b_route[:, :].unsqueeze(1).broadcast_to([P, GT, ROUTE]), ALU.add))
                        sq = wide[1][:, 0:GT * PROJ].rearrange("p (u c) -> p u c", u=GT)
                        step(dve.tensor_tensor(sq, rs[:, :, 0:PROJ], rs[:, :, 0:PROJ], ALU.mult))
                        step(dve.tensor_reduce(tiny["d"][:, :], sq, AX, ALU.add))
                        dve.tensor_scalar(tiny["a"][:, :], tiny["d"][:, :], 1e-24, float(2 ** LOG_SCALE),
                                          ALU.max, ALU.mult).then_inc(norm_ready.sem, 1)
                        if ahead:
                            normalise(dve, g + 1, 1 - par)
                        dve.wait_ge(norm_ready.sem, norm_ready.at(g, 1))
                        dve.wait_ge(root_steps.sem, root_steps.at(g, 2))
                        a, b, c, d = (tiny[n][:, :] for n in "abcd")
                        step(dve.tensor_tensor(d, c, c, ALU.mult))
                        step(dve.tensor_tensor(d, d, a, ALU.mult))
                        step(dve.tensor_scalar(d, d, -0.5, 1.5, ALU.mult, ALU.add))
                        step(dve.tensor_tensor(d, d, c, ALU.mult))
                        lg = small["a"][:, :, 0:NLR]
                        step(dve.tensor_tensor(lg, rs[:, :, PROJ:PROJ + NLR],
                                               d.unsqueeze(2).broadcast_to([P, GT, NLR]), ALU.mult))
                        step(dve.tensor_reduce(tiny["e"][:, :], lg, AX, ALU.max))
                        dve.tensor_tensor(lg, lg, tiny["e"][:, :].unsqueeze(2).broadcast_to([P, GT, NLR]),
                                          ALU.subtract).then_inc(logit_ready.sem, 1)
                        dve.wait_ge(logit_ready.sem, logit_ready.at(g, 1))
                        step(dve.tensor_scalar(small["c"][:, :, 0:NLR], lg, 0.0, None, ALU.is_equal))
                        step(dve.tensor_copy(col("d", 0), col("c", 0)))
                        for i in range(1, NLR):
                            step(dve.tensor_tensor(col("e", i), col("c", i), col("d", i - 1), ALU.is_gt))
                            if i < NLR - 1:
                                step(dve.tensor_tensor(col("d", i), col("d", i - 1), col("c", i), ALU.max))
                        step(dve.tensor_copy(col("e", 0), col("c", 0)))
                        dve.wait_ge(expo_ready.sem, expo_ready.at(g, 1))
                        step(dve.tensor_reduce(tiny["f"][:, :], small["b"][:, :, 0:NLR], AX, ALU.add))
                        step(dve.reciprocal(tiny["f"][:, :], tiny["f"][:, :]))
                        step(dve.tensor_tensor(small["e"][:, :, 0:NLR], small["e"][:, :, 0:NLR],
                                               small["b"][:, :, 0:NLR], ALU.mult))
                        step(dve.tensor_tensor(small["e"][:, :, 0:NLR], small["e"][:, :, 0:NLR],
                                               tiny["f"][:, :].unsqueeze(2).broadcast_to([P, GT, NLR]), ALU.mult))
                        dve.wait_ge(gates_in_psum.sem, gates_in_psum.at(g, 0))
                        at = 0
                        for i, r in enumerate(RANKS):
                            dve.tensor_tensor(gates[:, :, at:at + r], rs[:, :, PROJ + NLR + at:PROJ + NLR + at + r],
                                              small["e"][:, :, i:i + 1].broadcast_to([P, GT, r]), ALU.mult)\
                               .then_inc(gates_ready.sem, 1)
                            at += r
                        while step.k < 25:
                            step.k += 1
                            dve.sem_inc(chain.sem, 1)
                        dve.wait_ge(y_done.sem, y_done.at(g, 1))
                        flat = xi[par][:, :, :].rearrange("p u c -> p (u c)")
                        dve.tensor_tensor(flat, ps_o[:, :], flat, ALU.add).then_inc(added.sem, 1)

                    norm_stats(dve, 0, 0)
                    normalise(dve, 0, 0)
                    run_groups(dve, body)
            close_stage()

        def mixture():
            open_front(1)
            CH = 16
            router_in_psum = signal("route_in_psum", 1)
            router_copied = signal("router_copied", 1)
            chain = signal("chain", CH)
            picked = signal("picked", 1)
            top_ready = signal("top_ready", GT)
            logit_ready = signal("logit_ready", 1)
            expo_ready = signal("expo_ready", 1)
            gates_ready = signal("gates_ready", 1)
            gates_in_psum = signal("gates_in_psum", 1)
            gates_t_ready = signal("gates_t_ready", 1)
            hidden_in_psum = signal("hidden_in_psum", EC)
            silu_done = signal("silu_done", EC, 2)
            times_up = signal("times_up", EC, 2)
            weighted = signal("weighted", EC, 2)
            mixed = signal("mixed", EC, 2)
            bank_g = [ps_scores[i][:, 0, :] for i in range(2)]
            bank_u = [ps_scores[i][:, 1, :] for i in range(2)]
            bank_s = [ps_pt[i][:, :] for i in range(2)]
            hid = wide

            with nc.Block() as block:
                @block.sync
                def _(sp):
                    move_windows(sp, 1)

                @block.tensor
                def _(pe):
                    pe.sem_inc(mixed.sem, 2)

                    def router(g, par):
                        pe.wait_ge(xt_ready.sem, xt_ready.at(g, 1))
                        for u in range(GT):
                            last = pe.matmul(ps_pj[:, u * EXPERTS:(u + 1) * EXPERTS],
                                             q_t[par][:, u * P:(u + 1) * P], w_gate[:, :], start=True, stop=True)
                        last.then_inc(router_in_psum.sem, 1)

                    def transpose_gates(g):
                        pe.wait_ge(gates_ready.sem, gates_ready.at(g, 1))
                        for u in range(GT):
                            last = pe.transpose(ps_pj[:, u * P:(u + 1) * P], gates[:, u, :], ident[:, :])
                        last.then_inc(gates_in_psum.sem, 1)

                    def hidden(g, c, par):
                        s = c % 2
                        if c == 0:
                            pe.wait_ge(gates_t_ready.sem, gates_t_ready.at(g, 1))
                        pe.wait_ge(silu_done.sem, silu_done.at(g, c + 1))
                        pe.matmul(bank_g[s], w_1[:, 2 * c:2 * c + 2, :].rearrange("p e i -> p (e i)"),
                                  q_t[par][:, :], start=True, stop=True)
                        pe.wait_ge(times_up.sem, times_up.at(g, c + 1))
                        pe.matmul(bank_u[s], w_3[:, 2 * c:2 * c + 2, :].rearrange("p e i -> p (e i)"),
                                  q_t[par][:, :], start=True, stop=True)
                        pe.wait_ge(weighted.sem, weighted.at(g, c + 1))
                        pe.matmul(bank_s[s], pick_expert[:, c, :], gates_t[par][:, :], start=True, stop=True)\
                          .then_inc(hidden_in_psum.sem, 1)

                    def mix(g, c):
                        pe.wait_ge(weighted.sem, weighted.at(g, c + 3))
                        if c == 0:
                            pe.wait_ge(added.sem, added.at(g, 0))
                        for u in range(GT):
                            last = pe.matmul(ps_o[:, u * P:(u + 1) * P], hid[c % 2][:, u * P:(u + 1) * P],
                                             w_2[:, c, :], start=c == 0 and u == 0, stop=c == EC - 1,
                                             skip_group_check=True)
                        last.then_inc(mixed.sem, 1)

                    def body(g, par, ahead):
                        for c in range(EC):
                            hidden(g, c, par)
                            if c:
                                mix(g, c - 1)
                            if ahead and c == 2:
                                transpose_x(pe, g + 1)
                            if ahead and c == 4:
                                router(g + 1, 1 - par)
                            if ahead and c == 7:
                                transpose_gates(g + 1)
                        mix(g, EC - 1)

                    transpose_x(pe, 0)
                    router(0, 0)
                    transpose_gates(0)
                    run_groups(pe, body)

                @block.scalar
                def _(act):
                    act.sem_inc(silu_done.sem, 2)

                    def exps(g):
                        act.wait_ge(logit_ready.sem, logit_ready.at(g, 1))
                        act.activation(small["b"][:, :, :], small["a"][:, :, :], ACT.Exp).then_inc(expo_ready.sem, 1)

                    def copy_gates(g, par):
                        act.wait_ge(gates_in_psum.sem, gates_in_psum.at(g, 1))
                        act.activation(gates_t[par][:, :], ps_pj[:, :], ACT.Copy).then_inc(gates_t_ready.sem, 1)

                    def silu(g, c):
                        act.wait_ge(hidden_in_psum.sem, hidden_in_psum.at(g, c + 1))
                        act.wait_ge(mixed.sem, mixed.at(g, c + 1))
                        act.activation(hid[c % 2][:, :], bank_g[c % 2], ACT.Silu).then_inc(silu_done.sem, 1)

                    def body(g, par, ahead):
                        for c in range(EC):
                            silu(g, c)
                            if ahead and c == 1:
                                root(act, g + 1)
                            if ahead and c == 3:
                                copy_x_transposed(act, g + 1, 1 - par, mixed, mixed.at(g, 2))
                            if ahead and c == 5:
                                exps(g + 1)
                            if ahead and c == 7:
                                copy_gates(g + 1, 1 - par)

                    root(act, 0)
                    copy_x_transposed(act, 0, 0, None, 0)
                    exps(0)
                    copy_gates(0, 0)
                    run_groups(act, body)

                @block.vector
                def _(dve):
                    dve.sem_inc(times_up.sem, 2)
                    dve.sem_inc(weighted.sem, 2)

                    def choose(g):
                        step = Steps(dve, chain, g)
                        lg, pick, eq = small["c"][:, :, :], small["d"][:, :, :], small["e"][:, :, :]
                        dve.wait_ge(router_in_psum.sem, router_in_psum.at(g, 1))
                        dve.tensor_copy(lg, ps_pj[:, 0:GT * EXPERTS].rearrange("p (u e) -> p u e", u=GT))\
                           .then_inc(router_copied.sem, 1)
                        dve.wait_ge(router_copied.sem, router_copied.at(g, 1))
                        dve.sem_inc(dve_turn.sem, 1)
                        for u in range(GT):
                            dve.max(top8[:, u, :], small["c"][:, u, :]).then_inc(top_ready.sem, 1)
                        dve.wait_ge(top_ready.sem, top_ready.at(g, GT))
                        dve.tensor_tensor(small["a"][:, :, :], lg, top8[:, :, 0:1].broadcast_to([P, GT, EXPERTS]),
                                          ALU.subtract).then_inc(logit_ready.sem, 1)
                        fourth = top8[:, :, TOPK - 1:TOPK].broadcast_to([P, GT, EXPERTS])
                        step(dve.tensor_tensor(pick, lg, fourth, ALU.is_gt))
                        step(dve.tensor_tensor(eq, lg, fourth, ALU.is_equal))
                        step(dve.tensor_reduce(tiny["a"][:, :], pick, AX, ALU.add))
                        src, at = "e", 1
                        for dst in ("f", "g", "f", "g"):
                            step(dve.tensor_copy(small[dst][:, :, 0:at], small[src][:, :, 0:at]))
                            step(dve.tensor_tensor(small[dst][:, :, at:], small[src][:, :, at:],
                                                   small[src][:, :, 0:EXPERTS - at], ALU.add))
                            src, at = dst, 2 * at
                        cnt = small[src][:, :, :]
                        step(dve.tensor_tensor(cnt, cnt, tiny["a"][:, :].unsqueeze(2).broadcast_to([P, GT, EXPERTS]),
                                               ALU.add))
                        step(dve.scalar_tensor_tensor(out=eq, in0=cnt, scalar=float(TOPK), in1=eq,
                                                      op0=ALU.is_le, op1=ALU.mult))
                        step(dve.tensor_tensor(pick, pick, eq, ALU.add))

                    def weigh(g):
                        step = Steps(dve, chain, g, CH - 2)
                        dve.wait_ge(expo_ready.sem, expo_ready.at(g, 1))
                        kept = small["h"][:, :, :]
                        dve.wait_ge(chain.sem, chain.at(g, CH - 2))
                        dve.tensor_tensor(kept, small["b"][:, :, :], small["d"][:, :, :], ALU.mult)\
                           .then_inc(picked.sem, 1)
                        dve.wait_ge(picked.sem, picked.at(g, 1))
                        step(dve.tensor_reduce(tiny["b"][:, :], kept, AX, ALU.add))
                        step(dve.reciprocal(tiny["b"][:, :], tiny["b"][:, :]))
                        dve.wait_ge(gates_in_psum.sem, gates_in_psum.at(g, 0))
                        dve.tensor_tensor(gates[:, :, 0:EXPERTS], kept,
                                          tiny["b"][:, :].unsqueeze(2).broadcast_to([P, GT, EXPERTS]), ALU.mult)\
                           .then_inc(gates_ready.sem, 1)

                    def combine(g, c):
                        h = hid[c % 2][:, :]
                        dve.wait_ge(silu_done.sem, silu_done.at(g, c + 3))
                        dve.tensor_tensor(h, h, bank_u[c % 2], ALU.mult).then_inc(times_up.sem, 1)
                        dve.wait_ge(times_up.sem, times_up.at(g, c + 3))
                        dve.tensor_tensor(h, h, bank_s[c % 2], ALU.mult).then_inc(weighted.sem, 1)

                    def body(g, par, ahead):
                        for c in range(EC):
                            combine(g, c)
                            if ahead and c == 0:
                                norm_stats(dve, g + 1, 1 - par)
                            if ahead and c == 1:
                                normalise(dve, g + 1, 1 - par)
                            if ahead and c == 4:
                                choose(g + 1)
                            if ahead and c == 5:
                                weigh(g + 1)
                        dve.wait_ge(mixed.sem, mixed.at(g, EC + 2))
                        flat = xi[par][:, :, :].rearrange("p u c -> p (u c)")
                        dve.tensor_tensor(flat, ps_o[:, :], flat, ALU.add).then_inc(added.sem, 1)

                    norm_stats(dve, 0, 0)
                    normalise(dve, 0, 0)
                    choose(0)
                    weigh(0)
                    run_groups(dve, body)
            close_stage()

        def channel_mix():
            open_front(1)
            damped = signal("damped", 2)
            blended = signal("blended", 4)
            rk_in_psum = signal("rk_in_psum", 2)
            relu_done = signal("relu_done", 1)
            squared = signal("squared", 1)
            v_done = signal("v_done", 1)
            sig = signal("sig", 1)
            chain = signal("chain", 3)
            bank_r, bank_k, bank_v = ps_scores[0][:, 0, :], ps_scores[1][:, 0, :], ps_o[:, :]
            blend = {"r": wide[0], "k": wide[1]}
            k_act, expo, damp = wide[2], wide[3], {"r": wide[4], "k": wide[5]}

            with nc.Block() as block:
                @block.sync
                def _(sp):
                    move_windows(sp, 1)

                @block.tensor
                def _(pe):
                    def body(g, par, ahead):
                        pe.wait_ge(blended.sem, blended.at(g, 4))
                        pe.wait_ge(relu_done.sem, relu_done.at(g, 0))
                        pe.matmul(bank_k, w_mix["k"][:, :], blend["k"][:, :], start=True, stop=True)\
                          .then_inc(rk_in_psum.sem, 1)
                        pe.wait_ge(sig.sem, sig.at(g, 0))
                        for u in range(GT):
                            last = pe.matmul(bank_r[:, u * P:(u + 1) * P], blend["r"][:, u * P:(u + 1) * P],
                                             w_mix["r"][:, :], start=True, stop=True)
                        last.then_inc(rk_in_psum.sem, 1)
                        if ahead:
                            transpose_x(pe, g + 1)
                        pe.wait_ge(squared.sem, squared.at(g, 1))
                        pe.wait_ge(chain.sem, chain.at(g, 0))
                        for u in range(GT):
                            last = pe.matmul(bank_v[:, u * P:(u + 1) * P], k_act[:, u * P:(u + 1) * P],
                                             w_mix["v"][:, :], start=True, stop=True)
                        last.then_inc(v_done.sem, 1)

                    transpose_x(pe, 0)
                    run_groups(pe, body)

                @block.scalar
                def _(act):
                    def body(g, par, ahead):
                        if ahead:
                            root(act, g + 1)
                        act.wait_ge(rk_in_psum.sem, rk_in_psum.at(g, 1))
                        act.wait_ge(v_done.sem, v_done.at(g, 0))
                        act.activation(k_act[:, :], bank_k, ACT.Relu).then_inc(relu_done.sem, 1)
                        act.wait_ge(rk_in_psum.sem, rk_in_psum.at(g, 2))
                        act.wait_ge(added.sem, added.at(g, 0))
                        act.activation(expo[:, :], bank_r, ACT.Exp, scale=-1.0).then_inc(sig.sem, 1)
                        if ahead:
                            copy_x_transposed(act, g + 1, 1 - par, blended, blended.at(g, 4))

                    root(act, 0)
                    copy_x_transposed(act, 0, 0, None, 0)
                    run_groups(act, body)

                @block.gpsimd
                def _(pool):
                    def body(g, par, ahead):
                        pool.wait_ge(relu_done.sem, relu_done.at(g, 1))
                        pool.tensor_tensor(k_act[:, :], k_act[:, :], k_act[:, :], ALU.mult).then_inc(squared.sem, 1)

                    run_groups(pool, body)

                @block.vector
                def _(dve):
                    def blend_rows(g, par):
                        dve.wait_ge(xt_ready.sem, xt_ready.at(g, 1))
                        dve.wait_ge(rk_in_psum.sem, rk_in_psum.at(g, 0))
                        n = q_t[par][:, :].rearrange("p (b t) -> p b t", t=S)
                        for c in "kr":
                            dve.tensor_scalar(damp[c][:, :], q_t[par][:, :], one_less_mu[c][:, 0:1], None, ALU.mult)\
                               .then_inc(damped.sem, 1)
                        dve.wait_ge(damped.sem, damped.at(g, 2))
                        for c in "kr":
                            b_ = blend[c][:, :].rearrange("p (b t) -> p b t", t=S)
                            d_ = damp[c][:, :].rearrange("p (b t) -> p b t", t=S)
                            dve.scalar_tensor_tensor(out=b_[:, :, 1:S], in0=n[:, :, 1:S], scalar=mu[c][:, 0:1],
                                                     in1=d_[:, :, 0:S - 1], op0=ALU.mult, op1=ALU.add)\
                               .then_inc(blended.sem, 1)
                            dve.tensor_scalar(b_[:, :, 0], n[:, :, 0], mu[c][:, 0:1], None, ALU.mult)\
                               .then_inc(blended.sem, 1)

                    def body(g, par, ahead):
                        step = Steps(dve, chain, g)
                        if ahead:
                            norm_stats(dve, g + 1, 1 - par)
                            normalise(dve, g + 1, 1 - par)
                        dve.wait_ge(sig.sem, sig.at(g, 1))
                        step(dve.tensor_scalar(expo[:, :], expo[:, :], 1.0, None, ALU.add))
                        step(dve.reciprocal(expo[:, :], expo[:, :]))
                        if ahead:
                            blend_rows(g + 1, 1 - par)
                        dve.wait_ge(v_done.sem, v_done.at(g, 1))
                        step(dve.tensor_tensor(expo[:, :], expo[:, :], bank_v, ALU.mult))
                        flat = xi[par][:, :, :].rearrange("p u c -> p (u c)")
                        dve.tensor_tensor(flat, expo[:, :], flat, ALU.add).then_inc(added.sem, 1)

                    for c in "rk":
                        dve.tensor_scalar(one_less_mu[c][:, :], mu[c][:, :], -1.0, 1.0, ALU.mult, ALU.add)\
                           .then_inc(mu_ready.sem, 1)
                    dve.wait_ge(mu_ready.sem, 2)
                    norm_stats(dve, 0, 0)
                    normalise(dve, 0, 0)
                    blend_rows(0, 0)
                    run_groups(dve, body)
            close_stage()

        shift_loaded = signal("shift_loaded")

        def move_shifted(sp, last=False):
            half = P // 2
            dst = out if last else x

            def load(g, par):
                rows = bass.ds(g * GT, GT)
                sp.dma_start(xi[par][:, :, :], x[:, rows, :]).then_inc(x_loaded.sem, 16)
                sp.dma_start(hi[par][:, :, 0:half], x[:, rows, 0:half]).then_inc(shift_loaded.sem, 16)
                for b in range(2):
                    sp.dma_start(hi[par][b * S + 1:(b + 1) * S, :, half:P],
                                 x[b * S:(b + 1) * S - 1, rows, half:P]).then_inc(shift_loaded.sem, 16)
                if last:
                    sp.dma_start(parked[par], out[:, rows, :]).then_inc(shift_loaded.sem, 16)

            def body(g, par, ahead):
                if ahead:
                    sp.wait_ge(stored.sem, stored.at(g, 0))
                    sp.sem_inc(sp_turn.sem, 1)
                    sp.wait_ge(xt_in_psum.sem, xt_in_psum.at(g, 1))
                    sp.sem_inc(sp_turn.sem, 1)
                    load(g + 1, 1 - par)
                sp.wait_ge(added.sem, added.at(g, added.per))
                sp.sem_inc(sp_turn.sem, 1)
                sp.dma_start(dst[:, bass.ds(g * GT, GT), :], xi[par][:, :, :]).then_inc(stored.sem, 16)

            sp.wait_ge(first_rows.sem, 4)
            load(0, 0)
            run_groups(sp, body)
            sp.wait_ge(stored.sem, stored.at(GROUPS, 0))

        first_rows = signal("first_rows")
        tables = signal("tables")

        def prepare_layers():
            with nc.Block() as block:
                @block.gpsimd
                def _(pool):
                    for i in range(2):
                        for b in range(2):
                            pool.memset(hi[i][b * S:b * S + 1, :, P // 2:P], 0.0).then_inc(first_rows.sem, 1)

                @block.vector
                def _(dve):
                    for i in range(2):
                        dve.memset(k_pair[i], 0.0).then_inc(tables.sem, 1)
                        dve.memset(v_pair[i], 0.0).then_inc(tables.sem, 1)
                    for l in range(DEPTH):
                        for a in range(2):
                            sc = rot_scale[:, l, a, :]
                            dve.tensor_tensor(rot[l][:, 2 * a, :], rot_base[:, 2 * a, :], sc, ALU.mult)\
                               .then_inc(tables.sem, 1)
                            for lo, hi_ in ((0, HALF), (HALF, 0)):
                                dve.tensor_tensor(rot[l][:, 2 * a + 1, lo:lo + HALF],
                                                  rot_base[:, 2 * a + 1, lo:lo + HALF],
                                                  sc[:, hi_:hi_ + HALF], ALU.mult).then_inc(tables.sem, 1)

        parked = [t[:, :].rearrange("p (u c) -> p u c", u=GT) for t in (k_t, x_norm_t)]

        def normalise_residual():
            in_out = signal("in_out")
            all_stats = signal("all_stats")
            all_chain = signal("all_chain")
            all_root = signal("all_root")
            centred = signal("centred")
            scaled = signal("scaled")
            bn_all = wide[0][:, 0:TILES * 6].rearrange("p (t s) -> p t s", s=6)
            mean_, gap_, dev_, log_, root_, work_ = (wide[1][:, i * TILES:(i + 1) * TILES] for i in range(6))
            front, back = slice(0, TILES * 5 // 8), slice(TILES * 5 // 8, TILES)

            with nc.Block() as block:
                @block.sync
                def _(sp):
                    sp.dma_start(out, x[:, :, :]).then_inc(in_out.sem, 16)
                    sp.wait_ge(in_out.sem, 16)

                @block.scalar
                def _(act):
                    act.wait_ge(all_chain.sem, 7)
                    act.activation(log_, dev_, ACT.Ln).then_inc(all_root.sem, 1)
                    act.wait_ge(all_root.sem, 1)
                    act.activation(root_, log_, ACT.Exp, scale=-0.5).then_inc(all_root.sem, 1)

                @block.gpsimd
                def _(pool):
                    tiles = x[:, back, :]
                    shape = [P, back.stop - back.start, P]
                    pool.wait_ge(in_out.sem, 16)
                    pool.wait_ge(all_chain.sem, 4)
                    pool.tensor_tensor(tiles, tiles, mean_[:, back].unsqueeze(2).broadcast_to(shape), ALU.subtract)\
                        .then_inc(centred.sem, 1)
                    pool.wait_ge(centred.sem, 1)
                    pool.wait_ge(all_chain.sem, 11)
                    pool.tensor_tensor(tiles, tiles, root_[:, back].unsqueeze(2).broadcast_to(shape), ALU.mult)\
                        .then_inc(centred.sem, 1)

                @block.vector
                def _(dve):
                    with dve.Fori(0, GROUPS) as g:
                        for i in range(GT):
                            dve.bn_stats(bn_all[:, bass.ds(g * GT + i, 1), :].rearrange("p a s -> p (a s)"),
                                         x[:, bass.ds(g * GT + i, 1), :].rearrange("p a c -> p (a c)"))\
                               .then_inc(all_stats.sem, 1)
                    step = Steps(dve, all_chain, 0)
                    dve.wait_ge(all_stats.sem, TILES)
                    step(dve.tensor_tensor(mean_, bn_all[:, :, 1], bn_all[:, :, 4], ALU.add))
                    step(dve.tensor_tensor(gap_, bn_all[:, :, 1], bn_all[:, :, 4], ALU.subtract))
                    step(dve.tensor_tensor(dev_, bn_all[:, :, 2], bn_all[:, :, 5], ALU.add))
                    step(dve.tensor_scalar(mean_, mean_, 0.5, None, ALU.mult))
                    step(dve.tensor_tensor(gap_, gap_, gap_, ALU.mult))
                    step(dve.tensor_scalar(dev_, dev_, 1.0 / P, LN_EPS, ALU.mult, ALU.add))
                    step(dve.scalar_tensor_tensor(out=dev_, in0=gap_, scalar=0.25, in1=dev_, op0=ALU.mult,
                                                  op1=ALU.add))
                    tiles = x[:, front, :]
                    shape = [P, front.stop, P]
                    dve.wait_ge(in_out.sem, 16)
                    dve.tensor_tensor(tiles, tiles, mean_[:, front].unsqueeze(2).broadcast_to(shape), ALU.subtract)\
                       .then_inc(scaled.sem, 1)
                    dve.wait_ge(all_root.sem, 2)
                    step(dve.tensor_tensor(work_, root_, root_, ALU.mult))
                    step(dve.tensor_tensor(work_, work_, dev_, ALU.mult))
                    step(dve.tensor_scalar(work_, work_, -0.5, 1.5, ALU.mult, ALU.add))
                    step(dve.tensor_tensor(root_, root_, work_, ALU.mult))
                    dve.wait_ge(scaled.sem, 1)
                    dve.tensor_tensor(tiles, tiles, root_[:, front].unsqueeze(2).broadcast_to(shape), ALU.mult)\
                       .then_inc(scaled.sem, 1)
            close_stage()

        def local_attention(l):
            open_front(GT, norm=False)
            shift_loaded.opens(3 * 16)
            qk_in_psum = signal("qk_in_psum", 2 * GT)
            v_in_psum = signal("lv_in_psum", GT)
            squared = signal("l_squared", 2 * GT)
            norms = signal("norms", 3 * GT)
            l_root = signal("l_root", 2 * GT)
            l_newton = signal("l_newton", 4 * GT)
            products = signal("products", 6 * GT)
            rotated = signal("rotated", 2 * GT)
            unit = signal("unit", 2 * GT)
            qk_turned = signal("qk_turned", 2 * GT)
            q_copied = signal("q_copied", GT)
            k_copied = signal("k_copied", 2 * GT)
            v_copied = signal("v_copied", 2 * GT)
            scored = signal("scored", GT)
            mask_added = signal("mask_added", GT)
            max_ready = signal("max_ready", GT)
            shifted = signal("shifted", GT)
            exp_ready = signal("exp_ready", GT)
            sums_ready = signal("sums_ready", GT)
            rec_ready = signal("rec_ready", GT)
            turned = signal("turned", GT)
            pt_copied = signal("pt_low", GT)
            summed = signal("summed", GT)
            o_ready = signal("o_ready", GT)
            ot_in_psum = signal("ot_in_psum", GT)
            ot_copied = signal("ot_ready", GT)
            y_ready = signal("y_ready", GT)

            bank_qk = [ps_scores[0][:, i, :] for i in range(2)]
            bank_s, bank_t = ps_pt[0], ps_pt[1]
            sq = [wide[0], wide[1]]
            part = [[wide[2], wide[3]], [wide[4], wide[5]]]
            qt, vp, kp = big["qt"], v_pair[0], k_pair[0]
            pl, pt, o_, ot = big["pl"], big["pt"], big["o"], big["ot"]
            nrm, nlog, nroot, nwork = (norm8[n] for n in "abcd")

            with nc.Block() as block:
                @block.sync
                def _(sp):
                    move_shifted(sp)

                @block.tensor
                def _(pe):
                    def transpose_window(g, par):
                        pe.wait_ge(shift_loaded.sem, shift_loaded.at(g, 48))
                        pe.wait_ge(x_loaded.sem, x_loaded.at(g, 16))
                        for u in range(GT):
                            last = pe.transpose(ps_pj[:, u * P:(u + 1) * P], hi[par][:, u, :], ident[:, :])
                        last.then_inc(xt_in_psum.sem, 1)

                    def project(g, u, par):
                        h = q_t[par]
                        if u == 0:
                            pe.wait_ge(xt_ready.sem, xt_ready.at(g, 1))
                        pe.wait_ge(products.sem, products.at(g, 6 * u))
                        for i in range(2):
                            pe.matmul(bank_qk[i], h[:, u * P:(u + 1) * P], w_qkv[l][:, i * INNER:(i + 1) * INNER],
                                      start=True, stop=True).then_inc(qk_in_psum.sem, 1)
                        pe.wait_ge(v_copied.sem, v_copied.at(g, 2 * u))
                        for b in range(2):
                            for j in range(2):
                                last = pe.matmul(ps_scores[1][j * S:(j + 1) * S, b, :],
                                                 h[:, (2 * u + b) * S:(2 * u + b + 1) * S],
                                                 w_qkv[l][:, 2 * INNER:3 * INNER], start=True, stop=True)
                        last.then_inc(v_in_psum.sem, 1)

                    def turn_qk(g, u, last_turned):
                        pe.wait_ge(unit.sem, unit.at(g, 2 * u + 1))
                        pe.wait_ge(added.sem, added.at(*last_turned[0]))
                        for r in range(LPAIRS):
                            last = pe.transpose(ps_pj[:, r * P:(r + 1) * P], part[0][0][:, r * P:(r + 1) * P],
                                                ident[:, :])
                        last.then_inc(qk_turned.sem, 1)
                        pe.wait_ge(unit.sem, unit.at(g, 2 * u + 2))
                        pe.wait_ge(pt_copied.sem, pt_copied.at(*last_turned[1]))
                        for r in range(LPAIRS):
                            last = pe.transpose(bank_t[:, r * P:(r + 1) * P], part[1][0][:, r * P:(r + 1) * P],
                                                ident[:, :])
                        last.then_inc(qk_turned.sem, 1)

                    def scores(g, u):
                        pe.wait_ge(q_copied.sem, q_copied.at(g, u + 1))
                        pe.wait_ge(k_copied.sem, k_copied.at(g, 2 * u + 2))
                        pe.wait_ge(ot_copied.sem, ot_copied.at(g, u))
                        for r in range(LPAIRS):
                            for b in range(2):
                                last = pe.matmul(bank_s[b * S:(b + 1) * S, r * P:(r + 1) * P],
                                                 qt[:, r * P + b * S:r * P + (b + 1) * S],
                                                 kp[:, r, b, :, :].rearrange("p j k -> p (j k)"), start=True, stop=True)
                        last.then_inc(scored.sem, 1)

                    def turn_probs(g, u):
                        pe.wait_ge(exp_ready.sem, exp_ready.at(g, u + 1))
                        for r in range(LPAIRS):
                            last = pe.transpose(bank_t[:, r * P:(r + 1) * P], pl[:, r * P:(r + 1) * P], ident[:, :])
                        last.then_inc(turned.sem, 1)

                    def weigh_values(g, u):
                        pe.wait_ge(pt_copied.sem, pt_copied.at(g, u + 1))
                        pe.wait_ge(v_copied.sem, v_copied.at(g, 2 * u + 2))
                        pe.wait_ge(o_ready.sem, o_ready.at(g, u))
                        for r in range(LPAIRS):
                            for b in range(2):
                                last = pe.matmul(ps_o[b * S:(b + 1) * S, r * P:(r + 1) * P],
                                                 pt[:, r * P + b * S:r * P + (b + 1) * S],
                                                 vp[:, b, r, :, :].rearrange("p j d -> p (j d)"), start=True, stop=True)
                        last.then_inc(summed.sem, 1)

                    def project_o(g, u, copied):
                        pe.wait_ge(o_ready.sem, o_ready.at(g, u + 1))
                        for r in range(LPAIRS):
                            last = pe.transpose(bank_s[:, r * P:(r + 1) * P], o_[:, r * P:(r + 1) * P], ident[:, :])
                        last.then_inc(ot_in_psum.sem, 1)
                        pe.wait_ge(ot_copied.sem, ot_copied.at(g, u + 1))
                        if copied is not None:
                            pe.wait_ge(q_copied.sem, q_copied.at(*copied))
                        for r in range(LPAIRS):
                            last = pe.matmul(ps_pj[:, 0:P], ot[:, r * P:(r + 1) * P], w_lo[l][:, r, :],
                                             start=r == 0, stop=r == LPAIRS - 1)
                        last.then_inc(y_ready.sem, 1)

                    def body(g, par, ahead):
                        for u in range(GT):
                            nxt = (g, u + 1) if u < GT - 1 else (g + 1, 0)
                            more = ahead or u < GT - 1
                            scores(g, u)
                            if more:
                                project(*nxt, par if u < GT - 1 else 1 - par)
                            turn_probs(g, u)
                            weigh_values(g, u)
                            if ahead and u == 1:
                                pe.wait_ge(added.sem, added.at(g, 1))
                                transpose_window(g + 1, 1 - par)
                                pe.wait_ge(xt_ready.sem, xt_ready.at(g + 1, 1))
                            if more:
                                turn_qk(*nxt, ((g, u), (g, u + 1)))
                            project_o(g, u, (nxt[0], nxt[1] + 1) if more else None)

                    pe.wait_ge(tables.sem, 4 + 6 * DEPTH)
                    transpose_window(0, 0)
                    pe.wait_ge(xt_ready.sem, xt_ready.at(0, 1))
                    project(0, 0, 0)
                    turn_qk(0, 0, ((0, 0), (0, 0)))
                    run_groups(pe, body)

                @block.scalar
                def _(act):
                    def copy_window(g, par, wait_use):
                        act.wait_ge(xt_in_psum.sem, xt_in_psum.at(g, 1))
                        if wait_use:
                            act.wait_ge(v_in_psum.sem, v_in_psum.at(g - 1, 0))
                        act.activation(q_t[par][:, :], ps_pj[:, :], ACT.Copy).then_inc(xt_ready.sem, 1)

                    def squares(g, u):
                        for i in range(2):
                            act.wait_ge(qk_in_psum.sem, qk_in_psum.at(g, 2 * u + i + 1))
                            act.wait_ge(norms.sem, norms.at(g, 3 * u))
                            act.activation(sq[i][:, :], bank_qk[i], ACT.Square).then_inc(squared.sem, 1)

                    def roots(g, u):
                        act.wait_ge(norms.sem, norms.at(g, 3 * u + 3))
                        act.wait_ge(l_newton.sem, l_newton.at(g, 4 * u))
                        act.activation(nlog, nrm, ACT.Ln).then_inc(l_root.sem, 1)
                        act.wait_ge(l_root.sem, l_root.at(g, 2 * u + 1))
                        act.activation(nroot, nlog, ACT.Exp, scale=-0.5).then_inc(l_root.sem, 1)

                    def copy_v(g, u):
                        act.wait_ge(v_in_psum.sem, v_in_psum.at(g, u + 1))
                        act.wait_ge(summed.sem, summed.at(g, u))
                        for j in range(2):
                            rows = slice(j * S, (j + 1) * S)
                            src = ps_scores[1][rows, :, :].rearrange("p b (r j d) -> p b r j d", r=LPAIRS, j=2)
                            act.activation(vp[rows, :, :, j, :], src[:, :, :, j, :], ACT.Copy)\
                               .then_inc(v_copied.sem, 1)

                    def copy_qk(g, u):
                        act.wait_ge(qk_turned.sem, qk_turned.at(g, 2 * u + 1))
                        act.wait_ge(scored.sem, scored.at(g, u))
                        act.activation(qt[:, :], ps_pj[:, :], ACT.Copy).then_inc(q_copied.sem, 1)
                        act.wait_ge(qk_turned.sem, qk_turned.at(g, 2 * u + 2))
                        for j in range(2):
                            rows = slice(j * S, (j + 1) * S)
                            act.activation(kp[rows, :, :, j, :],
                                           bank_t[rows, :].rearrange("p (r b k) -> p r b k", r=LPAIRS, b=2),
                                           ACT.Copy).then_inc(k_copied.sem, 1)

                    def exponentials(g, u):
                        act.wait_ge(shifted.sem, shifted.at(g, u + 1))
                        act.activation(pl[:, :], pl[:, :], ACT.Exp, scale=8.0).then_inc(exp_ready.sem, 1)

                    def copy_pt(g, u):
                        act.wait_ge(turned.sem, turned.at(g, u + 1))
                        act.wait_ge(summed.sem, summed.at(g, u))
                        act.activation(pt[:, :], bank_t[:, :], ACT.Copy).then_inc(pt_copied.sem, 1)

                    def copy_ot(g, u):
                        act.wait_ge(ot_in_psum.sem, ot_in_psum.at(g, u + 1))
                        act.wait_ge(y_ready.sem, y_ready.at(g, u))
                        act.activation(ot[:, :], bank_s[:, :], ACT.Copy).then_inc(ot_copied.sem, 1)

                    def body(g, par, ahead):
                        for u in range(GT):
                            nxt = (g, u + 1) if u < GT - 1 else (g + 1, 0)
                            more = ahead or u < GT - 1
                            if more:
                                squares(*nxt)
                            exponentials(g, u)
                            if more:
                                roots(*nxt)
                            copy_pt(g, u)
                            if more:
                                copy_v(*nxt)
                            if ahead and u == 1:
                                copy_window(g + 1, 1 - par, True)
                            if more:
                                copy_qk(*nxt)
                            copy_ot(g, u)

                    copy_window(0, 0, False)
                    squares(0, 0)
                    roots(0, 0)
                    copy_v(0, 0)
                    copy_qk(0, 0)
                    run_groups(act, body)

                @block.gpsimd
                def _(pool):
                    def unite(g, u):
                        for i in range(2):
                            a, b_ = part[i][0][:, :], part[i][1][:, :]
                            pool.wait_ge(products.sem, products.at(g, 6 * u + 3 * i + 3))
                            pool.tensor_tensor(a, a, b_, ALU.add).then_inc(rotated.sem, 1)
                        for i in range(2):
                            pool.wait_ge(rotated.sem, rotated.at(g, 2 * u + i + 1))
                            pool.wait_ge(l_newton.sem, l_newton.at(g, 4 * u + 4))
                            a = part[i][0][:, :].rearrange("p (h d) -> p h d", d=LD)
                            pool.tensor_tensor(a, a, nroot[:, i, :].unsqueeze(2).broadcast_to([P, LHEADS, LD]),
                                               ALU.mult).then_inc(unit.sem, 1)

                    def body(g, par, ahead):
                        for u in range(GT):
                            if u < GT - 1:
                                unite(g, u + 1)
                            elif ahead:
                                unite(g + 1, 0)

                    unite(0, 0)
                    run_groups(pool, body)

                @block.vector
                def _(dve):
                    def rotate(g, u):
                        for i in range(2):
                            dve.wait_ge(squared.sem, squared.at(g, 2 * u + i + 1))
                            if i == 0:
                                dve.wait_ge(l_root.sem, l_root.at(g, 2 * u))
                            dve.tensor_reduce(nwork[:, i, :], sq[i][:, :].rearrange("p (h d) -> p h d", d=LD),
                                              AX, ALU.add).then_inc(norms.sem, 1)
                        dve.wait_ge(norms.sem, norms.at(g, 3 * u + 2))
                        dve.tensor_scalar(nrm, nwork, 1e-24, float(2 ** LOG_SCALE), ALU.max, ALU.mult)\
                           .then_inc(norms.sem, 1)
                        dve.wait_ge(qk_turned.sem, qk_turned.at(g, 2 * u))
                        for i in range(2):
                            src = bank_qk[i].rearrange("p (h d) -> p h d", d=LD)
                            a, b_ = (part[i][n][:, :].rearrange("p (h d) -> p h d", d=LD) for n in range(2))

                            def table(n, lo, w_):
                                return rot[l][:, n, lo:lo + w_].unsqueeze(1).broadcast_to([P, LHEADS, w_])
                            dve.tensor_tensor(a, src, table(2 * i, 0, LD), ALU.mult).then_inc(products.sem, 1)
                            dve.tensor_tensor(b_[:, :, 0:HALF], src[:, :, HALF:LD], table(2 * i + 1, 0, HALF),
                                              ALU.mult).then_inc(products.sem, 1)
                            dve.tensor_tensor(b_[:, :, HALF:LD], src[:, :, 0:HALF], table(2 * i + 1, HALF, HALF),
                                              ALU.mult).then_inc(products.sem, 1)
                        step = Steps(dve, l_newton, g, 4 * u)
                        dve.wait_ge(l_root.sem, l_root.at(g, 2 * u + 2))
                        step(dve.tensor_tensor(nwork, nroot, nroot, ALU.mult))
                        step(dve.tensor_tensor(nwork, nwork, nrm, ALU.mult))
                        step(dve.tensor_scalar(nwork, nwork, -0.5, 1.5, ALU.mult, ALU.add))
                        step(dve.tensor_tensor(nroot, nroot, nwork, ALU.mult))

                    def softmax(g, u):
                        p3 = pl[:, :].rearrange("p (h k) -> p h k", k=S)
                        dve.wait_ge(scored.sem, scored.at(g, u + 1))
                        dve.wait_ge(turned.sem, turned.at(g, u))
                        dve.tensor_tensor(p3, bank_s[:, :].rearrange("p (h k) -> p h k", k=S),
                                          causal[:, :].unsqueeze(1).broadcast_to([P, LHEADS, S]), ALU.add)\
                           .then_inc(mask_added.sem, 1)
                        dve.wait_ge(mask_added.sem, mask_added.at(g, u + 1))
                        dve.tensor_reduce(row_max[0][:, 0:LHEADS], p3, AX, ALU.max).then_inc(max_ready.sem, 1)
                        dve.wait_ge(max_ready.sem, max_ready.at(g, u + 1))
                        dve.tensor_tensor(p3, p3, row_max[0][:, 0:LHEADS].unsqueeze(2).broadcast_to([P, LHEADS, S]),
                                          ALU.subtract).then_inc(shifted.sem, 1)

                    def sums(g, u):
                        dve.wait_ge(exp_ready.sem, exp_ready.at(g, u + 1))
                        dve.tensor_reduce(row_max[1][:, 0:LHEADS], pl[:, :].rearrange("p (h k) -> p h k", k=S),
                                          AX, ALU.add).then_inc(sums_ready.sem, 1)
                        dve.wait_ge(sums_ready.sem, sums_ready.at(g, u + 1))
                        dve.reciprocal(row_max[1][:, 0:LHEADS], row_max[1][:, 0:LHEADS]).then_inc(rec_ready.sem, 1)

                    def divide(g, u):
                        dve.wait_ge(summed.sem, summed.at(g, u + 1))
                        dve.wait_ge(rec_ready.sem, rec_ready.at(g, u + 1))
                        dve.wait_ge(ot_in_psum.sem, ot_in_psum.at(g, u))
                        dve.tensor_tensor(o_[:, :].rearrange("p (h d) -> p h d", d=LD),
                                          ps_o[:, :].rearrange("p (h d) -> p h d", d=LD),
                                          row_max[1][:, 0:LHEADS].unsqueeze(2).broadcast_to([P, LHEADS, LD]),
                                          ALU.mult).then_inc(o_ready.sem, 1)

                    def residual(g, u, par):
                        dve.wait_ge(y_ready.sem, y_ready.at(g, u + 1))
                        dve.tensor_tensor(xi[par][:, u, :], xi[par][:, u, :], ps_pj[:, 0:P], ALU.add)\
                           .then_inc(added.sem, 1)

                    def body(g, par, ahead):
                        for u in range(GT):
                            softmax(g, u)
                            if u:
                                residual(g, u - 1, par)
                            if u < GT - 1:
                                rotate(g, u + 1)
                            elif ahead:
                                rotate(g + 1, 0)
                            sums(g, u)
                            divide(g, u)
                        residual(g, GT - 1, par)

                    rotate(0, 0)
                    run_groups(dve, body)
            close_stage()

        def gated_mlp(l):
            NC = len(HC)
            open_front(1)
            last = l == DEPTH - 1
            shift_loaded.opens(4 * 16 if last else 3 * 16)
            g_in_psum = signal("g_in_psum", NC)
            a_in_psum = signal("a_in_psum", NC)
            gelu_done = signal("gelu_done", NC)
            gated = signal("gated", NC)
            y_done = signal("y_done", 1)
            unparked = signal("unparked", 1 if last else 0)
            bank_g = [ps_scores[i][:, 0, :] for i in range(2)]
            bank_a = [ps_scores[i][:, 1, :] for i in range(2)]

            with nc.Block() as block:
                @block.sync
                def _(sp):
                    move_shifted(sp, last)

                @block.tensor
                def _(pe):
                    def body(g, par, ahead):
                        pe.wait_ge(xt_ready.sem, xt_ready.at(g, 1))
                        for c, (at, m) in enumerate(HC):
                            pe.wait_ge(gated.sem, gated.at(g, max(c - 1, 0)))
                            pe.matmul(bank_g[c % 2][0:m, :], w_up1[l][:, HID + at:HID + at + m], q_t[par][:, :],
                                      start=True, stop=True).then_inc(g_in_psum.sem, 1)
                            pe.matmul(bank_a[c % 2][0:m, :], w_up1[l][:, at:at + m], q_t[par][:, :],
                                      start=True, stop=True).then_inc(a_in_psum.sem, 1)
                        if ahead:
                            transpose_x(pe, g + 1)
                        pe.wait_ge(added.sem, added.at(g, 0))
                        for c, (at, m) in enumerate(HC):
                            pe.wait_ge(gated.sem, gated.at(g, c + 1))
                            for u in range(GT):
                                pe.matmul(ps_o[:, u * P:(u + 1) * P], wide[c][0:m, u * P:(u + 1) * P],
                                          w_dn[l][0:m, c, :], start=c == 0 and u == 0, stop=False,
                                          skip_group_check=True)
                        for u in range(GT):
                            last = pe.matmul(ps_o[:, u * P:(u + 1) * P], ones[:, :], b_dn[l][:, :], start=False,
                                             stop=True, skip_group_check=True)
                        last.then_inc(y_done.sem, 1)

                    transpose_x(pe, 0)
                    run_groups(pe, body)

                @block.scalar
                def _(act):
                    def copy_normed(g, par, wait_use):
                        act.wait_ge(xt_in_psum.sem, xt_in_psum.at(g, 1))
                        if wait_use:
                            act.wait_ge(a_in_psum.sem, a_in_psum.at(g - 1, 0))
                        act.activation(q_t[par][:, :], ps_pj[:, :], ACT.Identity, scale=ln_gb[l][:, 0:1],
                                       bias=ln_gb[l][:, 1:2]).then_inc(xt_ready.sem, 1)

                    def body(g, par, ahead):
                        if ahead:
                            root(act, g + 1)
                        for c, (at, m) in enumerate(HC):
                            act.wait_ge(g_in_psum.sem, g_in_psum.at(g, c + 1))
                            act.wait_ge(y_done.sem, y_done.at(g, 0))
                            act.activation(wide[3 + c][0:m, :], bank_g[c % 2][0:m, :], ACT.Gelu,
                                           bias=b_up1[l][0:m, NC + c:NC + c + 1]).then_inc(gelu_done.sem, 1)
                        if ahead:
                            copy_normed(g + 1, 1 - par, True)

                    root(act, 0)
                    copy_normed(0, 0, False)
                    run_groups(act, body)

                @block.vector
                def _(dve):
                    def body(g, par, ahead):
                        if ahead:
                            dve.wait_ge(shift_loaded.sem, shift_loaded.at(g + 1, shift_loaded.per))
                            norm_stats(dve, g + 1, 1 - par, hi)
                        flat = xi[par][:, :, :].rearrange("p u c -> p (u c)")
                        if last:
                            dve.tensor_tensor(flat, flat, parked[par].rearrange("p u c -> p (u c)"), ALU.add)\
                               .then_inc(unparked.sem, 1)
                        for c, (at, m) in enumerate(HC):
                            dve.wait_ge(a_in_psum.sem, a_in_psum.at(g, c + 1))
                            dve.wait_ge(gelu_done.sem, gelu_done.at(g, c + 1))
                            dve.wait_ge(y_done.sem, y_done.at(g, 0))
                            dve.scalar_tensor_tensor(out=wide[c][0:m, :], in0=bank_a[c % 2][0:m, :],
                                                     scalar=b_up1[l][0:m, c:c + 1], in1=wide[3 + c][0:m, :],
                                                     op0=ALU.add, op1=ALU.mult).then_inc(gated.sem, 1)
                            if ahead and c == 0:
                                normalise(dve, g + 1, 1 - par, hi)
                        dve.wait_ge(y_done.sem, y_done.at(g, 1))
                        if last:
                            dve.wait_ge(unparked.sem, unparked.at(g, 1))
                        dve.tensor_tensor(flat, ps_o[:, :], flat, ALU.add).then_inc(added.sem, 1)

                    dve.wait_ge(shift_loaded.sem, shift_loaded.at(0, shift_loaded.per))
                    norm_stats(dve, 0, 0, hi)
                    normalise(dve, 0, 0, hi)
                    run_groups(dve, body)
            close_stage()

        flat_big = kblk[0][:, :, :].rearrange("p h t -> p (h t)")
        big = {n: flat_big[:, i * 512:(i + 1) * 512] for i, n in enumerate(("qt", "pl", "pt", "o", "ot"))}
        k_pair = [flat_big[:, 2560 + i * 1024:2560 + (i + 1) * 1024]
                  .rearrange("p (r b j k) -> p r b j k", r=LPAIRS, b=2, j=2) for i in range(2)]
        v_pair = [flat_big[:, 4608 + i * 1024:4608 + (i + 1) * 1024]
                  .rearrange("p (b r j d) -> p b r j d", r=LPAIRS, b=2, j=2) for i in range(2)]
        norm8 = {n: small[n][:, 0, :].rearrange("p (i h) -> p i h", i=2) for n in "abcd"}

        mu_ready = signal("mu_ready")

        def layers():
            prepare_layers()
            normalise_residual()
            for l in range(DEPTH):
                local_attention(l)
                gated_mlp(l)

        steps = {
            "F3": layers,
            "F0": lambda: (prepare_low_rank(), low_rank_experts()),
            "F1": mixture,
            "F2": channel_mix,
            "L0": lambda: cross_attention("L0", 1.0 / np.sqrt(HD)),
            "L1": lambda: cross_attention("L1", 1.0 / np.sqrt(HD), mask=mask_l1_sb),
            "L2": lambda: cross_attention("L2", 1.0, mask_per_seq=mask_l2, project=False, relu=True),
            "L3": lambda: cross_attention("L3", 1.0 / np.sqrt(HD), mask=mask_l3_sb),
        }
        for n in STEPS:
            steps[n]()

        with nc.Block() as block:
            @block.sync
            def _(sp):
                written = signal("written")
                if "F3" not in STEPS:
                    sp.dma_start(out, x[:, :, :]).then_inc(written.sem, 16)
                    sp.wait_ge(written.sem, 16)


STEPS = ["L0","F0","L1","F1","L2","F2","L3","F3"]


def rotary_tables():
    half = np.arange(0, LD, 2, dtype=np.float32)
    t = np.arange(S, dtype=np.float32)
    freqs = t[:, None] * (np.float32(1) / np.float32(10000) ** (half / np.float32(LD)))[None, :]
    freqs = np.concatenate([freqs, freqs], axis=1)
    base = (half + np.float32(0.4 * LD)) / np.float32(1.4 * LD)
    scale = base[None, :] ** ((t - S // 2) / np.float32(S // 2))[:, None]
    scale = np.concatenate([scale, scale], axis=1)
    sign = np.where(np.arange(LD) < HALF, -1.0, 1.0).astype(np.float32)
    cos, sin, up = np.cos(freqs), np.sin(freqs) * sign, np.float32(2 ** (LOG_SCALE // 2))
    t4 = np.stack([cos * scale * up, sin * scale * up, cos / scale * up, sin / scale * up], axis=1)
    return np.concatenate([t4, t4]).astype(np.float32)


def columns(b):
    out = np.zeros((DEPTH, P, 2 * len(HC)), b.dtype)
    for i in range(2):
        for c, (at, m) in enumerate(HC):
            out[:, :m, i * len(HC) + c] = b[:, i, at:at + m]
    return out


def chunks(w2):
    out = np.zeros((DEPTH, P, len(HC), P), w2.dtype)
    for c, (at, m) in enumerate(HC):
        out[:, :m, c, :] = w2[:, at:at + m, :]
    return out


def kernel(**inputs):
    import concourse.bacc as bacc
    from concourse.bass_utils import run_bass_kernel_spmd

    a = {k: np.asarray(v) for k, v in inputs.items()}

    def row(v):
        return v.reshape(1, -1)

    arrays = {
        "x_in": a["x"].reshape(TILES, P, P).transpose(1, 0, 2),
        "ctx_t": a["ctx_1024"].reshape(TILES * P, P).T,
        "mask_l2": a["mask_Bx1xSxS2_ff0"].reshape(TILES, P, S).transpose(1, 0, 2),
        "mask_l3": a["mask_SxS2_bk1"],
        "L0_q": a["L0_xattn_w_q"].T, "L0_k": a["L0_xattn_w_k"].T,
        "L0_v": a["L0_xattn_w_v"].T, "L0_o": a["L0_xattn_w_o"].T,
        "L1_q": a["L1_xattn_Wq"].T, "L1_k": a["L1_xattn_Wk"].T,
        "L1_v": a["L1_xattn_Wv"].T, "L1_o": a["L1_xattn_Wo"].T,
        "L2_o": a["L2_xattn_wo_w"].T,
        "L3_q": a["L3_xattn_Wq"], "L3_k": a["L3_xattn_Wk"],
        "L3_v": a["L3_xattn_Wv"], "L3_o": a["L3_xattn_Wo"],
        "bL1_v": row(a["L1_xattn_bv"]), "bL1_o": row(a["L1_xattn_bo"]), "bL2_o": row(a["L2_xattn_wo_b"]),
        "bL3_v": row(a["L3_xattn_bv"]), "bL3_o": row(a["L3_xattn_bo"]),
        "low_W": a["L0_ffn_W"].T, "low_Wp": a["L0_ffn_Wp"], "low_WpT": a["L0_ffn_Wp"].T,
        "low_sim": a["L0_ffn_sim"], "low_bp": a["L0_ffn_bp"].reshape(-1, 1),
        "low_temp": np.broadcast_to(a["L0_ffn_temp"].reshape(1, 1), (P, 1)),
        "low_Wd": np.concatenate([a[f"L0_ffn_Wd{i}"] for i in range(NLR)]).T,
        "low_Wu": np.concatenate([a[f"L0_ffn_Wu{i}"] for i in range(NLR)], axis=1).T,
        "moe_gate": a["L1_ffn_gate_w"].T,
        "moe_1": a["L1_ffn_w1"].transpose(1, 0, 2), "moe_3": a["L1_ffn_w3"].transpose(1, 0, 2),
        "moe_2": a["L1_ffn_w2"].reshape(EC, P, P).transpose(1, 0, 2),
        "mix_r": a["L2_ffn_W_r"].T, "mix_k": a["L2_ffn_W_k"].T, "mix_v": a["L2_ffn_W_v"].T,
        "mu_r": a["L2_ffn_mu_r"].reshape(P, 1), "mu_k": a["L2_ffn_mu_k"].reshape(P, 1),
        "rot": rotary_tables(), "rot_scale": np.broadcast_to(
            np.stack([a["L3_ffn_q_scale"], a["L3_ffn_k_scale"]], axis=1), (P, DEPTH, 2, LD)),
        "wqkv": a["L3_ffn_wqkv"], "lo": a["L3_ffn_wo"].reshape(DEPTH, LPAIRS, P, P).transpose(0, 2, 1, 3),
        "up1": a["L3_ffn_w1"], "b_up1": columns(a["L3_ffn_b1"].reshape(DEPTH, 2, HID)),
        "dn": chunks(a["L3_ffn_w2"]), "b_dn": a["L3_ffn_b2"].reshape(DEPTH, 1, P),
        "ln": np.stack([a["L3_ffn_ln_g"], a["L3_ffn_ln_b"]], axis=2),
        "bL3_q": a["L3_xattn_bq"].reshape(P, 1), "bL3_k": a["L3_xattn_bk"].reshape(P, 1),
    }
    nc = bacc.Bacc("TRN2", target_bir_lowering=False, num_devices=1)
    feed, args = {}, {}
    for name, v in arrays.items():
        v = np.ascontiguousarray(v)
        feed["in_" + name] = v
        args[name] = nc.dram_tensor("in_" + name, v.shape, mybir.dt.from_np(v.dtype), kind="ExternalInput").ap()
    out = nc.dram_tensor("out", (P, TILES, P), F32, kind="ExternalOutput").ap()
    main = {n: args.pop(n) for n in ("x_in", "ctx_t", "mask_l2", "mask_l3")}
    build_program(nc, args, main["x_in"], main["ctx_t"], main["mask_l2"], main["mask_l3"], out)
    r = run_bass_kernel_spmd(nc, [feed], core_ids=[0])
    return r.results[0]["out"].transpose(1, 0, 2).reshape(NSEQ, S, P)
```

```python
from contextlib import ExitStack

import numpy as np
import concourse.bass as bass
from concourse import mybir

F32 = mybir.dt.float32
ACT = mybir.ActivationFunctionType
ALU = mybir.AluOpType
AX = mybir.AxisListType.X

P = 128
S = 64
NSEQ = 128
TILES = NSEQ * S // P
GT = 4
GROUPS = TILES // GT
GTOK = GT * P
GSEQ = GTOK // S
HEADS = 16
HD = P // HEADS
PAIRS = HEADS // 2
VC = HD + 1
LN_EPS = 1e-5
LN_EXP = "natural_log_exp_and_others"
PROJ, RANKS = 32, (1, 2, 4, 8)
NLR, RSUM = len(RANKS), sum(RANKS)
ROUTE = PROJ + NLR + RSUM
LOG_SCALE = 20
EXPERTS, INTER, TOPK = 16, 64, 4
EC = EXPERTS * INTER // P
LHEADS, LD, LPAIRS = 8, 64, 4
INNER = LHEADS * LD
HALF = LD // 2
DEPTH = 2
HID = 341
HC = [(c * P, min(P, HID - c * P)) for c in range((HID + P - 1) // P)]
GROUP_SIGNALS = """
a_in_psum added blended bn_done c_loaded chain damped exp_ready expo_ready g_in_psum gated
gates_in_psum gates_ready gates_t_ready gelu_done hidden_in_psum k_copied k_in_psum k_placed
kt_ready l_newton l_root l_squared ln_ready logit_ready lv_in_psum m_loaded mask_added max_ready
mixed newton norm_ready norms o_ready ot_in_psum ot_ready last_y picked products pt_ready pt_low q_copied
q_in_psum qk_in_psum qk_turned qt_ready r0_ready rec_ready relu_done rk_in_psum root_steps rotated
route_in_psum router_copied scored shift_loaded shifted sig silu_done squared summed
sums_ready times_up top_ready turned unit unparked v_copied v_done v_even v_in_psum v_odd var_ready
weighted x_norm_ready xt_in_psum xt_ready y_done y_ready""".split()
NEG = -(2.0 ** 100)


class Signal:

    def __init__(self, sem):
        self.sem, self.base, self.per, self.ahead = sem, 0, 0, 0

    def opens(self, per, ahead=0):
        self.per, self.ahead = per, ahead

    def closes(self, groups):
        self.base += self.per * groups + self.ahead
        self.per = self.ahead = 0

    def at(self, g, k):
        return g * self.per + (self.base + k)


def build_program(nc, w, x_in, ctx_t, mask_l2, mask_l3, out):
    with ExitStack() as ctx:
        def sb(name, shape, dt=F32):
            return ctx.enter_context(nc.sbuf_tensor(name, shape, dt))

        signals = {}

        def signal(name, per=0, ahead=0):
            if name not in signals:
                assert per == 0 or name in GROUP_SIGNALS, name
                signals[name] = Signal(ctx.enter_context(nc.semaphore(name)))
            signals[name].opens(per, ahead)
            return signals[name]

        def close_stage(groups=GROUPS):
            for s in signals.values():
                s.closes(groups)

        for n in GROUP_SIGNALS:
            signal(n).base = 1

        x = sb("x", [P, TILES, P])
        ident = sb("ident", [P, P])
        ones = sb("ones", [P, P])
        attn_w = {n: sb("w_" + n, [P, P]) for n in (
            "L0_q", "L0_k", "L0_v", "L0_o", "L1_q", "L1_k", "L1_v", "L1_o", "L2_o",
            "L3_q", "L3_k", "L3_v", "L3_o")}
        row_bias = {n: sb("b_" + n, [P, P]) for n in ("L1_v", "L1_o", "L2_o", "L3_v", "L3_o")}
        col_bias = {n: sb("b_" + n, [P, 1]) for n in ("L3_q", "L3_k")}
        mask_l1_sb = sb("mask_l1_sb", [P, S])
        mask_l3_in = sb("mask_l3_in", [P, S], mybir.dt.uint8)

        ci = [sb(f"ci{i}", [P, GSEQ, 2, S]) for i in range(2)]
        kblk = [sb(f"kblk{i}", [P, HEADS, GTOK]) for i in range(2)]
        q_t = [sb(f"q_t{i}", [P, GTOK]) for i in range(2)]
        k_t = sb("k_t", [P, GTOK])
        v2 = [sb(f"v2{i}", [P, GSEQ, PAIRS, 2, VC]) for i in range(2)]
        x_norm = sb("x_norm", [P, GT, P])
        x_norm_t = sb("x_norm_t", [P, GTOK])
        bn = sb("bn", [P, GT, 6])
        mean = sb("mean", [P, GT])
        mean_gap = sb("mean_gap", [P, GT])
        dev = sb("dev", [P, GT])
        var_eps = sb("var_eps", [P, GT])
        var_log = sb("var_log", [P, GT])
        r0 = sb("r0", [P, GT])
        r_sq = sb("r_sq", [P, GT])
        rstd = sb("rstd", [P, GT])
        probs = [sb(f"probs{i}", [P, HEADS, S]) for i in range(2)]
        row_max = [sb(f"row_max{i}", [P, HEADS]) for i in range(2)]
        mask2 = [sb(f"mask2{i}", [P, GT, S]) for i in range(2)]
        probs_t = sb("probs_t", [P, PAIRS, P])
        wide = [t[:, :, :].rearrange("p a b -> p (a b)")[:, i * GTOK:(i + 1) * GTOK]
                for t in (*probs, probs_t) for i in range(2)]
        hi = [t[:, :, :, :].rearrange("p b j k -> p (b j k)")[:, 0:GTOK].rearrange("p (u c) -> p u c", u=GT)
              for t in ci]
        rec = sb("rec", [P, PAIRS, 2])
        o = sb("o", [P, HEADS, HD])
        o_t = sb("o_t", [P, P])

        w_low = {"W": sb("w_low", [P, P]), "Wp": sb("w_low_p", [PROJ, P]), "sim": sb("w_sim", [PROJ, NLR]),
                 "bp": sb("w_bp", [PROJ, 1]), "temp": sb("w_temp", [P, 1])}
        w_route = sb("w_route", [P, ROUTE])
        b_route = sb("b_route", [P, ROUTE])
        w_up = sb("w_up", [P, P])
        w_gate = sb("w_gate", [P, EXPERTS])
        w_1 = sb("w_1", [P, EXPERTS, INTER])
        w_3 = sb("w_3", [P, EXPERTS, INTER])
        w_2 = sb("w_2", [P, EC, P])
        pick_expert = sb("pick_expert", [P, EC, P])
        w_mix = {n: sb("w_mix_" + n, [P, P]) for n in "rkv"}
        mu = {n: sb("mu_" + n, [P, 1]) for n in "rk"}
        one_less_mu = {n: sb("one_less_mu_" + n, [P, 1]) for n in "rk"}
        w_qkv = [sb(f"w_qkv{l}", [P, 3 * INNER]) for l in range(DEPTH)]
        w_lo = [sb(f"w_lo{l}", [P, LPAIRS, P]) for l in range(DEPTH)]
        rot_base = sb("rot_base", [P, 4, LD])
        rot = [sb(f"rot{l}", [P, 4, LD]) for l in range(DEPTH)]
        rot_scale = sb("rot_scale", [P, DEPTH, 2, LD])
        w_up1 = [sb(f"w_up1{l}", [P, 2 * HID]) for l in range(DEPTH)]
        b_up1 = [sb(f"b_up1{l}", [P, 2 * len(HC)]) for l in range(DEPTH)]
        w_dn = [sb(f"w_dn{l}", [P, len(HC), P]) for l in range(DEPTH)]
        b_dn = [sb(f"b_dn{l}", [P, P]) for l in range(DEPTH)]
        ln_gb = [sb(f"ln_gb{l}", [P, 2]) for l in range(DEPTH)]
        causal = sb("causal", [P, S])
        ident_16 = sb("ident_16", [P, P], mybir.dt.bfloat16)
        masks = {n: sb("mask_16_" + n, [P, S], mybir.dt.bfloat16) for n in ("L1", "L3", "causal")}
        gates = sb("gates", [P, GT, P])
        gates_t = [k_t, x_norm_t]
        route = sb("route", [P, GT, ROUTE])
        small = {n: sb("small_" + n, [P, GT, 16]) for n in "abcdefgh"}
        tiny = {n: sb("tiny_" + n, [P, GT]) for n in "abcdef"}
        top8 = sb("top8", [P, GT, 8])

        ps_scores = [ctx.enter_context(nc.psum_tensor(f"ps_s{i}", [P, 2, 512], F32)) for i in range(2)]
        ps_pt = ctx.enter_context(nc.psum_tensor("ps_pt", [P, 2, 512], F32))
        ps_o = ctx.enter_context(nc.psum_tensor("ps_o", [P, 512], F32))
        ps_pj = ctx.enter_context(nc.psum_tensor("ps_pj", [P, 512], F32))

        loaded = signal("loaded")
        zeroed = signal("zeroed")
        marked = signal("marked")
        drawn = signal("drawn")
        loads = [(x[:, :, :], x_in), (mask_l3_in[0:S, :], mask_l3), (mask_l3_in[S:P, :], mask_l3)]
        loads += [(attn_w[n][:, :], w[n]) for n in attn_w]
        loads += [(row_bias[n][0:1, :], w["b" + n]) for n in row_bias]
        loads += [(col_bias[n][:, :], w["b" + n]) for n in col_bias]

        loads += [(w_low[n][:, :], w["low_" + n]) for n in ("W", "Wp", "sim", "bp", "temp")]
        loads += [(w_route[:, 0:PROJ], w["low_WpT"]), (w_route[:, PROJ + NLR:ROUTE], w["low_Wd"]),
                  (w_up[0:RSUM, :], w["low_Wu"]), (w_gate[:, :], w["moe_gate"]), (w_1[:, :, :], w["moe_1"]),
                  (w_3[:, :, :], w["moe_3"]), (w_2[:, :, :], w["moe_2"])]
        loads += [(w_mix[n][:, :], w["mix_" + n]) for n in "rkv"]
        loads += [(mu[n][:, :], w["mu_" + n]) for n in "rk"]

        loads += [(rot_base[:, :, :], w["rot"]), (rot_scale[:, :, :, :], w["rot_scale"])]
        for l in range(DEPTH):
            loads += [(w_qkv[l][:, :], w["wqkv"][l]), (w_lo[l][:, :, :], w["lo"][l]), (w_up1[l][:, :], w["up1"][l]),
                      (b_up1[l][:, :], w["b_up1"][l]), (w_dn[l][:, :, :], w["dn"][l]),
                      (b_dn[l][0:1, :], w["b_dn"][l]), (ln_gb[l][:, :], w["ln"][l])]

        with nc.Block() as block:
            @block.sync
            def _(sp):
                sp.wait_ge(zeroed.sem, 8 + DEPTH)
                for dst, src in loads:
                    sp.dma_start(dst, src).then_inc(loaded.sem, 16)
                sp.wait_ge(loaded.sem, 16 * len(loads))

            @block.vector
            def _(dve):
                for n in row_bias:
                    dve.memset(row_bias[n][:, :], 0.0).then_inc(zeroed.sem, 1)
                dve.memset(ones[:, :], 1.0).then_inc(zeroed.sem, 1)
                dve.memset(w_up[:, :], 0.0).then_inc(zeroed.sem, 1)
                dve.memset(gates[:, :, :], 0.0).then_inc(zeroed.sem, 1)
                for l in range(DEPTH):
                    dve.memset(b_dn[l][:, :], 0.0).then_inc(zeroed.sem, 1)
                for i in range(2):
                    dve.memset(kblk[i][:, :, :], 0.0).then_inc(zeroed.sem, 1)
                    dve.memset(v2[i][:, :, :, :, :], 0.0).then_inc(zeroed.sem, 1)
                dve.wait_ge(zeroed.sem, 12 + DEPTH)
                for i in range(2):
                    for j in range(2):
                        dve.memset(v2[i][j * S:(j + 1) * S, :, :, j, HD:VC], 1.0).then_inc(marked.sem, 1)
                dve.wait_ge(loaded.sem, 16 * len(loads))
                dve.tensor_scalar(masks["L3"][:, :], mask_l3_in[:, :], -NEG, NEG, ALU.mult, ALU.add)\
                   .then_inc(marked.sem, 1)
                dve.wait_ge(drawn.sem, 10)
                for to, of in ((ident_16, ident), (masks["L1"], mask_l1_sb), (masks["causal"], causal)):
                    dve.tensor_copy(to[:, :], of[:, :]).then_inc(marked.sem, 1)

            @block.gpsimd
            def _(pool):
                for n in GROUP_SIGNALS:
                    pool.sem_inc(signals[n].sem, 1)
                pool.memset(ident[:, :], 0.0).then_inc(drawn.sem, 1)
                pool.wait_ge(drawn.sem, 1)
                pool.affine_select(out=ident[:, :], in_=ident[:, :], compare_op=ALU.not_equal, fill=1.0,
                                   base=0, pattern=[[-1, P]], channel_multiplier=1).then_inc(drawn.sem, 1)
                pool.wait_ge(drawn.sem, 2)
                pool.memset(mask_l1_sb[:, :], 0.0).then_inc(drawn.sem, 1)
                for b in range(2):
                    rows = mask_l1_sb[b * S:(b + 1) * S, :]
                    pool.wait_ge(drawn.sem, 3 + 2 * b)
                    pool.affine_select(out=rows, in_=rows, compare_op=ALU.is_gt, fill=NEG,
                                       base=0, pattern=[[-1, S]], channel_multiplier=1)\
                        .then_inc(drawn.sem, 1)
                    pool.wait_ge(drawn.sem, 4 + 2 * b)
                    pool.memset(rows[0:1, 0:1], 0.0).then_inc(drawn.sem, 1)
                pool.wait_ge(drawn.sem, 7)
                pool.memset(causal[:, :], 0.0).then_inc(drawn.sem, 1)
                for b in range(2):
                    rows = causal[b * S:(b + 1) * S, :]
                    pool.wait_ge(drawn.sem, 8 + b)
                    pool.affine_select(out=rows, in_=rows, compare_op=ALU.is_ge, fill=NEG,
                                       base=0, pattern=[[-1, S]], channel_multiplier=1)\
                        .then_inc(drawn.sem, 1)
                pool.wait_ge(drawn.sem, 10)
                pool.memset(pick_expert[:, :, :], 0.0).then_inc(drawn.sem, 1)
                pool.wait_ge(drawn.sem, 11)
                picks = pick_expert[:, :, :].rearrange("p c (j i) -> p c j i", j=2)
                pool.affine_select(out=picks, in_=picks, compare_op=ALU.not_equal, fill=1.0, base=0,
                                   pattern=[[-2, EC], [-1, 2], [0, INTER]], channel_multiplier=1)\
                    .then_inc(drawn.sem, 1)

        sp_turn = signal("sp_turn")
        pool_turn = signal("pool_turn")
        dve_turn = signal("dve_turn")
        bn_done = signal("bn_done")
        var_ready = signal("var_ready")
        ln_ready = signal("ln_ready")
        r0_ready = signal("r0_ready")
        newton = signal("newton")
        x_norm_ready = signal("x_norm_ready")
        xt_in_psum = signal("xt_in_psum")
        xt_ready = signal("xt_ready")
        added = signal("added")

        def open_front(added_per, norm=True):
            for s, per in ((xt_in_psum, 1), (xt_ready, 1), (added, added_per)):
                s.opens(per)
            if norm:
                for s, per in ((bn_done, GT + 6), (var_ready, 1), (ln_ready, 1), (r0_ready, 1), (newton, 4),
                               (x_norm_ready, GT)):
                    s.opens(per)

        def tile_of(g, u):
            return x[:, bass.ds(g * GT + u, 1), :].rearrange("p a c -> p (a c)")

        def window_of(g):
            return x[:, bass.ds(g * GT, GT), :].rearrange("p u c -> p (u c)")

        def norm_stats(dve, g, shifted=None):
            for u in range(GT):
                rows = tile_of(g, u) if shifted is None else shifted[:, u, :]
                dve.bn_stats(bn[:, u, :], rows).then_inc(bn_done.sem, 1)
            dve.wait_ge(bn_done.sem, bn_done.at(g, GT))
            dve.tensor_tensor(mean[:, :], bn[:, :, 1], bn[:, :, 4], ALU.add).then_inc(bn_done.sem, 1)
            dve.tensor_tensor(mean_gap[:, :], bn[:, :, 1], bn[:, :, 4], ALU.subtract)\
               .then_inc(bn_done.sem, 1)
            dve.tensor_tensor(dev[:, :], bn[:, :, 2], bn[:, :, 5], ALU.add).then_inc(bn_done.sem, 1)
            dve.wait_ge(bn_done.sem, bn_done.at(g, GT + 3))
            dve.tensor_scalar(mean[:, :], mean[:, :], 0.5, None, ALU.mult).then_inc(bn_done.sem, 1)
            dve.tensor_tensor(mean_gap[:, :], mean_gap[:, :], mean_gap[:, :], ALU.mult)\
               .then_inc(bn_done.sem, 1)
            dve.tensor_scalar(dev[:, :], dev[:, :], 1.0 / P, LN_EPS, ALU.mult, ALU.add)\
               .then_inc(bn_done.sem, 1)
            dve.wait_ge(bn_done.sem, bn_done.at(g, GT + 6))
            dve.scalar_tensor_tensor(out=var_eps[:, :], in0=mean_gap[:, :], scalar=0.25,
                                     in1=dev[:, :], op0=ALU.mult, op1=ALU.add)\
               .then_inc(var_ready.sem, 1)

        def normalise(dve, g, shifted=None):
            dve.wait_ge(r0_ready.sem, r0_ready.at(g, 1))
            dve.tensor_tensor(r_sq[:, :], r0[:, :], r0[:, :], ALU.mult).then_inc(newton.sem, 1)
            dve.wait_ge(newton.sem, newton.at(g, 1))
            dve.tensor_tensor(r_sq[:, :], r_sq[:, :], var_eps[:, :], ALU.mult).then_inc(newton.sem, 1)
            dve.wait_ge(newton.sem, newton.at(g, 2))
            dve.tensor_scalar(r_sq[:, :], r_sq[:, :], -0.5, 1.5, ALU.mult, ALU.add)\
               .then_inc(newton.sem, 1)
            dve.wait_ge(newton.sem, newton.at(g, 3))
            dve.tensor_tensor(rstd[:, :], r0[:, :], r_sq[:, :], ALU.mult).then_inc(newton.sem, 1)
            dve.wait_ge(newton.sem, newton.at(g, 4))
            dve.wait_ge(xt_in_psum.sem, xt_in_psum.at(g, 0))
            for u in range(GT):
                rows = tile_of(g, u) if shifted is None else shifted[:, u, :]
                dve.tensor_scalar(x_norm[:, u, :], rows, mean[:, u:u + 1],
                                  rstd[:, u:u + 1], ALU.subtract, ALU.mult)\
                   .then_inc(x_norm_ready.sem, 1)

        def root(act, g):
            act.wait_ge(var_ready.sem, var_ready.at(g, 1))
            act.activation(var_log[:, :], var_eps[:, :], ACT.Ln).then_inc(ln_ready.sem, 1)
            act.wait_ge(ln_ready.sem, ln_ready.at(g, 1))
            act.wait_ge(newton.sem, newton.at(g, 0))
            act.activation(r0[:, :], var_log[:, :], ACT.Exp, scale=-0.5).then_inc(r0_ready.sem, 1)

        def transpose_x(pe, g):
            pe.wait_ge(x_norm_ready.sem, x_norm_ready.at(g, GT))
            for u in range(GT):
                last = pe.transpose(ps_pj[:, u * P:(u + 1) * P], x_norm[:, u, :], ident[:, :])
            last.then_inc(xt_in_psum.sem, 1)

        def run_groups_2(eng, body):
            with eng.Fori(0, GROUPS // 2 - 1) as pair:
                body(pair * 2, 0, True, True)
                body(pair * 2 + 1, 1, True, True)
            body(GROUPS - 2, 0, True, False)
            body(GROUPS - 1, 1, False, False)

        def cross_attention(name, scale, mask=None, mask_per_seq=None, project=True, relu=False):
            wq, wk, wv, wo = (attn_w.get(f"{name}_{n}", ident) for n in "qkvo")
            bv, bo = row_bias.get(name + "_v"), row_bias.get(name + "_o")
            bq, bk = col_bias.get(name + "_q"), col_bias.get(name + "_k")
            masked = mask_per_seq is not None

            open_front(GT)
            c_loaded = signal("c_loaded", 32)
            m_loaded = signal("m_loaded", 16 if mask_per_seq is not None else 0)
            k_placed = signal("k_placed", 16 * HEADS)
            k_in_psum = signal("k_in_psum", 1 if project else 0)
            kt_ready = signal("kt_ready", 1 if project else 0)
            v_in_psum = signal("v_in_psum", 2)
            v_even = signal("v_even", 2)
            v_odd = signal("v_odd", 2)
            q_in_psum = signal("q_in_psum", 1 if project else 0)
            qt_ready = signal("qt_ready", 1 if project else 0)
            scored = signal("scored", GT)
            max_ready = signal("max_ready", GT)
            mask_added = signal("mask_added", GT if masked else 0)
            shifted = signal("shifted", GT)
            exp_ready = signal("exp_ready", GT)
            turned = signal("turned", GT, 2)
            pt_ready = signal("pt_ready", GT)
            summed = signal("summed", GT)
            rec_ready = signal("rec_ready", 2 * GT)
            o_ready = signal("o_ready", 2 * GT)
            ot_in_psum = signal("ot_in_psum", GT)
            ot_ready = signal("ot_ready", GT)
            last_y = signal("last_y", 1)

            q_signal = qt_ready if project else xt_ready
            accumulated = ps_o[:, 0:PAIRS * 2 * 2 * VC].rearrange("p (r b j c) -> p r b j c", b=2, j=2, c=VC)
            projected = ps_o[:, 384:384 + P]

            with nc.Block() as block:
                @block.sync
                def _(sp):
                    def load(g, par, first):
                        if not first:
                            sp.wait_ge(v_in_psum.sem, v_in_psum.at(g - 1, 1))
                            sp.sem_inc(sp_turn.sem, 1)
                        src = ctx_t[:, bass.ds(g * GTOK, GTOK)].rearrange("p (b k) -> p b k", k=S)
                        for j in range(2):
                            sp.dma_start(ci[par][:, :, j, :], src).then_inc(c_loaded.sem, 16)

                    def load_mask(g, par, first):
                        if mask_per_seq is None:
                            return
                        if not first:
                            sp.wait_ge(mask_added.sem, mask_added.at(g - 1, 1))
                            sp.sem_inc(sp_turn.sem, 1)
                        sp.dma_start(mask2[par][:, :, :], mask_per_seq[:, bass.ds(g * GT, GT), :])\
                          .then_inc(m_loaded.sem, 16)

                    def place_keys(g, par, first):
                        if project:
                            sp.wait_ge(kt_ready.sem, kt_ready.at(g, 1))
                        else:
                            sp.wait_ge(c_loaded.sem, c_loaded.at(g, 32))
                        sp.sem_inc(sp_turn.sem, 1)
                        if not first:
                            sp.wait_ge(scored.sem, scored.at(g - 1, 1))
                            sp.sem_inc(sp_turn.sem, 1)
                        src = k_t[:, :] if project else ci[par][:, :, 0, :]
                        for h in range(HEADS):
                            rows = slice(h * HD, (h + 1) * HD)
                            dst = kblk[par][rows, h, :]
                            if not project:
                                dst = dst.rearrange("p (b k) -> p b k", k=S)
                            sp.dma_start(dst, src[rows]).then_inc(k_placed.sem, 16)

                    def body(g, par, ahead, ahead2):
                        if ahead2:
                            load(g + 2, par, False)
                            load_mask(g + 2, par, False)
                            place_keys(g + 2, par, False)

                    load(0, 0, True)
                    load_mask(0, 0, True)
                    place_keys(0, 0, True)
                    load(1, 1, False)
                    load_mask(1, 1, False)
                    place_keys(1, 1, False)
                    run_groups_2(sp, body)

                @block.vector
                def _(dve):
                    def values_even(g, par, c, first):
                        if not first:
                            dve.wait_ge(summed.sem, summed.at(g - 1, 0))
                        dve.wait_ge(v_in_psum.sem, v_in_psum.at(g, c + 1))
                        src = ps_pj[0:S, :].rearrange("p (b r j d) -> p b r j d", b=4, r=PAIRS, j=2)
                        dve.tensor_copy(v2[par][0:S, 4 * c:4 * c + 4, :, 0, 0:HD], src[:, :, :, 0, :])\
                           .then_inc(v_even.sem, 1)

                    def softmax(g, u, par):
                        s = u % 2
                        scores = ps_scores[s][:, :, :].rearrange("p a (h k) -> p (a h) k", k=S)
                        if u == 0 and mask_per_seq is not None:
                            dve.wait_ge(m_loaded.sem, m_loaded.at(g, 16))
                        dve.wait_ge(scored.sem, scored.at(g, u + 1))
                        dve.wait_ge(turned.sem, turned.at(g, u))
                        if masked:
                            m = mask2[par][:, u, :].unsqueeze(1).broadcast_to([P, HEADS, S])
                            dve.tensor_tensor(probs[s][:, :, :], scores, m, ALU.add).then_inc(mask_added.sem, 1)
                            scores = probs[s][:, :, :]
                            dve.wait_ge(mask_added.sem, mask_added.at(g, u + 1))
                        dve.tensor_reduce(row_max[s][:, :], scores, AX, ALU.max).then_inc(max_ready.sem, 1)
                        dve.wait_ge(max_ready.sem, max_ready.at(g, u + 1))
                        dve.tensor_tensor(probs[s][:, :, :], scores,
                                          row_max[s][:, :].unsqueeze(2).broadcast_to([P, HEADS, S]),
                                          ALU.subtract).then_inc(shifted.sem, 1)

                    def divide(g, u):
                        dve.wait_ge(summed.sem, summed.at(g, u + 1))
                        dve.wait_ge(ot_in_psum.sem, ot_in_psum.at(g, u))
                        for b in range(2):
                            rows = slice(b * S, (b + 1) * S)
                            dve.reciprocal(rec[rows, :, :], accumulated[rows, :, b, :, HD]).then_inc(rec_ready.sem, 1)
                        for b in range(2):
                            rows = slice(b * S, (b + 1) * S)
                            dve.wait_ge(rec_ready.sem, rec_ready.at(g, 2 * u + b + 1))
                            dve.tensor_tensor(o[rows, :, :].rearrange("p (r j) d -> p r j d", j=2),
                                              accumulated[rows, :, b, :, 0:HD],
                                              rec[rows, :, :].unsqueeze(3).broadcast_to([S, PAIRS, 2, HD]),
                                              ALU.mult).then_inc(o_ready.sem, 1)

                    def add_residual(g, u):
                        if u == GT - 1:
                            dve.wait_ge(last_y.sem, last_y.at(g, 1))
                        else:
                            dve.wait_ge(summed.sem, summed.at(g, u + 2))
                        rows = tile_of(g, u)
                        if relu:
                            dve.scalar_tensor_tensor(out=rows, in0=projected, scalar=0.0, in1=rows, op0=ALU.max,
                                                     op1=ALU.add).then_inc(added.sem, 1)
                        else:
                            dve.tensor_tensor(rows, projected, rows, ALU.add).then_inc(added.sem, 1)

                    def body(g, par, ahead, ahead2):
                        other = 1 - par
                        softmax(g, 1, par)
                        divide(g, 0)
                        softmax(g, 2, par)
                        divide(g, 1)
                        add_residual(g, 0)
                        if ahead:
                            values_even(g + 1, other, 0, False)
                        softmax(g, 3, par)
                        if ahead2:
                            norm_stats(dve, g + 2)
                        divide(g, 2)
                        add_residual(g, 1)
                        if ahead:
                            softmax(g + 1, 0, other)
                        if ahead2:
                            normalise(dve, g + 2)
                        divide(g, 3)
                        add_residual(g, 2)
                        if ahead:
                            values_even(g + 1, other, 1, False)
                        add_residual(g, 3)

                    norm_stats(dve, 0)
                    normalise(dve, 0)
                    for c in range(2):
                        values_even(0, 0, c, True)
                    norm_stats(dve, 1)
                    normalise(dve, 1)
                    softmax(0, 0, 0)
                    run_groups_2(dve, body)

                @block.scalar
                def _(act):
                    act.preload_act_table_set(LN_EXP)
                    def keys(g):
                        if not project:
                            return
                        act.wait_ge(k_in_psum.sem, k_in_psum.at(g, 1))
                        act.wait_ge(k_placed.sem, k_placed.at(g, 0))
                        if bk is None:
                            act.activation(k_t[:, :], ps_pj[:, :], ACT.Copy).then_inc(kt_ready.sem, 1)
                        else:
                            act.activation(k_t[:, :], ps_pj[:, :], ACT.Identity, bias=bk[:, 0:1])\
                               .then_inc(kt_ready.sem, 1)

                    def values_odd(g, par, c, first):
                        if not first:
                            act.wait_ge(summed.sem, summed.at(g - 1, 0))
                        act.wait_ge(v_in_psum.sem, v_in_psum.at(g, c + 1))
                        src = ps_pj[S:P, :].rearrange("p (b r j d) -> p b r j d", b=4, r=PAIRS, j=2)
                        act.activation(v2[par][S:P, 4 * c:4 * c + 4, :, 1, 0:HD], src[:, :, :, 1, :], ACT.Copy)\
                           .then_inc(v_odd.sem, 1)

                    def x_transposed(g, par, first):
                        act.wait_ge(xt_in_psum.sem, xt_in_psum.at(g, 1))
                        if project:
                            act.wait_ge(q_in_psum.sem, q_in_psum.at(g, 0))
                            act.activation(x_norm_t[:, :], ps_pj[:, :], ACT.Copy).then_inc(xt_ready.sem, 1)
                        else:
                            if not first:
                                act.wait_ge(scored.sem, scored.at(g - 1, 0))
                            act.activation(q_t[par][:, :], ps_pj[:, :], ACT.Copy).then_inc(xt_ready.sem, 1)

                    def queries(g, par, first):
                        if not project:
                            return
                        act.wait_ge(q_in_psum.sem, q_in_psum.at(g, 1))
                        if not first:
                            act.wait_ge(scored.sem, scored.at(g - 1, 0))
                        if bq is None:
                            act.activation(q_t[par][:, :], ps_pj[:, :], ACT.Copy).then_inc(qt_ready.sem, 1)
                        else:
                            act.activation(q_t[par][:, :], ps_pj[:, :], ACT.Identity, bias=bq[:, 0:1])\
                               .then_inc(qt_ready.sem, 1)

                    def exponentials(g, u):
                        act.wait_ge(shifted.sem, shifted.at(g, u + 1))
                        p = probs[u % 2][:, :, :]
                        act.activation(p, p, ACT.Exp, scale=scale).then_inc(exp_ready.sem, 1)

                    def copy_turned(g, u):
                        act.wait_ge(turned.sem, turned.at(g, 2 + u + 1))
                        act.wait_ge(summed.sem, summed.at(g, u))
                        act.activation(probs_t[:, :, :], ps_pt[:, :, :].rearrange("p a (r t) -> p (a r) t", t=P),
                                       ACT.Copy).then_inc(pt_ready.sem, 1)

                    def o_transposed(g, u):
                        act.wait_ge(ot_in_psum.sem, ot_in_psum.at(g, u + 1))
                        act.activation(o_t[:, :], ps_pt[:, 0, 0:P], ACT.Copy).then_inc(ot_ready.sem, 1)

                    def body(g, par, ahead, ahead2):
                        other = 1 - par
                        copy_turned(g, 0)
                        exponentials(g, 1)
                        if ahead:
                            x_transposed(g + 1, other, False)
                        copy_turned(g, 1)
                        o_transposed(g, 0)
                        exponentials(g, 2)
                        if ahead:
                            queries(g + 1, other, False)
                            values_odd(g + 1, other, 0, False)
                        copy_turned(g, 2)
                        o_transposed(g, 1)
                        exponentials(g, 3)
                        if ahead2:
                            root(act, g + 2)
                        copy_turned(g, 3)
                        o_transposed(g, 2)
                        if ahead:
                            exponentials(g + 1, 0)
                            values_odd(g + 1, other, 1, False)
                        o_transposed(g, 3)
                        if ahead2:
                            keys(g + 2)

                    keys(0)
                    root(act, 0)
                    x_transposed(0, 0, True)
                    queries(0, 0, True)
                    for c in range(2):
                        values_odd(0, 0, c, True)
                    keys(1)
                    root(act, 1)
                    exponentials(0, 0)
                    run_groups_2(act, body)

                @block.tensor
                def _(pe):
                    pe.sem_inc(turned.sem, 2)

                    def project_k(g, par, first):
                        if not first:
                            pe.wait_ge(v_even.sem, v_even.at(g - 1, 2))
                            pe.wait_ge(v_odd.sem, v_odd.at(g - 1, 2))
                        if project:
                            pe.wait_ge(c_loaded.sem, c_loaded.at(g, 32))
                            pe.matmul(ps_pj[:, :], wk[:, :], ci[par][:, :, 0, :], start=True, stop=True)\
                              .then_inc(k_in_psum.sem, 1)

                    def turn_x(g):
                        if project:
                            pe.wait_ge(kt_ready.sem, kt_ready.at(g, 1))
                        transpose_x(pe, g)

                    def project_q(g):
                        if not project:
                            return
                        pe.wait_ge(xt_ready.sem, xt_ready.at(g, 1))
                        pe.matmul(ps_pj[:, :], wq[:, :], x_norm_t[:, :], start=True, stop=True)\
                          .then_inc(q_in_psum.sem, 1)

                    def project_v(g, par, c):
                        if c == 0:
                            pe.wait_ge(c_loaded.sem, c_loaded.at(g, 32))
                            pe.wait_ge(q_signal.sem, q_signal.at(g, 1))
                        else:
                            pe.wait_ge(v_even.sem, v_even.at(g, 1))
                            pe.wait_ge(v_odd.sem, v_odd.at(g, 1))
                        for b in range(4):
                            twice = ci[par][:, 4 * c + b, :, :].rearrange("p j k -> p (j k)")
                            dst = ps_pj[:, b * P:(b + 1) * P]
                            last = pe.matmul(dst, twice, wv[:, :], start=True, stop=bv is None)
                            if bv is not None:
                                last = pe.matmul(dst, ones[:, :], bv[:, :], start=False, stop=True)
                        last.then_inc(v_in_psum.sem, 1)

                    def scores(g, u, par, reuse=True):
                        if u == 0:
                            pe.wait_ge(q_signal.sem, q_signal.at(g, 1))
                            pe.wait_ge(k_placed.sem, k_placed.at(g, 16 * HEADS))
                        if reuse:
                            free = mask_added if masked else shifted
                            pe.wait_ge(free.sem, free.at(g, u - 1))
                        for half in range(2):
                            if mask is not None:
                                pe.matmul(ps_scores[u % 2][:, half, :].rearrange("p (h k) -> p h k", k=S),
                                          ident_16[:, :], mask[:, :].unsqueeze(1).broadcast_to([P, PAIRS, S]),
                                          start=True, stop=False, skip_group_check=True)
                            for b in range(2):
                                tok = slice((2 * u + b) * S, (2 * u + b + 1) * S)
                                last = pe.matmul(
                                    ps_scores[u % 2][b * S:(b + 1) * S, half, :], q_t[par][:, tok],
                                    kblk[par][:, half * 8:half * 8 + 8, tok], start=mask is None, stop=True,
                                    skip_group_check=mask is not None)
                        last.then_inc(scored.sem, 1)

                    def turn_probs(g, u):
                        pe.wait_ge(exp_ready.sem, exp_ready.at(g, u + 1))
                        flat = probs[u % 2][:, :, :].rearrange("p h k -> p (h k)")
                        for r in range(PAIRS):
                            last = pe.transpose(ps_pt[:, r // 4, (r % 4) * P:(r % 4 + 1) * P],
                                                flat[:, r * P:(r + 1) * P], ident[:, :])
                        last.then_inc(turned.sem, 1)

                    def turn_o(g, u, last_turned):
                        pe.wait_ge(pt_ready.sem, pt_ready.at(g, last_turned + 1))
                        pe.wait_ge(o_ready.sem, o_ready.at(g, 2 * u + 2))
                        pe.transpose(ps_pt[:, 0, 0:P], o[:, :, :].rearrange("p h d -> p (h d)"), ident[:, :])\
                          .then_inc(ot_in_psum.sem, 1)

                    def weigh_values(g, u, par):
                        pe.wait_ge(pt_ready.sem, pt_ready.at(g, u + 1))
                        if u == 0:
                            pe.wait_ge(v_even.sem, v_even.at(g, 2))
                            pe.wait_ge(v_odd.sem, v_odd.at(g, 2))
                        pe.wait_ge(o_ready.sem, o_ready.at(g, 2 * u))
                        pe.wait_ge(added.sem, added.at(g, max(u - 1, 0)))
                        for r in range(PAIRS):
                            n = 4 * VC
                            last = pe.matmul(ps_o[:, r * n:(r + 1) * n], probs_t[:, r, :],
                                             v2[par][:, 2 * u:2 * u + 2, r, :, :], start=True, stop=True)
                        if u:
                            last = project_o(g, u - 1)
                        last.then_inc(summed.sem, 1)

                    def project_o(g, u):
                        pe.wait_ge(ot_ready.sem, ot_ready.at(g, u + 1))
                        last = pe.matmul(projected, o_t[:, :], wo[:, :], start=True, stop=bo is None)
                        if bo is not None:
                            last = pe.matmul(projected, ones[:, :], bo[:, :], start=False, stop=True)
                        return last

                    def body(g, par, ahead, ahead2):
                        other = 1 - par
                        turn_probs(g, 0)
                        scores(g, 2, par)
                        weigh_values(g, 0, par)
                        if ahead:
                            turn_x(g + 1)
                        turn_probs(g, 1)
                        scores(g, 3, par)
                        turn_o(g, 0, 1)
                        if ahead:
                            project_q(g + 1)
                        weigh_values(g, 1, par)
                        if ahead:
                            project_v(g + 1, other, 0)
                        turn_probs(g, 2)
                        if ahead:
                            scores(g + 1, 0, other)
                        turn_o(g, 1, 2)
                        weigh_values(g, 2, par)
                        turn_probs(g, 3)
                        if ahead:
                            scores(g + 1, 1, other)
                        turn_o(g, 2, 3)
                        weigh_values(g, 3, par)
                        if ahead:
                            project_v(g + 1, other, 1)
                        turn_o(g, 3, 3)
                        if ahead2:
                            project_k(g + 2, par, False)
                        pe.wait_ge(added.sem, added.at(g, GT - 1))
                        project_o(g, GT - 1).then_inc(last_y.sem, 1)

                    project_k(0, 0, True)
                    turn_x(0)
                    project_q(0)
                    for c in range(2):
                        project_v(0, 0, c)
                    project_k(1, 1, False)
                    scores(0, 0, 0, False)
                    scores(0, 1, 0, False)
                    run_groups_2(pe, body)
            close_stage()

        def run_groups(eng, body):
            with eng.Fori(0, GROUPS - 2, 2) as g:
                body(g, 0, True)
                body(g + 1, 1, True)
            body(GROUPS - 2, 0, True)
            body(GROUPS - 1, 1, False)

        class Steps:

            def __init__(self, eng, sig, g, k=0):
                self.eng, self.sig, self.g, self.k = eng, sig, g, k

            def __call__(self, ins):
                self.k += 1
                ins.then_inc(self.sig.sem, 1)
                self.eng.wait_ge(self.sig.sem, self.sig.at(self.g, self.k))

        def copy_x_transposed(act, g, par, used, used_value):
            act.wait_ge(xt_in_psum.sem, xt_in_psum.at(g, 1))
            if used is not None:
                act.wait_ge(used.sem, used_value)
            act.activation(q_t[par][:, :], ps_pj[:, :], ACT.Copy).then_inc(xt_ready.sem, 1)

        def prepare_low_rank():
            prep = signal("prep_dve")
            prep_pe, prep_act = signal("prep_pe"), signal("prep_act")
            sim, sq, nrm = w_low["sim"], small["a"][:, 0, 0:NLR], small["b"][:, 0, 0:NLR]
            root_, work = small["c"][:, 0, 0:NLR], small["d"][:, 0, 0:NLR]
            temp = w_low["temp"]
            with nc.Block() as block:
                @block.vector
                def _(dve):
                    step = Steps(dve, prep, 0)
                    step(dve.tensor_tensor(sq[0:PROJ, :], sim[:, :], sim[:, :], ALU.mult))
                    step(dve.tensor_scalar(temp[:, :], temp[:, :], float(np.log(100.0)), None, ALU.min))
                    step(dve.memset(route[0:PROJ, 0:3, 0:P // 4], 0.0))
                    step(dve.memset(wide[0][:, 0:P], 0.0))
                    step(dve.tensor_scalar(wide[0][0:PROJ, 0:P], ones[0:PROJ, :], w_low["bp"][:, 0:1], None, ALU.mult))
                    dve.wait_ge(prep_pe.sem, 1)
                    step(dve.tensor_scalar(nrm, ps_pj[:, 0:NLR], 1e-24, float(2 ** LOG_SCALE), ALU.max, ALU.mult))
                    dve.wait_ge(prep_act.sem, 3)
                    step(dve.tensor_tensor(work, root_, root_, ALU.mult))
                    step(dve.tensor_tensor(work, work, nrm, ALU.mult))
                    step(dve.tensor_scalar(work, work, -0.5, 1.5, ALU.mult, ALU.add))
                    step(dve.tensor_tensor(root_, root_, work, ALU.mult))
                    step(dve.tensor_scalar(root_, root_, float(2 ** LOG_SCALE), None, ALU.mult))
                    step(dve.tensor_scalar(root_, root_, temp[:, 0:1], None, ALU.mult))
                    step(dve.tensor_tensor(sim[:, :], sim[:, :], root_[0:PROJ, :], ALU.mult))
                    dve.wait_ge(prep_pe.sem, 3)
                    step(dve.tensor_copy(w_route[:, PROJ:PROJ + NLR], ps_pj[:, 0:NLR]))
                    step(dve.tensor_copy(b_route[:, 0:PROJ + NLR], ps_o[:, 0:PROJ + NLR]))
                    step(dve.memset(b_route[:, PROJ + NLR:ROUTE], 0.0))

                @block.scalar
                def _(act):
                    act.preload_act_table_set(LN_EXP)
                    act.wait_ge(prep.sem, prep.at(0, 2))
                    act.activation(temp[:, :], temp[:, :], ACT.Exp).then_inc(prep_act.sem, 1)
                    act.wait_ge(prep.sem, prep.at(0, 6))
                    act.activation(work, nrm, ACT.Ln).then_inc(prep_act.sem, 1)
                    act.wait_ge(prep_act.sem, 2)
                    act.activation(root_, work, ACT.Exp, scale=-0.5).then_inc(prep_act.sem, 1)

                @block.tensor
                def _(pe):
                    pe.wait_ge(prep.sem, prep.at(0, 5))
                    pe.matmul(ps_pj[:, 0:NLR], ones[0:PROJ, :], sq[0:PROJ, :], start=True, stop=True)\
                      .then_inc(prep_pe.sem, 1)
                    pe.wait_ge(prep.sem, prep.at(0, 13))
                    pe.matmul(ps_pj[:, 0:NLR], w_low["Wp"][:, :], sim[:, :], start=True, stop=True)\
                      .then_inc(prep_pe.sem, 1)
                    pe.matmul(ps_o[:, 0:PROJ], wide[0][0:PROJ, 0:P], ident[0:PROJ, 0:PROJ], start=True, stop=True)
                    pe.matmul(ps_o[:, PROJ:PROJ + NLR], wide[0][0:PROJ, 0:P], sim[:, :], start=True, stop=True)\
                      .then_inc(prep_pe.sem, 1)

        def low_rank_experts():
            open_front(1)
            route_in_psum = signal("route_in_psum", 1)
            chain = signal("chain", 25)
            norm_ready = signal("norm_ready", 1)
            root_steps = signal("root_steps", 2)
            logit_ready = signal("logit_ready", 1)
            expo_ready = signal("expo_ready", 1)
            gates_ready = signal("gates_ready", NLR)
            gates_in_psum = signal("gates_in_psum", 1)
            gates_t_ready = signal("gates_t_ready", 1)
            y_done = signal("y_done", 1)

            with nc.Block() as block:
                @block.tensor
                def _(pe):
                    def route_and_base(g, par):
                        pe.wait_ge(xt_ready.sem, xt_ready.at(g, 1))
                        pe.wait_ge(chain.sem, chain.at(g, 0))
                        for u in range(GT):
                            last = pe.matmul(ps_pt[:, 0, u * ROUTE:(u + 1) * ROUTE],
                                             q_t[par][:, u * P:(u + 1) * P], w_route[:, :],
                                             start=True, stop=True)
                        last.then_inc(route_in_psum.sem, 1)
                        pe.wait_ge(added.sem, added.at(g, 0))
                        for u in range(GT):
                            pe.matmul(ps_o[:, u * P:(u + 1) * P], q_t[par][:, u * P:(u + 1) * P],
                                      w_low["W"][:, :], start=u == 0, stop=False, skip_group_check=True)

                    def up(g):
                        pe.wait_ge(gates_ready.sem, gates_ready.at(g, NLR))
                        pe.wait_ge(gates_t_ready.sem, gates_t_ready.at(g, 0))
                        for u in range(GT):
                            last = pe.transpose(ps_pt[:, 1, u * P:(u + 1) * P], gates[:, u, :], ident[:, :])
                        last.then_inc(gates_in_psum.sem, 1)
                        pe.wait_ge(gates_t_ready.sem, gates_t_ready.at(g, 1))
                        for u in range(GT):
                            last = pe.matmul(ps_o[:, u * P:(u + 1) * P], gates_t[0][:, u * P:(u + 1) * P],
                                             w_up[:, :], start=False, stop=True, skip_group_check=True)
                        last.then_inc(y_done.sem, 1)

                    def body(g, par, ahead):
                        route_and_base(g, par)
                        if ahead:
                            pe.wait_ge(xt_ready.sem, xt_ready.at(g, 1))
                            transpose_x(pe, g + 1)
                        up(g)

                    transpose_x(pe, 0)
                    run_groups(pe, body)

                @block.scalar
                def _(act):
                    act.preload_act_table_set(LN_EXP)
                    def body(g, par, ahead):
                        act.wait_ge(norm_ready.sem, norm_ready.at(g, 1))
                        act.activation(tiny["b"][:, :], tiny["a"][:, :], ACT.Ln).then_inc(root_steps.sem, 1)
                        act.wait_ge(root_steps.sem, root_steps.at(g, 1))
                        act.activation(tiny["c"][:, :], tiny["b"][:, :], ACT.Exp, scale=-0.5)\
                           .then_inc(root_steps.sem, 1)
                        if ahead:
                            root(act, g + 1)
                        act.wait_ge(logit_ready.sem, logit_ready.at(g, 1))
                        act.activation(small["b"][:, :, 0:NLR], small["a"][:, :, 0:NLR], ACT.Exp)\
                           .then_inc(expo_ready.sem, 1)
                        if ahead:
                            copy_x_transposed(act, g + 1, 1 - par, y_done, y_done.at(g, 0))
                        act.wait_ge(gates_in_psum.sem, gates_in_psum.at(g, 1))
                        act.wait_ge(y_done.sem, y_done.at(g, 0))
                        act.activation(gates_t[0][:, :], ps_pt[:, 1, :], ACT.Copy).then_inc(gates_t_ready.sem, 1)

                    root(act, 0)
                    copy_x_transposed(act, 0, 0, None, 0)
                    run_groups(act, body)

                @block.vector
                def _(dve):
                    def col(t, i):
                        return small[t][:, :, i]

                    def body(g, par, ahead):
                        step = Steps(dve, chain, g)
                        if ahead:
                            norm_stats(dve, g + 1)
                        dve.wait_ge(route_in_psum.sem, route_in_psum.at(g, 1))
                        rs = route[:, :, :]
                        step(dve.tensor_tensor(rs, ps_pt[:, 0, 0:GT * ROUTE].rearrange("p (u c) -> p u c", u=GT),
                                               b_route[:, :].unsqueeze(1).broadcast_to([P, GT, ROUTE]), ALU.add))
                        sq = wide[1][:, 0:GT * PROJ].rearrange("p (u c) -> p u c", u=GT)
                        step(dve.tensor_tensor(sq, rs[:, :, 0:PROJ], rs[:, :, 0:PROJ], ALU.mult))
                        step(dve.tensor_reduce(tiny["d"][:, :], sq, AX, ALU.add))
                        dve.tensor_scalar(tiny["a"][:, :], tiny["d"][:, :], 1e-24, float(2 ** LOG_SCALE),
                                          ALU.max, ALU.mult).then_inc(norm_ready.sem, 1)
                        if ahead:
                            normalise(dve, g + 1)
                        dve.wait_ge(norm_ready.sem, norm_ready.at(g, 1))
                        dve.wait_ge(root_steps.sem, root_steps.at(g, 2))
                        a, b, c, d = (tiny[n][:, :] for n in "abcd")
                        step(dve.tensor_tensor(d, c, c, ALU.mult))
                        step(dve.tensor_tensor(d, d, a, ALU.mult))
                        step(dve.tensor_scalar(d, d, -0.5, 1.5, ALU.mult, ALU.add))
                        step(dve.tensor_tensor(d, d, c, ALU.mult))
                        lg = small["a"][:, :, 0:NLR]
                        step(dve.tensor_tensor(lg, rs[:, :, PROJ:PROJ + NLR],
                                               d.unsqueeze(2).broadcast_to([P, GT, NLR]), ALU.mult))
                        step(dve.tensor_reduce(tiny["e"][:, :], lg, AX, ALU.max))
                        dve.tensor_tensor(lg, lg, tiny["e"][:, :].unsqueeze(2).broadcast_to([P, GT, NLR]),
                                          ALU.subtract).then_inc(logit_ready.sem, 1)
                        dve.wait_ge(logit_ready.sem, logit_ready.at(g, 1))
                        step(dve.tensor_scalar(small["c"][:, :, 0:NLR], lg, 0.0, None, ALU.is_equal))
                        step(dve.tensor_copy(col("d", 0), col("c", 0)))
                        for i in range(1, NLR):
                            step(dve.tensor_tensor(col("e", i), col("c", i), col("d", i - 1), ALU.is_gt))
                            if i < NLR - 1:
                                step(dve.tensor_tensor(col("d", i), col("d", i - 1), col("c", i), ALU.max))
                        step(dve.tensor_copy(col("e", 0), col("c", 0)))
                        dve.wait_ge(expo_ready.sem, expo_ready.at(g, 1))
                        step(dve.tensor_reduce(tiny["f"][:, :], small["b"][:, :, 0:NLR], AX, ALU.add))
                        step(dve.reciprocal(tiny["f"][:, :], tiny["f"][:, :]))
                        step(dve.tensor_tensor(small["e"][:, :, 0:NLR], small["e"][:, :, 0:NLR],
                                               small["b"][:, :, 0:NLR], ALU.mult))
                        step(dve.tensor_tensor(small["e"][:, :, 0:NLR], small["e"][:, :, 0:NLR],
                                               tiny["f"][:, :].unsqueeze(2).broadcast_to([P, GT, NLR]), ALU.mult))
                        dve.wait_ge(gates_in_psum.sem, gates_in_psum.at(g, 0))
                        at = 0
                        for i, r in enumerate(RANKS):
                            dve.tensor_tensor(gates[:, :, at:at + r], rs[:, :, PROJ + NLR + at:PROJ + NLR + at + r],
                                              small["e"][:, :, i:i + 1].broadcast_to([P, GT, r]), ALU.mult)\
                               .then_inc(gates_ready.sem, 1)
                            at += r
                        while step.k < 25:
                            step.k += 1
                            dve.sem_inc(chain.sem, 1)
                        dve.wait_ge(y_done.sem, y_done.at(g, 1))
                        flat = window_of(g)
                        dve.tensor_tensor(flat, ps_o[:, :], flat, ALU.add).then_inc(added.sem, 1)

                    norm_stats(dve, 0)
                    normalise(dve, 0)
                    run_groups(dve, body)
            close_stage()

        def mixture():
            open_front(1)
            CH = 16
            router_in_psum = signal("route_in_psum", 1)
            router_copied = signal("router_copied", 1)
            chain = signal("chain", CH)
            picked = signal("picked", 1)
            top_ready = signal("top_ready", GT)
            logit_ready = signal("logit_ready", 1)
            expo_ready = signal("expo_ready", 1)
            gates_ready = signal("gates_ready", 1)
            gates_in_psum = signal("gates_in_psum", 1)
            gates_t_ready = signal("gates_t_ready", 1)
            hidden_in_psum = signal("hidden_in_psum", EC)
            silu_done = signal("silu_done", EC, 2)
            times_up = signal("times_up", EC, 2)
            weighted = signal("weighted", EC, 2)
            mixed = signal("mixed", EC, 2)
            bank_g = [ps_scores[i][:, 0, :] for i in range(2)]
            bank_u = [ps_scores[i][:, 1, :] for i in range(2)]
            bank_s = [ps_pt[:, i, :] for i in range(2)]
            hid = wide

            with nc.Block() as block:
                @block.tensor
                def _(pe):
                    pe.sem_inc(mixed.sem, 2)

                    def router(g, par):
                        pe.wait_ge(xt_ready.sem, xt_ready.at(g, 1))
                        for u in range(GT):
                            last = pe.matmul(ps_pj[:, u * EXPERTS:(u + 1) * EXPERTS],
                                             q_t[par][:, u * P:(u + 1) * P], w_gate[:, :], start=True, stop=True)
                        last.then_inc(router_in_psum.sem, 1)

                    def transpose_gates(g):
                        pe.wait_ge(gates_ready.sem, gates_ready.at(g, 1))
                        for u in range(GT):
                            last = pe.transpose(ps_pj[:, u * P:(u + 1) * P], gates[:, u, :], ident[:, :])
                        last.then_inc(gates_in_psum.sem, 1)

                    def hidden(g, c, par):
                        s = c % 2
                        if c == 0:
                            pe.wait_ge(gates_t_ready.sem, gates_t_ready.at(g, 1))
                        pe.wait_ge(silu_done.sem, silu_done.at(g, c + 1))
                        pe.matmul(bank_g[s], w_1[:, 2 * c:2 * c + 2, :].rearrange("p e i -> p (e i)"),
                                  q_t[par][:, :], start=True, stop=True)
                        pe.wait_ge(times_up.sem, times_up.at(g, c + 1))
                        pe.matmul(bank_u[s], w_3[:, 2 * c:2 * c + 2, :].rearrange("p e i -> p (e i)"),
                                  q_t[par][:, :], start=True, stop=True)
                        pe.wait_ge(weighted.sem, weighted.at(g, c + 1))
                        pe.matmul(bank_s[s], pick_expert[:, c, :], gates_t[par][:, :], start=True, stop=True)\
                          .then_inc(hidden_in_psum.sem, 1)

                    def mix(g, c):
                        pe.wait_ge(weighted.sem, weighted.at(g, c + 3))
                        if c == 0:
                            pe.wait_ge(added.sem, added.at(g, 0))
                        for u in range(GT):
                            last = pe.matmul(ps_o[:, u * P:(u + 1) * P], hid[c % 2][:, u * P:(u + 1) * P],
                                             w_2[:, c, :], start=c == 0 and u == 0, stop=c == EC - 1,
                                             skip_group_check=True)
                        last.then_inc(mixed.sem, 1)

                    def body(g, par, ahead):
                        for c in range(EC):
                            hidden(g, c, par)
                            if c:
                                mix(g, c - 1)
                            if ahead and c == 2:
                                transpose_x(pe, g + 1)
                            if ahead and c == 4:
                                router(g + 1, 1 - par)
                            if ahead and c == 7:
                                transpose_gates(g + 1)
                        mix(g, EC - 1)

                    transpose_x(pe, 0)
                    router(0, 0)
                    transpose_gates(0)
                    run_groups(pe, body)

                @block.scalar
                def _(act):
                    act.preload_act_table_set(LN_EXP)
                    act.sem_inc(silu_done.sem, 2)

                    def exps(g):
                        act.wait_ge(logit_ready.sem, logit_ready.at(g, 1))
                        act.activation(small["b"][:, :, :], small["a"][:, :, :], ACT.Exp).then_inc(expo_ready.sem, 1)

                    def copy_gates(g, par):
                        act.wait_ge(gates_in_psum.sem, gates_in_psum.at(g, 1))
                        act.activation(gates_t[par][:, :], ps_pj[:, :], ACT.Copy).then_inc(gates_t_ready.sem, 1)

                    def silu(g, c):
                        act.wait_ge(hidden_in_psum.sem, hidden_in_psum.at(g, c + 1))
                        act.wait_ge(mixed.sem, mixed.at(g, c + 1))
                        act.activation(hid[c % 2][:, :], bank_g[c % 2], ACT.Silu).then_inc(silu_done.sem, 1)

                    def body(g, par, ahead):
                        for c in range(EC):
                            silu(g, c)
                            if ahead and c == 1:
                                root(act, g + 1)
                            if ahead and c == 3:
                                copy_x_transposed(act, g + 1, 1 - par, mixed, mixed.at(g, 2))
                            if ahead and c == 5:
                                exps(g + 1)
                            if ahead and c == 7:
                                copy_gates(g + 1, 1 - par)

                    root(act, 0)
                    copy_x_transposed(act, 0, 0, None, 0)
                    exps(0)
                    copy_gates(0, 0)
                    run_groups(act, body)

                @block.vector
                def _(dve):
                    dve.sem_inc(times_up.sem, 2)
                    dve.sem_inc(weighted.sem, 2)

                    def choose(g):
                        step = Steps(dve, chain, g)
                        lg, pick, eq = small["c"][:, :, :], small["d"][:, :, :], small["e"][:, :, :]
                        dve.wait_ge(router_in_psum.sem, router_in_psum.at(g, 1))
                        dve.tensor_copy(lg, ps_pj[:, 0:GT * EXPERTS].rearrange("p (u e) -> p u e", u=GT))\
                           .then_inc(router_copied.sem, 1)
                        dve.wait_ge(router_copied.sem, router_copied.at(g, 1))
                        dve.sem_inc(dve_turn.sem, 1)
                        for u in range(GT):
                            dve.max(top8[:, u, :], small["c"][:, u, :]).then_inc(top_ready.sem, 1)
                        dve.wait_ge(top_ready.sem, top_ready.at(g, GT))
                        dve.tensor_tensor(small["a"][:, :, :], lg, top8[:, :, 0:1].broadcast_to([P, GT, EXPERTS]),
                                          ALU.subtract).then_inc(logit_ready.sem, 1)
                        fourth = top8[:, :, TOPK - 1:TOPK].broadcast_to([P, GT, EXPERTS])
                        step(dve.tensor_tensor(pick, lg, fourth, ALU.is_gt))
                        step(dve.tensor_tensor(eq, lg, fourth, ALU.is_equal))
                        step(dve.tensor_reduce(tiny["a"][:, :], pick, AX, ALU.add))
                        src, at = "e", 1
                        for dst in ("f", "g", "f", "g"):
                            step(dve.tensor_copy(small[dst][:, :, 0:at], small[src][:, :, 0:at]))
                            step(dve.tensor_tensor(small[dst][:, :, at:], small[src][:, :, at:],
                                                   small[src][:, :, 0:EXPERTS - at], ALU.add))
                            src, at = dst, 2 * at
                        cnt = small[src][:, :, :]
                        step(dve.tensor_tensor(cnt, cnt, tiny["a"][:, :].unsqueeze(2).broadcast_to([P, GT, EXPERTS]),
                                               ALU.add))
                        step(dve.scalar_tensor_tensor(out=eq, in0=cnt, scalar=float(TOPK), in1=eq,
                                                      op0=ALU.is_le, op1=ALU.mult))
                        step(dve.tensor_tensor(pick, pick, eq, ALU.add))

                    def weigh(g):
                        step = Steps(dve, chain, g, CH - 2)
                        dve.wait_ge(expo_ready.sem, expo_ready.at(g, 1))
                        kept = small["h"][:, :, :]
                        dve.wait_ge(chain.sem, chain.at(g, CH - 2))
                        dve.tensor_tensor(kept, small["b"][:, :, :], small["d"][:, :, :], ALU.mult)\
                           .then_inc(picked.sem, 1)
                        dve.wait_ge(picked.sem, picked.at(g, 1))
                        step(dve.tensor_reduce(tiny["b"][:, :], kept, AX, ALU.add))
                        step(dve.reciprocal(tiny["b"][:, :], tiny["b"][:, :]))
                        dve.wait_ge(gates_in_psum.sem, gates_in_psum.at(g, 0))
                        dve.tensor_tensor(gates[:, :, 0:EXPERTS], kept,
                                          tiny["b"][:, :].unsqueeze(2).broadcast_to([P, GT, EXPERTS]), ALU.mult)\
                           .then_inc(gates_ready.sem, 1)

                    def combine(g, c):
                        h = hid[c % 2][:, :]
                        dve.wait_ge(silu_done.sem, silu_done.at(g, c + 3))
                        dve.tensor_tensor(h, h, bank_u[c % 2], ALU.mult).then_inc(times_up.sem, 1)
                        dve.wait_ge(times_up.sem, times_up.at(g, c + 3))
                        dve.tensor_tensor(h, h, bank_s[c % 2], ALU.mult).then_inc(weighted.sem, 1)

                    def body(g, par, ahead):
                        for c in range(EC):
                            combine(g, c)
                            if ahead and c == 0:
                                norm_stats(dve, g + 1)
                            if ahead and c == 1:
                                normalise(dve, g + 1)
                            if ahead and c == 4:
                                choose(g + 1)
                            if ahead and c == 5:
                                weigh(g + 1)
                        dve.wait_ge(mixed.sem, mixed.at(g, EC + 2))
                        flat = window_of(g)
                        dve.tensor_tensor(flat, ps_o[:, :], flat, ALU.add).then_inc(added.sem, 1)

                    norm_stats(dve, 0)
                    normalise(dve, 0)
                    choose(0)
                    weigh(0)
                    run_groups(dve, body)
            close_stage()

        def channel_mix():
            open_front(1)
            damped = signal("damped", 2)
            blended = signal("blended", 4)
            rk_in_psum = signal("rk_in_psum", 2)
            relu_done = signal("relu_done", 1)
            squared = signal("squared", 1)
            v_done = signal("v_done", 1)
            sig = signal("sig", 1)
            chain = signal("chain", 3)
            bank_r, bank_k, bank_v = ps_scores[0][:, 0, :], ps_scores[1][:, 0, :], ps_o[:, :]
            blend = {"r": wide[0], "k": wide[1]}
            k_act, expo, damp = wide[2], wide[3], {"r": wide[4], "k": wide[5]}

            with nc.Block() as block:
                @block.tensor
                def _(pe):
                    def body(g, par, ahead):
                        pe.wait_ge(blended.sem, blended.at(g, 4))
                        pe.wait_ge(relu_done.sem, relu_done.at(g, 0))
                        pe.matmul(bank_k, w_mix["k"][:, :], blend["k"][:, :], start=True, stop=True)\
                          .then_inc(rk_in_psum.sem, 1)
                        pe.wait_ge(sig.sem, sig.at(g, 0))
                        for u in range(GT):
                            last = pe.matmul(bank_r[:, u * P:(u + 1) * P], blend["r"][:, u * P:(u + 1) * P],
                                             w_mix["r"][:, :], start=True, stop=True)
                        last.then_inc(rk_in_psum.sem, 1)
                        if ahead:
                            transpose_x(pe, g + 1)
                        pe.wait_ge(squared.sem, squared.at(g, 1))
                        pe.wait_ge(chain.sem, chain.at(g, 0))
                        for u in range(GT):
                            last = pe.matmul(bank_v[:, u * P:(u + 1) * P], k_act[:, u * P:(u + 1) * P],
                                             w_mix["v"][:, :], start=True, stop=True)
                        last.then_inc(v_done.sem, 1)

                    transpose_x(pe, 0)
                    run_groups(pe, body)

                @block.scalar
                def _(act):
                    act.preload_act_table_set(LN_EXP)
                    def body(g, par, ahead):
                        if ahead:
                            root(act, g + 1)
                        act.wait_ge(rk_in_psum.sem, rk_in_psum.at(g, 1))
                        act.wait_ge(v_done.sem, v_done.at(g, 0))
                        act.activation(k_act[:, :], bank_k, ACT.Relu).then_inc(relu_done.sem, 1)
                        act.wait_ge(rk_in_psum.sem, rk_in_psum.at(g, 2))
                        act.wait_ge(added.sem, added.at(g, 0))
                        act.activation(expo[:, :], bank_r, ACT.Exp, scale=-1.0).then_inc(sig.sem, 1)
                        if ahead:
                            copy_x_transposed(act, g + 1, 1 - par, blended, blended.at(g, 4))

                    root(act, 0)
                    copy_x_transposed(act, 0, 0, None, 0)
                    run_groups(act, body)

                @block.gpsimd
                def _(pool):
                    def body(g, par, ahead):
                        pool.wait_ge(relu_done.sem, relu_done.at(g, 1))
                        pool.tensor_tensor(k_act[:, :], k_act[:, :], k_act[:, :], ALU.mult).then_inc(squared.sem, 1)

                    run_groups(pool, body)

                @block.vector
                def _(dve):
                    def blend_rows(g, par):
                        dve.wait_ge(xt_ready.sem, xt_ready.at(g, 1))
                        dve.wait_ge(rk_in_psum.sem, rk_in_psum.at(g, 0))
                        n = q_t[par][:, :].rearrange("p (b t) -> p b t", t=S)
                        for c in "kr":
                            dve.tensor_scalar(damp[c][:, :], q_t[par][:, :], one_less_mu[c][:, 0:1], None, ALU.mult)\
                               .then_inc(damped.sem, 1)
                        dve.wait_ge(damped.sem, damped.at(g, 2))
                        for c in "kr":
                            b_ = blend[c][:, :].rearrange("p (b t) -> p b t", t=S)
                            d_ = damp[c][:, :].rearrange("p (b t) -> p b t", t=S)
                            dve.scalar_tensor_tensor(out=b_[:, :, 1:S], in0=n[:, :, 1:S], scalar=mu[c][:, 0:1],
                                                     in1=d_[:, :, 0:S - 1], op0=ALU.mult, op1=ALU.add)\
                               .then_inc(blended.sem, 1)
                            dve.tensor_scalar(b_[:, :, 0], n[:, :, 0], mu[c][:, 0:1], None, ALU.mult)\
                               .then_inc(blended.sem, 1)

                    def body(g, par, ahead):
                        step = Steps(dve, chain, g)
                        if ahead:
                            norm_stats(dve, g + 1)
                            normalise(dve, g + 1)
                        dve.wait_ge(sig.sem, sig.at(g, 1))
                        step(dve.tensor_scalar(expo[:, :], expo[:, :], 1.0, None, ALU.add))
                        step(dve.reciprocal(expo[:, :], expo[:, :]))
                        if ahead:
                            blend_rows(g + 1, 1 - par)
                        dve.wait_ge(v_done.sem, v_done.at(g, 1))
                        step(dve.tensor_tensor(expo[:, :], expo[:, :], bank_v, ALU.mult))
                        flat = window_of(g)
                        dve.tensor_tensor(flat, expo[:, :], flat, ALU.add).then_inc(added.sem, 1)

                    for c in "rk":
                        dve.tensor_scalar(one_less_mu[c][:, :], mu[c][:, :], -1.0, 1.0, ALU.mult, ALU.add)\
                           .then_inc(mu_ready.sem, 1)
                    dve.wait_ge(mu_ready.sem, 2)
                    norm_stats(dve, 0)
                    normalise(dve, 0)
                    blend_rows(0, 0)
                    run_groups(dve, body)
            close_stage()

        shift_loaded = signal("shift_loaded")

        def move_shifted(sp, last=False):
            half = P // 2

            def load(g, par):
                rows = bass.ds(g * GT, GT)
                sp.dma_start(hi[par][:, :, 0:half], x[:, rows, 0:half]).then_inc(shift_loaded.sem, 16)
                for b in range(2):
                    sp.dma_start(hi[par][b * S + 1:(b + 1) * S, :, half:P],
                                 x[b * S:(b + 1) * S - 1, rows, half:P]).then_inc(shift_loaded.sem, 16)
                if last:
                    sp.dma_start(parked[par], out[:, rows, :]).then_inc(shift_loaded.sem, 16)

            def body(g, par, ahead):
                if ahead:
                    sp.wait_ge(xt_in_psum.sem, xt_in_psum.at(g, 1))
                    sp.sem_inc(sp_turn.sem, 1)
                    load(g + 1, 1 - par)
                if last:
                    sp.wait_ge(added.sem, added.at(g, added.per))
                    sp.sem_inc(sp_turn.sem, 1)
                    sp.dma_start(out[:, bass.ds(g * GT, GT), :], x[:, bass.ds(g * GT, GT), :])\
                      .then_inc(result_out.sem, 16)

            sp.wait_ge(first_rows.sem, 4)
            load(0, 0)
            run_groups(sp, body)
            if last:
                sp.wait_ge(result_out.sem, 16 * GROUPS)

        result_out = signal("result_out")
        first_rows = signal("first_rows")
        tables = signal("tables")

        def prepare_layers():
            with nc.Block() as block:
                @block.gpsimd
                def _(pool):
                    for i in range(2):
                        for b in range(2):
                            pool.memset(hi[i][b * S:b * S + 1, :, P // 2:P], 0.0).then_inc(first_rows.sem, 1)

                @block.vector
                def _(dve):
                    for i in range(2):
                        dve.memset(v_pair[i], 0.0).then_inc(tables.sem, 1)
                    dve.memset(k_pair, 0.0).then_inc(tables.sem, 1)
                    for l in range(DEPTH):
                        for a in range(2):
                            sc = rot_scale[:, l, a, :]
                            dve.tensor_tensor(rot[l][:, 2 * a, :], rot_base[:, 2 * a, :], sc, ALU.mult)\
                               .then_inc(tables.sem, 1)
                            for lo, hi_ in ((0, HALF), (HALF, 0)):
                                dve.tensor_tensor(rot[l][:, 2 * a + 1, lo:lo + HALF],
                                                  rot_base[:, 2 * a + 1, lo:lo + HALF],
                                                  sc[:, hi_:hi_ + HALF], ALU.mult).then_inc(tables.sem, 1)

        parked = [t[:, :].rearrange("p (u c) -> p u c", u=GT) for t in (k_t, x_norm_t)]

        def normalise_residual():
            in_out = signal("in_out")
            all_stats = signal("all_stats")
            all_chain = signal("all_chain")
            all_root = signal("all_root")
            centred = signal("centred")
            scaled = signal("scaled")
            bn_all = wide[0][:, 0:TILES * 6].rearrange("p (t s) -> p t s", s=6)
            mean_, gap_, dev_, log_, root_, work_ = (wide[1][:, i * TILES:(i + 1) * TILES] for i in range(6))
            front, back = slice(0, TILES * 5 // 8), slice(TILES * 5 // 8, TILES)

            with nc.Block() as block:
                @block.sync
                def _(sp):
                    sp.dma_start(out, x[:, :, :]).then_inc(in_out.sem, 16)
                    sp.wait_ge(in_out.sem, 16)

                @block.scalar
                def _(act):
                    act.preload_act_table_set(LN_EXP)
                    act.wait_ge(all_chain.sem, 7)
                    act.activation(log_, dev_, ACT.Ln).then_inc(all_root.sem, 1)
                    act.wait_ge(all_root.sem, 1)
                    act.activation(root_, log_, ACT.Exp, scale=-0.5).then_inc(all_root.sem, 1)

                @block.gpsimd
                def _(pool):
                    tiles = x[:, back, :]
                    shape = [P, back.stop - back.start, P]
                    pool.wait_ge(in_out.sem, 16)
                    pool.wait_ge(all_chain.sem, 4)
                    pool.tensor_tensor(tiles, tiles, mean_[:, back].unsqueeze(2).broadcast_to(shape), ALU.subtract)\
                        .then_inc(centred.sem, 1)
                    pool.wait_ge(centred.sem, 1)
                    pool.wait_ge(all_chain.sem, 11)
                    pool.tensor_tensor(tiles, tiles, root_[:, back].unsqueeze(2).broadcast_to(shape), ALU.mult)\
                        .then_inc(centred.sem, 1)

                @block.vector
                def _(dve):
                    with dve.Fori(0, GROUPS) as g:
                        for i in range(GT):
                            dve.bn_stats(bn_all[:, bass.ds(g * GT + i, 1), :].rearrange("p a s -> p (a s)"),
                                         x[:, bass.ds(g * GT + i, 1), :].rearrange("p a c -> p (a c)"))\
                               .then_inc(all_stats.sem, 1)
                    step = Steps(dve, all_chain, 0)
                    dve.wait_ge(all_stats.sem, TILES)
                    step(dve.tensor_tensor(mean_, bn_all[:, :, 1], bn_all[:, :, 4], ALU.add))
                    step(dve.tensor_tensor(gap_, bn_all[:, :, 1], bn_all[:, :, 4], ALU.subtract))
                    step(dve.tensor_tensor(dev_, bn_all[:, :, 2], bn_all[:, :, 5], ALU.add))
                    step(dve.tensor_scalar(mean_, mean_, 0.5, None, ALU.mult))
                    step(dve.tensor_tensor(gap_, gap_, gap_, ALU.mult))
                    step(dve.tensor_scalar(dev_, dev_, 1.0 / P, LN_EPS, ALU.mult, ALU.add))
                    step(dve.scalar_tensor_tensor(out=dev_, in0=gap_, scalar=0.25, in1=dev_, op0=ALU.mult,
                                                  op1=ALU.add))
                    tiles = x[:, front, :]
                    shape = [P, front.stop, P]
                    dve.wait_ge(in_out.sem, 16)
                    dve.tensor_tensor(tiles, tiles, mean_[:, front].unsqueeze(2).broadcast_to(shape), ALU.subtract)\
                       .then_inc(scaled.sem, 1)
                    dve.wait_ge(all_root.sem, 2)
                    step(dve.tensor_tensor(work_, root_, root_, ALU.mult))
                    step(dve.tensor_tensor(work_, work_, dev_, ALU.mult))
                    step(dve.tensor_scalar(work_, work_, -0.5, 1.5, ALU.mult, ALU.add))
                    step(dve.tensor_tensor(root_, root_, work_, ALU.mult))
                    dve.wait_ge(scaled.sem, 1)
                    dve.tensor_tensor(tiles, tiles, root_[:, front].unsqueeze(2).broadcast_to(shape), ALU.mult)\
                       .then_inc(scaled.sem, 1)
            close_stage()

        def local_attention(l):
            open_front(GT, norm=False)
            shift_loaded.opens(3 * 16)
            qk_in_psum = signal("qk_in_psum", 2 * GT)
            v_in_psum = signal("lv_in_psum", GT)
            squared = signal("l_squared", 2 * GT)
            norms = signal("norms", 3 * GT)
            l_root = signal("l_root", 2 * GT)
            l_newton = signal("l_newton", 4 * GT)
            products = signal("products", 6 * GT)
            rotated = signal("rotated", 2 * GT)
            unit = signal("unit", 2 * GT)
            qk_turned = signal("qk_turned", 2 * GT)
            q_copied = signal("q_copied", GT)
            k_copied = signal("k_copied", 2 * GT)
            v_copied = signal("v_copied", 2 * GT)
            scored = signal("scored", GT)
            max_ready = signal("max_ready", GT)
            shifted = signal("shifted", GT)
            exp_ready = signal("exp_ready", GT)
            sums_ready = signal("sums_ready", GT)
            rec_ready = signal("rec_ready", GT)
            turned = signal("turned", GT)
            pt_copied = signal("pt_ready", GT)
            summed = signal("summed", GT)
            o_ready = signal("o_ready", GT)
            ot_in_psum = signal("ot_in_psum", GT)
            ot_copied = signal("ot_ready", GT)
            y_ready = signal("y_ready", GT)

            bank_qk = [ps_scores[0][:, i, :] for i in range(2)]
            bank_v = ps_scores[1]
            bank_s, bank_t = ps_pt[:, 0, :], ps_pt[:, 1, :]
            sq = [wide[0], wide[1]]
            qt, kp = big["qt"], k_pair
            pl, pt, o_, ot = big["pl"], big["pt"], big["o"], big["ot"]
            nrm, nlog, nroot, nwork, nstep = (norm8[n] for n in "abcde")

            with nc.Block() as block:
                @block.sync
                def _(sp):
                    move_shifted(sp)

                @block.tensor
                def _(pe):
                    def transpose_window(g, par):
                        pe.wait_ge(shift_loaded.sem, shift_loaded.at(g, 48))
                        for u in range(GT):
                            last = pe.transpose(ps_pj[:, u * P:(u + 1) * P], hi[par][:, u, :], ident[:, :])
                        last.then_inc(xt_in_psum.sem, 1)

                    def project_qk(g, n, par):
                        h = q_t[(par + n // GT) % 2][:, n % GT * P:(n % GT + 1) * P]
                        if n % GT == 0:
                            pe.wait_ge(xt_ready.sem, xt_ready.at(g + n // GT, 1))
                        pe.wait_ge(products.sem, products.at(g, 6 * n))
                        for i in range(2):
                            pe.matmul(bank_qk[i], h, w_qkv[l][:, i * INNER:(i + 1) * INNER],
                                      start=True, stop=True).then_inc(qk_in_psum.sem, 1)

                    def project_v(g, n, par):
                        h = q_t[(par + n // GT) % 2][:, n % GT * P:(n % GT + 1) * P]
                        pe.wait_ge(v_copied.sem, v_copied.at(g, 2 * n))
                        for b in range(2):
                            for j in range(2):
                                last = pe.matmul(bank_v[j * S:(j + 1) * S, b, :], h[:, b * S:(b + 1) * S],
                                                 w_qkv[l][:, 2 * INNER:3 * INNER], start=True, stop=True)
                        last.then_inc(v_in_psum.sem, 1)

                    def turn_qk(g, n):
                        pe.wait_ge(unit.sem, unit.at(g, 2 * n + 1))
                        for r in range(LPAIRS):
                            last = pe.transpose(ps_pj[:, r * P:(r + 1) * P], part[n % 2][0][0][:, r * P:(r + 1) * P],
                                                ident[:, :])
                        last.then_inc(qk_turned.sem, 1)
                        pe.wait_ge(unit.sem, unit.at(g, 2 * n + 2))
                        for r in range(LPAIRS):
                            last = pe.transpose(bank_s[:, r * P:(r + 1) * P], part[n % 2][1][0][:, r * P:(r + 1) * P],
                                                ident[:, :])
                        last.then_inc(qk_turned.sem, 1)

                    def scores(g, n):
                        pe.wait_ge(q_copied.sem, q_copied.at(g, n + 1))
                        pe.wait_ge(k_copied.sem, k_copied.at(g, 2 * n + 2))
                        pe.matmul(bank_s.rearrange("p (h k) -> p h k", k=S), ident_16[:, :],
                                  masks["causal"][:, :].unsqueeze(1).broadcast_to([P, LHEADS, S]),
                                  start=True, stop=False, skip_group_check=True)
                        for r in range(LPAIRS):
                            for b in range(2):
                                last = pe.matmul(bank_s[b * S:(b + 1) * S, r * P:(r + 1) * P],
                                                 qt[:, r * P + b * S:r * P + (b + 1) * S],
                                                 kp[:, r, b, :, :].rearrange("p j k -> p (j k)"),
                                                 start=False, stop=True, skip_group_check=True)
                        last.then_inc(scored.sem, 1)

                    def turn_probs(g, u):
                        pe.wait_ge(exp_ready.sem, exp_ready.at(g, u + 1))
                        pe.wait_ge(ot_copied.sem, ot_copied.at(g, u))
                        for r in range(LPAIRS):
                            last = pe.transpose(bank_t[:, r * P:(r + 1) * P], pl[:, r * P:(r + 1) * P], ident[:, :])
                        last.then_inc(turned.sem, 1)

                    def weigh_values(g, u):
                        pe.wait_ge(pt_copied.sem, pt_copied.at(g, u + 1))
                        pe.wait_ge(v_copied.sem, v_copied.at(g, 2 * u + 2))
                        pe.wait_ge(o_ready.sem, o_ready.at(g, u))
                        for r in range(LPAIRS):
                            for b in range(2):
                                last = pe.matmul(ps_o[b * S:(b + 1) * S, r * P:(r + 1) * P],
                                                 pt[:, r * P + b * S:r * P + (b + 1) * S],
                                                 v_pair[u % 2][:, b, r, :, :].rearrange("p j d -> p (j d)"),
                                                 start=True, stop=True)
                        last.then_inc(summed.sem, 1)

                    def turn_o(g, u):
                        pe.wait_ge(o_ready.sem, o_ready.at(g, u + 1))
                        for r in range(LPAIRS):
                            last = pe.transpose(bank_t[:, r * P:(r + 1) * P], o_[:, r * P:(r + 1) * P], ident[:, :])
                        last.then_inc(ot_in_psum.sem, 1)

                    def project_o(g, u):
                        pe.wait_ge(ot_copied.sem, ot_copied.at(g, u + 1))
                        pe.wait_ge(added.sem, added.at(g, u))
                        for r in range(LPAIRS):
                            last = pe.matmul(ps_pj[:, 0:P], ot[:, r * P:(r + 1) * P], w_lo[l][:, r, :],
                                             start=r == 0, stop=r == LPAIRS - 1)
                        last.then_inc(y_ready.sem, 1)

                    def body(g, par, ahead):
                        for u in range(GT):
                            if ahead or u + 2 < GT:
                                project_qk(g, u + 2, par)
                            pe.wait_ge(added.sem, added.at(g, u))
                            if ahead and u == 1:
                                transpose_window(g + 1, 1 - par)
                            turn_probs(g, u)
                            if ahead and u == 1:
                                pe.wait_ge(xt_ready.sem, xt_ready.at(g + 1, 1))
                            if ahead or u + 1 < GT:
                                turn_qk(g, u + 1)
                            weigh_values(g, u)
                            if ahead or u + 2 < GT:
                                project_v(g, u + 2, par)
                            turn_o(g, u)
                            if ahead or u + 1 < GT:
                                scores(g, u + 1)
                            project_o(g, u)

                    pe.wait_ge(tables.sem, 3 + 6 * DEPTH)
                    transpose_window(0, 0)
                    for n in range(2):
                        project_qk(0, n, 0)
                        project_v(0, n, 0)
                    turn_qk(0, 0)
                    scores(0, 0)
                    run_groups(pe, body)

                @block.scalar
                def _(act):
                    act.preload_act_table_set(LN_EXP)

                    def copy_window(g, par, first):
                        act.wait_ge(xt_in_psum.sem, xt_in_psum.at(g, 1))
                        if not first:
                            act.wait_ge(v_in_psum.sem, v_in_psum.at(g - 1, 0))
                        act.activation(q_t[par][:, :], ps_pj[:, :], ACT.Copy).then_inc(xt_ready.sem, 1)

                    def squares(g, n, i):
                        act.wait_ge(qk_in_psum.sem, qk_in_psum.at(g, 2 * n + i + 1))
                        act.wait_ge(norms.sem, norms.at(g, 3 * n))
                        act.activation(sq[i][:, :], bank_qk[i], ACT.Square).then_inc(squared.sem, 1)

                    def roots(g, n):
                        act.wait_ge(norms.sem, norms.at(g, 3 * n + 3))
                        act.activation(nlog, nrm, ACT.Ln).then_inc(l_root.sem, 1)
                        act.wait_ge(l_root.sem, l_root.at(g, 2 * n + 1))
                        act.wait_ge(unit.sem, unit.at(g, 2 * n))
                        act.activation(nroot, nlog, ACT.Exp, scale=-0.5).then_inc(l_root.sem, 1)

                    def copy_v(g, n, first):
                        act.wait_ge(v_in_psum.sem, v_in_psum.at(g, n + 1))
                        if not first:
                            act.wait_ge(summed.sem, summed.at(g, n - 1))
                        for j in range(2):
                            rows = slice(j * S, (j + 1) * S)
                            src = bank_v[rows, :, :].rearrange("p b (r j d) -> p b r j d", r=LPAIRS, j=2)
                            act.activation(v_pair[n % 2][rows, :, :, j, :], src[:, :, :, j, :], ACT.Copy)\
                               .then_inc(v_copied.sem, 1)

                    def copy_qk(g, n):
                        act.wait_ge(qk_turned.sem, qk_turned.at(g, 2 * n + 1))
                        act.wait_ge(scored.sem, scored.at(g, n))
                        act.activation(qt[:, :], ps_pj[:, :], ACT.Copy).then_inc(q_copied.sem, 1)
                        act.wait_ge(qk_turned.sem, qk_turned.at(g, 2 * n + 2))
                        for j in range(2):
                            rows = slice(j * S, (j + 1) * S)
                            act.activation(kp[rows, :, :, j, :],
                                           bank_s[rows, :].rearrange("p (r b k) -> p r b k", r=LPAIRS, b=2),
                                           ACT.Copy).then_inc(k_copied.sem, 1)

                    def exponentials(g, u):
                        act.wait_ge(shifted.sem, shifted.at(g, u + 1))
                        act.activation(pl[:, :], pl[:, :], ACT.Exp, scale=8.0).then_inc(exp_ready.sem, 1)

                    def copy_pt(g, u):
                        act.wait_ge(turned.sem, turned.at(g, u + 1))
                        act.wait_ge(summed.sem, summed.at(g, u))
                        act.activation(pt[:, :], bank_t[:, :], ACT.Copy).then_inc(pt_copied.sem, 1)

                    def copy_ot(g, u):
                        act.wait_ge(ot_in_psum.sem, ot_in_psum.at(g, u + 1))
                        act.wait_ge(y_ready.sem, y_ready.at(g, u))
                        act.activation(ot[:, :], bank_t[:, :], ACT.Copy).then_inc(ot_copied.sem, 1)

                    def body(g, par, ahead):
                        for u in range(GT):
                            two = ahead or u + 2 < GT
                            if two:
                                squares(g, u + 2, 0)
                            exponentials(g, u)
                            if two:
                                squares(g, u + 2, 1)
                            if ahead and u == 1:
                                copy_window(g + 1, 1 - par, False)
                            copy_pt(g, u)
                            if ahead or u + 1 < GT:
                                copy_qk(g, u + 1)
                            if two:
                                roots(g, u + 2)
                            copy_ot(g, u)
                            if two:
                                copy_v(g, u + 2, False)

                    copy_window(0, 0, True)
                    for n in range(2):
                        for i in range(2):
                            squares(0, n, i)
                        copy_v(0, n, True)
                        roots(0, n)
                    copy_qk(0, 0)
                    run_groups(act, body)

                @block.gpsimd
                def _(pool):
                    def unite(g, n):
                        for i in range(2):
                            a, b_ = part[n % 2][i][0][:, :], part[n % 2][i][1][:, :]
                            pool.wait_ge(products.sem, products.at(g, 6 * n + 3 * i + 3))
                            pool.tensor_tensor(a, a, b_, ALU.add).then_inc(rotated.sem, 1)
                        step = Steps(pool, l_newton, g, 4 * n)
                        pool.wait_ge(l_root.sem, l_root.at(g, 2 * n + 2))
                        step(pool.tensor_tensor(nstep, nroot, nroot, ALU.mult))
                        step(pool.tensor_tensor(nstep, nstep, nrm, ALU.mult))
                        pool.sem_inc(pool_turn.sem, 1)
                        step(pool.tensor_scalar(nstep, nstep, -0.5, 1.5, ALU.mult, ALU.add))
                        step(pool.tensor_tensor(nroot, nroot, nstep, ALU.mult))
                        for i in range(2):
                            pool.wait_ge(rotated.sem, rotated.at(g, 2 * n + i + 1))
                            a = part[n % 2][i][0][:, :].rearrange("p (h d) -> p h d", d=LD)
                            pool.tensor_tensor(a, a, nroot[:, i, :].unsqueeze(2).broadcast_to([P, LHEADS, LD]),
                                               ALU.mult).then_inc(unit.sem, 1)

                    def body(g, par, ahead):
                        for u in range(GT):
                            if ahead or u + 2 < GT:
                                unite(g, u + 2)

                    unite(0, 0)
                    unite(0, 1)
                    run_groups(pool, body)

                @block.vector
                def _(dve):
                    def rotate(g, n, i, first):
                        src = bank_qk[i].rearrange("p (h d) -> p h d", d=LD)
                        a, b_ = (part[n % 2][i][m][:, :].rearrange("p (h d) -> p h d", d=LD) for m in range(2))

                        def table(m, lo, width):
                            return rot[l][:, m, lo:lo + width].unsqueeze(1).broadcast_to([P, LHEADS, width])

                        dve.wait_ge(squared.sem, squared.at(g, 2 * n + i + 1))
                        if not first:
                            dve.wait_ge(qk_turned.sem, qk_turned.at(g, 2 * n - 2))
                        dve.tensor_tensor(a, src, table(2 * i, 0, LD), ALU.mult).then_inc(products.sem, 1)
                        dve.tensor_tensor(b_[:, :, 0:HALF], src[:, :, HALF:LD], table(2 * i + 1, 0, HALF),
                                          ALU.mult).then_inc(products.sem, 1)
                        dve.tensor_tensor(b_[:, :, HALF:LD], src[:, :, 0:HALF], table(2 * i + 1, HALF, HALF),
                                          ALU.mult).then_inc(products.sem, 1)

                    def sum_squares(g, n, i):
                        dve.wait_ge(squared.sem, squared.at(g, 2 * n + i + 1))
                        dve.tensor_reduce(nwork[:, i, :], sq[i][:, :].rearrange("p (h d) -> p h d", d=LD),
                                          AX, ALU.add).then_inc(norms.sem, 1)

                    def clip(g, n):
                        dve.wait_ge(norms.sem, norms.at(g, 3 * n + 2))
                        dve.wait_ge(l_newton.sem, l_newton.at(g, 4 * n))
                        dve.tensor_scalar(nrm, nwork, 1e-24, float(2 ** LOG_SCALE), ALU.max, ALU.mult)\
                           .then_inc(norms.sem, 1)

                    def softmax(g, u):
                        p3 = pl[:, :].rearrange("p (h k) -> p h k", k=S)
                        s3 = bank_s.rearrange("p (h k) -> p h k", k=S)
                        dve.wait_ge(scored.sem, scored.at(g, u + 1))
                        dve.tensor_reduce(row_max[0][:, 0:LHEADS], s3, AX, ALU.max).then_inc(max_ready.sem, 1)
                        dve.wait_ge(max_ready.sem, max_ready.at(g, u + 1))
                        dve.wait_ge(turned.sem, turned.at(g, u))
                        dve.tensor_tensor(p3, s3, row_max[0][:, 0:LHEADS].unsqueeze(2).broadcast_to([P, LHEADS, S]),
                                          ALU.subtract).then_inc(shifted.sem, 1)

                    def sums(g, u):
                        dve.wait_ge(exp_ready.sem, exp_ready.at(g, u + 1))
                        dve.tensor_reduce(row_max[1][:, 0:LHEADS], pl[:, :].rearrange("p (h k) -> p h k", k=S),
                                          AX, ALU.add).then_inc(sums_ready.sem, 1)
                        dve.wait_ge(sums_ready.sem, sums_ready.at(g, u + 1))
                        dve.reciprocal(row_max[1][:, 0:LHEADS], row_max[1][:, 0:LHEADS]).then_inc(rec_ready.sem, 1)

                    def divide(g, u):
                        dve.wait_ge(summed.sem, summed.at(g, u + 1))
                        dve.wait_ge(rec_ready.sem, rec_ready.at(g, u + 1))
                        dve.wait_ge(ot_in_psum.sem, ot_in_psum.at(g, u))
                        dve.tensor_tensor(o_[:, :].rearrange("p (h d) -> p h d", d=LD),
                                          ps_o[:, :].rearrange("p (h d) -> p h d", d=LD),
                                          row_max[1][:, 0:LHEADS].unsqueeze(2).broadcast_to([P, LHEADS, LD]),
                                          ALU.mult).then_inc(o_ready.sem, 1)

                    def residual(g, u):
                        dve.wait_ge(y_ready.sem, y_ready.at(g, u + 1))
                        dve.tensor_tensor(tile_of(g, u), tile_of(g, u), ps_pj[:, 0:P], ALU.add)\
                           .then_inc(added.sem, 1)

                    def body(g, par, ahead):
                        for u in range(GT):
                            two = ahead or u + 2 < GT
                            softmax(g, u)
                            if u:
                                residual(g, u - 1)
                            if two:
                                rotate(g, u + 2, 0, False)
                            sums(g, u)
                            if two:
                                sum_squares(g, u + 2, 0)
                                sum_squares(g, u + 2, 1)
                                clip(g, u + 2)
                            divide(g, u)
                            if two:
                                rotate(g, u + 2, 1, False)
                        residual(g, GT - 1)

                    for n in range(2):
                        for i in range(2):
                            rotate(0, n, i, True)
                            sum_squares(0, n, i)
                        clip(0, n)
                    run_groups(dve, body)
            close_stage()

        def gated_mlp(l):
            NC = len(HC)
            open_front(1)
            last = l == DEPTH - 1
            shift_loaded.opens(4 * 16 if last else 3 * 16)
            g_in_psum = signal("g_in_psum", NC)
            a_in_psum = signal("a_in_psum", NC)
            gelu_done = signal("gelu_done", NC)
            gated = signal("gated", NC)
            y_done = signal("y_done", 1)
            unparked = signal("unparked", 1 if last else 0)
            bank_g = [ps_scores[i][:, 0, :] for i in range(2)]
            bank_a = [ps_scores[i][:, 1, :] for i in range(2)]

            with nc.Block() as block:
                @block.sync
                def _(sp):
                    move_shifted(sp, last)

                @block.tensor
                def _(pe):
                    def body(g, par, ahead):
                        pe.wait_ge(xt_ready.sem, xt_ready.at(g, 1))
                        for c, (at, m) in enumerate(HC):
                            pe.wait_ge(gated.sem, gated.at(g, max(c - 1, 0)))
                            pe.matmul(bank_g[c % 2][0:m, :], w_up1[l][:, HID + at:HID + at + m], q_t[par][:, :],
                                      start=True, stop=True).then_inc(g_in_psum.sem, 1)
                            pe.matmul(bank_a[c % 2][0:m, :], w_up1[l][:, at:at + m], q_t[par][:, :],
                                      start=True, stop=True).then_inc(a_in_psum.sem, 1)
                        if ahead:
                            transpose_x(pe, g + 1)
                        pe.wait_ge(added.sem, added.at(g, 0))
                        for c, (at, m) in enumerate(HC):
                            pe.wait_ge(gated.sem, gated.at(g, c + 1))
                            for u in range(GT):
                                pe.matmul(ps_o[:, u * P:(u + 1) * P], wide[c][0:m, u * P:(u + 1) * P],
                                          w_dn[l][0:m, c, :], start=c == 0 and u == 0, stop=False,
                                          skip_group_check=True)
                        for u in range(GT):
                            last = pe.matmul(ps_o[:, u * P:(u + 1) * P], ones[:, :], b_dn[l][:, :], start=False,
                                             stop=True, skip_group_check=True)
                        last.then_inc(y_done.sem, 1)

                    transpose_x(pe, 0)
                    run_groups(pe, body)

                @block.scalar
                def _(act):
                    act.preload_act_table_set(LN_EXP)
                    def copy_normed(g, par, wait_use):
                        act.wait_ge(xt_in_psum.sem, xt_in_psum.at(g, 1))
                        if wait_use:
                            act.wait_ge(a_in_psum.sem, a_in_psum.at(g - 1, 0))
                        act.activation(q_t[par][:, :], ps_pj[:, :], ACT.Identity, scale=ln_gb[l][:, 0:1],
                                       bias=ln_gb[l][:, 1:2]).then_inc(xt_ready.sem, 1)

                    def body(g, par, ahead):
                        if ahead:
                            root(act, g + 1)
                        for c, (at, m) in enumerate(HC):
                            act.wait_ge(g_in_psum.sem, g_in_psum.at(g, c + 1))
                            act.wait_ge(y_done.sem, y_done.at(g, 0))
                            act.activation(wide[3 + c][0:m, :], bank_g[c % 2][0:m, :], ACT.Gelu,
                                           bias=b_up1[l][0:m, NC + c:NC + c + 1]).then_inc(gelu_done.sem, 1)
                        if ahead:
                            copy_normed(g + 1, 1 - par, True)

                    root(act, 0)
                    copy_normed(0, 0, False)
                    run_groups(act, body)

                @block.vector
                def _(dve):
                    def body(g, par, ahead):
                        if ahead:
                            dve.wait_ge(shift_loaded.sem, shift_loaded.at(g + 1, shift_loaded.per))
                            norm_stats(dve, g + 1, hi[1 - par])
                        flat = window_of(g)
                        if last:
                            dve.tensor_tensor(flat, flat, parked[par].rearrange("p u c -> p (u c)"), ALU.add)\
                               .then_inc(unparked.sem, 1)
                        for c, (at, m) in enumerate(HC):
                            dve.wait_ge(a_in_psum.sem, a_in_psum.at(g, c + 1))
                            dve.wait_ge(gelu_done.sem, gelu_done.at(g, c + 1))
                            dve.wait_ge(y_done.sem, y_done.at(g, 0))
                            dve.scalar_tensor_tensor(out=wide[c][0:m, :], in0=bank_a[c % 2][0:m, :],
                                                     scalar=b_up1[l][0:m, c:c + 1], in1=wide[3 + c][0:m, :],
                                                     op0=ALU.add, op1=ALU.mult).then_inc(gated.sem, 1)
                            if ahead and c == 0:
                                normalise(dve, g + 1, hi[1 - par])
                        dve.wait_ge(y_done.sem, y_done.at(g, 1))
                        if last:
                            dve.wait_ge(unparked.sem, unparked.at(g, 1))
                        dve.tensor_tensor(flat, ps_o[:, :], flat, ALU.add).then_inc(added.sem, 1)

                    dve.wait_ge(shift_loaded.sem, shift_loaded.at(0, shift_loaded.per))
                    norm_stats(dve, 0, hi[0])
                    normalise(dve, 0, hi[0])
                    run_groups(dve, body)
            close_stage()

        flat_big = kblk[0][:, :, :].rearrange("p h t -> p (h t)")
        big = {n: flat_big[:, i * 512:(i + 1) * 512] for i, n in enumerate(("qt", "pl", "pt", "o", "ot"))}
        k_pair = flat_big[:, 2560:2560 + 1024].rearrange("p (r b j k) -> p r b j k", r=LPAIRS, b=2, j=2)
        v_pair = [flat_big[:, 3584 + i * 1024:3584 + (i + 1) * 1024]
                  .rearrange("p (b r j d) -> p b r j d", r=LPAIRS, b=2, j=2) for i in range(2)]
        flat_parts = kblk[1][:, :, :].rearrange("p h t -> p (h t)")
        part = [[[flat_parts[:, k * 512:(k + 1) * 512] for k in (4 * m + 2 * i, 4 * m + 2 * i + 1)]
                 for i in range(2)] for m in range(2)]
        norm8 = {n: small[n][:, 0, :].rearrange("p (i h) -> p i h", i=2) for n in "abcde"}

        mu_ready = signal("mu_ready")

        def layers():
            prepare_layers()
            normalise_residual()
            for l in range(DEPTH):
                local_attention(l)
                gated_mlp(l)

        steps = {
            "F3": layers,
            "F0": lambda: (prepare_low_rank(), low_rank_experts()),
            "F1": mixture,
            "F2": channel_mix,
            "L0": lambda: cross_attention("L0", 1.0 / np.sqrt(HD)),
            "L1": lambda: cross_attention("L1", 1.0 / np.sqrt(HD), mask=masks["L1"]),
            "L2": lambda: cross_attention("L2", 1.0, mask_per_seq=mask_l2, project=False, relu=True),
            "L3": lambda: cross_attention("L3", 1.0 / np.sqrt(HD), mask=masks["L3"]),
        }
        for n in STEPS:
            steps[n]()

        with nc.Block() as block:
            @block.sync
            def _(sp):
                written = signal("written")
                if "F3" not in STEPS:
                    sp.dma_start(out, x[:, :, :]).then_inc(written.sem, 16)
                    sp.wait_ge(written.sem, 16)


STEPS = ["L0","F0","L1","F1","L2","F2","L3","F3"]


def rotary_tables():
    half = np.arange(0, LD, 2, dtype=np.float32)
    t = np.arange(S, dtype=np.float32)
    freqs = t[:, None] * (np.float32(1) / np.float32(10000) ** (half / np.float32(LD)))[None, :]
    freqs = np.concatenate([freqs, freqs], axis=1)
    base = (half + np.float32(0.4 * LD)) / np.float32(1.4 * LD)
    scale = base[None, :] ** ((t - S // 2) / np.float32(S // 2))[:, None]
    scale = np.concatenate([scale, scale], axis=1)
    sign = np.where(np.arange(LD) < HALF, -1.0, 1.0).astype(np.float32)
    cos, sin, up = np.cos(freqs), np.sin(freqs) * sign, np.float32(2 ** (LOG_SCALE // 2))
    t4 = np.stack([cos * scale * up, sin * scale * up, cos / scale * up, sin / scale * up], axis=1)
    return np.concatenate([t4, t4]).astype(np.float32)


def columns(b):
    out = np.zeros((DEPTH, P, 2 * len(HC)), b.dtype)
    for i in range(2):
        for c, (at, m) in enumerate(HC):
            out[:, :m, i * len(HC) + c] = b[:, i, at:at + m]
    return out


def chunks(w2):
    out = np.zeros((DEPTH, P, len(HC), P), w2.dtype)
    for c, (at, m) in enumerate(HC):
        out[:, :m, c, :] = w2[:, at:at + m, :]
    return out


def kernel(**inputs):
    import concourse.bacc as bacc
    from concourse.bass_utils import run_bass_kernel_spmd

    a = {k: np.asarray(v) for k, v in inputs.items()}

    def row(v):
        return v.reshape(1, -1)

    arrays = {
        "x_in": a["x"].reshape(TILES, P, P).transpose(1, 0, 2),
        "ctx_t": a["ctx_1024"].reshape(TILES * P, P).T,
        "mask_l2": a["mask_Bx1xSxS2_ff0"].reshape(TILES, P, S).transpose(1, 0, 2),
        "mask_l3": a["mask_SxS2_bk1"],
        "L0_q": a["L0_xattn_w_q"].T, "L0_k": a["L0_xattn_w_k"].T,
        "L0_v": a["L0_xattn_w_v"].T, "L0_o": a["L0_xattn_w_o"].T,
        "L1_q": a["L1_xattn_Wq"].T, "L1_k": a["L1_xattn_Wk"].T,
        "L1_v": a["L1_xattn_Wv"].T, "L1_o": a["L1_xattn_Wo"].T,
        "L2_o": a["L2_xattn_wo_w"].T,
        "L3_q": a["L3_xattn_Wq"], "L3_k": a["L3_xattn_Wk"],
        "L3_v": a["L3_xattn_Wv"], "L3_o": a["L3_xattn_Wo"],
        "bL1_v": row(a["L1_xattn_bv"]), "bL1_o": row(a["L1_xattn_bo"]), "bL2_o": row(a["L2_xattn_wo_b"]),
        "bL3_v": row(a["L3_xattn_bv"]), "bL3_o": row(a["L3_xattn_bo"]),
        "low_W": a["L0_ffn_W"].T, "low_Wp": a["L0_ffn_Wp"], "low_WpT": a["L0_ffn_Wp"].T,
        "low_sim": a["L0_ffn_sim"], "low_bp": a["L0_ffn_bp"].reshape(-1, 1),
        "low_temp": np.broadcast_to(a["L0_ffn_temp"].reshape(1, 1), (P, 1)),
        "low_Wd": np.concatenate([a[f"L0_ffn_Wd{i}"] for i in range(NLR)]).T,
        "low_Wu": np.concatenate([a[f"L0_ffn_Wu{i}"] for i in range(NLR)], axis=1).T,
        "moe_gate": a["L1_ffn_gate_w"].T,
        "moe_1": a["L1_ffn_w1"].transpose(1, 0, 2), "moe_3": a["L1_ffn_w3"].transpose(1, 0, 2),
        "moe_2": a["L1_ffn_w2"].reshape(EC, P, P).transpose(1, 0, 2),
        "mix_r": a["L2_ffn_W_r"].T, "mix_k": a["L2_ffn_W_k"].T, "mix_v": a["L2_ffn_W_v"].T,
        "mu_r": a["L2_ffn_mu_r"].reshape(P, 1), "mu_k": a["L2_ffn_mu_k"].reshape(P, 1),
        "rot": rotary_tables(), "rot_scale": np.broadcast_to(
            np.stack([a["L3_ffn_q_scale"], a["L3_ffn_k_scale"]], axis=1), (P, DEPTH, 2, LD)),
        "wqkv": a["L3_ffn_wqkv"], "lo": a["L3_ffn_wo"].reshape(DEPTH, LPAIRS, P, P).transpose(0, 2, 1, 3),
        "up1": a["L3_ffn_w1"], "b_up1": columns(a["L3_ffn_b1"].reshape(DEPTH, 2, HID)),
        "dn": chunks(a["L3_ffn_w2"]), "b_dn": a["L3_ffn_b2"].reshape(DEPTH, 1, P),
        "ln": np.stack([a["L3_ffn_ln_g"], a["L3_ffn_ln_b"]], axis=2),
        "bL3_q": a["L3_xattn_bq"].reshape(P, 1), "bL3_k": a["L3_xattn_bk"].reshape(P, 1),
    }
    nc = bacc.Bacc("TRN2", target_bir_lowering=False, num_devices=1)
    feed, args = {}, {}
    for name, v in arrays.items():
        v = np.ascontiguousarray(v)
        feed["in_" + name] = v
        args[name] = nc.dram_tensor("in_" + name, v.shape, mybir.dt.from_np(v.dtype), kind="ExternalInput").ap()
    out = nc.dram_tensor("out", (P, TILES, P), F32, kind="ExternalOutput").ap()
    main = {n: args.pop(n) for n in ("x_in", "ctx_t", "mask_l2", "mask_l3")}
    build_program(nc, args, main["x_in"], main["ctx_t"], main["mask_l2"], main["mask_l3"], out)
    r = run_bass_kernel_spmd(nc, [feed], core_ids=[0])
    return r.results[0]["out"].transpose(1, 0, 2).reshape(NSEQ, S, P)
```

```python
from contextlib import ExitStack

import numpy as np
import concourse.bass as bass
from concourse import mybir

F32 = mybir.dt.float32
ACT = mybir.ActivationFunctionType
ALU = mybir.AluOpType
AX = mybir.AxisListType.X

P = 128
S = 64
NSEQ = 128
TILES = NSEQ * S // P
GT = 4
GROUPS = TILES // GT
GTOK = GT * P
GSEQ = GTOK // S
HEADS = 16
HD = P // HEADS
PAIRS = HEADS // 2
VC = HD + 1
LN_EPS = 1e-5
LN_EXP = "natural_log_exp_and_others"
PROJ, RANKS = 32, (1, 2, 4, 8)
NLR, RSUM = len(RANKS), sum(RANKS)
ROUTE = PROJ + NLR + RSUM
LOG_SCALE = 20
EXPERTS, INTER, TOPK = 16, 64, 4
EC = EXPERTS * INTER // P
LHEADS, LD, LPAIRS = 8, 64, 4
INNER = LHEADS * LD
HALF = LD // 2
DEPTH = 2
HID = 341
HC = [(c * P, min(P, HID - c * P)) for c in range((HID + P - 1) // P)]
GROUP_SIGNALS = """
gated_v bias_added a_in_psum added blended bn_done c_loaded chain damped exp_ready expo_ready g_in_psum gated
gates_in_psum gates_ready gates_t_ready gelu_done hidden_in_psum k_copied k_in_psum k_placed
kt_ready l_newton l_root l_squared ln_ready logit_ready lv_in_psum m_loaded mask_added max_ready
mixed newton norm_ready norms o_ready ot_in_psum ot_ready last_y picked products pt_ready pt_low q_copied
q_in_psum qk_in_psum qk_turned qt_ready r0_ready rec_ready relu_done rk_in_psum root_steps rotated
route_in_psum router_copied scored shift_loaded shifted sig silu_done squared summed
sums_ready times_up top_ready turned unit unparked v_copied v_done v_even v_in_psum v_odd var_ready
weighted x_norm_ready xt_in_psum xt_ready y_done y_ready""".split()
NEG = -(2.0 ** 100)


class Signal:

    def __init__(self, sem):
        self.sem, self.base, self.per, self.ahead = sem, 0, 0, 0

    def opens(self, per, ahead=0):
        self.per, self.ahead = per, ahead

    def closes(self, groups):
        self.base += self.per * groups + self.ahead
        self.per = self.ahead = 0

    def at(self, g, k):
        return g * self.per + (self.base + k)


def build_program(nc, w, x_in, ctx_t, mask_l2, mask_l3, out):
    with ExitStack() as ctx:
        def sb(name, shape, dt=F32):
            return ctx.enter_context(nc.sbuf_tensor(name, shape, dt))

        signals = {}

        def signal(name, per=0, ahead=0):
            if name not in signals:
                assert per == 0 or name in GROUP_SIGNALS, name
                signals[name] = Signal(ctx.enter_context(nc.semaphore(name)))
            signals[name].opens(per, ahead)
            return signals[name]

        def close_stage(groups=GROUPS):
            for s in signals.values():
                s.closes(groups)

        for n in GROUP_SIGNALS:
            signal(n).base = 1

        x = sb("x", [P, TILES, P])
        ident = sb("ident", [P, P])
        ones = sb("ones", [P, P])
        minus_half = sb("minus_half", [P, TILES])
        attn_w = {n: sb("w_" + n, [P, P]) for n in (
            "L0_q", "L0_k", "L0_v", "L0_o", "L1_q", "L1_k", "L1_v", "L1_o", "L2_o",
            "L3_q", "L3_k", "L3_v", "L3_o")}
        row_bias = {n: sb("b_" + n, [P, P]) for n in ("L1_o", "L2_o", "L3_o")}
        col_bias = {n: sb("b_" + n, [P, 1]) for n in ("L1_v", "L3_v", "L3_q", "L3_k")}
        out_bias = {n: sb("out_bias_" + n, [P, P]) for n in ("L1", "L3")}
        mask_l1_sb = sb("mask_l1_sb", [P, S])
        causal = sb("causal", [P, S])
        mask_l3_in = sb("mask_l3_in", [P, S], mybir.dt.uint8)

        ci = [sb(f"ci{i}", [P, GSEQ, 2, S]) for i in range(2)]
        kblk = [sb(f"kblk{i}", [P, HEADS, GTOK]) for i in range(2)]
        q_t = [sb(f"q_t{i}", [P, GTOK]) for i in range(2)]
        k_t = sb("k_t", [P, GTOK])
        v2 = [sb(f"v2{i}", [P, GSEQ, PAIRS, 2, VC]) for i in range(2)]
        x_norm = sb("x_norm", [P, GT, P])
        x_norm_t = sb("x_norm_t", [P, GTOK])
        bn = sb("bn", [P, GT, 6])
        mean = sb("mean", [P, GT])
        mean_gap = sb("mean_gap", [P, GT])
        dev = sb("dev", [P, GT])
        var_eps = sb("var_eps", [P, GT])
        var_log = sb("var_log", [P, GT])
        r0 = sb("r0", [P, GT])
        r_sq = sb("r_sq", [P, GT])
        rstd = sb("rstd", [P, GT])
        probs = [sb(f"probs{i}", [P, HEADS, S]) for i in range(2)]
        row_max = [sb(f"row_max{i}", [P, HEADS]) for i in range(2)]
        mask2 = [sb(f"mask2{i}", [P, GT, S]) for i in range(2)]
        probs_t = sb("probs_t", [P, PAIRS, P])
        wide = [t[:, :, :].rearrange("p a b -> p (a b)")[:, i * GTOK:(i + 1) * GTOK]
                for t in (*probs, probs_t) for i in range(2)]
        hi = [t[:, :, :, :].rearrange("p b j k -> p (b j k)")[:, 0:GTOK].rearrange("p (u c) -> p u c", u=GT)
              for t in ci]
        rec = sb("rec", [P, PAIRS, 2])
        o = sb("o", [P, HEADS, HD])
        o_t = sb("o_t", [P, P])

        w_low = {"W": sb("w_low", [P, P]), "Wp": sb("w_low_p", [PROJ, P]), "sim": sb("w_sim", [PROJ, NLR]),
                 "bp": sb("w_bp", [PROJ, 1]), "temp": sb("w_temp", [P, 1])}
        w_route = sb("w_route", [P, ROUTE])
        b_route = sb("b_route", [P, ROUTE])
        w_up = sb("w_up", [P, P])
        w_gate = sb("w_gate", [P, EXPERTS])
        w_1 = sb("w_1", [P, EXPERTS, INTER])
        w_3 = sb("w_3", [P, EXPERTS, INTER])
        w_2 = sb("w_2", [P, EC, P])
        pick_expert = sb("pick_expert", [P, EC, P], mybir.dt.bfloat16)
        w_mix = {n: sb("w_mix_" + n, [P, P]) for n in "rkv"}
        mu = {n: sb("mu_" + n, [P, 1]) for n in "rk"}
        one_less_mu = {n: sb("one_less_mu_" + n, [P, 1]) for n in "rk"}
        w_qkv = [sb(f"w_qkv{l}", [P, 3 * INNER]) for l in range(DEPTH)]
        w_lo = [sb(f"w_lo{l}", [P, LPAIRS, P]) for l in range(DEPTH)]
        rot_base = sb("rot_base", [P, 4, LD])
        rot = [sb(f"rot{l}", [P, 4, LD]) for l in range(DEPTH)]
        rot_scale = sb("rot_scale", [P, DEPTH, 2, LD])
        w_up1 = [sb(f"w_up1{l}", [P, 2 * HID]) for l in range(DEPTH)]
        b_up1 = [sb(f"b_up1{l}", [P, 2 * len(HC)]) for l in range(DEPTH)]
        w_dn = [sb(f"w_dn{l}", [P, len(HC), P]) for l in range(DEPTH)]
        b_dn = [sb(f"b_dn{l}", [P, P]) for l in range(DEPTH)]
        ln_gb = [sb(f"ln_gb{l}", [P, 2]) for l in range(DEPTH)]
        ident_16 = sb("ident_16", [P, P], mybir.dt.bfloat16)
        masks = {n: sb("mask_16_" + n, [P, S], mybir.dt.bfloat16) for n in ("L1", "L3", "causal")}
        gates = sb("gates", [P, GT, P])
        gates_t = k_t
        gates_t16 = [sb(f"gates_t16{i}", [P, GTOK], mybir.dt.bfloat16) for i in range(2)]
        gate_high, gate_mid = (sb("gate_" + n, [P, GT, EXPERTS], mybir.dt.bfloat16) for n in ("high", "mid"))
        route = sb("route", [P, GT, ROUTE])
        small = {n: sb("small_" + n, [P, GT, 16]) for n in "abcdefgh"}
        tiny = {n: sb("tiny_" + n, [P, GT]) for n in "abcdef"}
        top8 = sb("top8", [P, GT, 8])

        ps_scores = [ctx.enter_context(nc.psum_tensor(f"ps_s{i}", [P, 2, 512], F32)) for i in range(2)]
        ps_pt = ctx.enter_context(nc.psum_tensor("ps_pt", [P, 2, 512], F32))
        ps_o = ctx.enter_context(nc.psum_tensor("ps_o", [P, 512], F32))
        ps_pj = ctx.enter_context(nc.psum_tensor("ps_pj", [P, 512], F32))

        loaded = signal("loaded")
        loaded_late = signal("loaded_late")
        zeroed = signal("zeroed")
        marked = signal("marked")
        drawn = signal("drawn")
        blanked = [signal("blanked0"), signal("blanked1")]
        picks_32 = probs[0][:, :, :].rearrange("p h k -> p (h k)")
        loads = [(x[:, :, :], x_in), (mask_l3_in[0:S, :], mask_l3), (mask_l3_in[S:P, :], mask_l3)]
        loads += [(attn_w[n][:, :], w[n]) for n in attn_w if n.startswith("L0")]
        late_loads = [(attn_w[n][:, :], w[n]) for n in attn_w if not n.startswith("L0")]
        late_loads += [(row_bias[n][0:1, :], w["b" + n]) for n in row_bias]
        late_loads += [(col_bias[n][:, :], w["b" + n]) for n in col_bias]
        late_loads += [(w_low[n][:, :], w["low_" + n]) for n in ("W", "Wp", "sim", "bp", "temp")]
        late_loads += [(w_route[:, 0:PROJ], w["low_WpT"]), (w_route[:, PROJ + NLR:ROUTE], w["low_Wd"]),
                       (w_up[0:RSUM, :], w["low_Wu"]), (w_gate[:, :], w["moe_gate"]), (w_1[:, :, :], w["moe_1"]),
                       (w_3[:, :, :], w["moe_3"]), (w_2[:, :, :], w["moe_2"])]
        late_loads += [(w_mix[n][:, :], w["mix_" + n]) for n in "rkv"]
        late_loads += [(mu[n][:, :], w["mu_" + n]) for n in "rk"]
        late_loads += [(rot_base[:, :, :], w["rot"]), (rot_scale[:, :, :, :], w["rot_scale"])]
        for l in range(DEPTH):
            late_loads += [(w_qkv[l][:, :], w["wqkv"][l]), (w_lo[l][:, :, :], w["lo"][l]),
                           (w_up1[l][:, :], w["up1"][l]),
                           (b_up1[l][:, :], w["b_up1"][l]), (w_dn[l][:, :, :], w["dn"][l]),
                           (b_dn[l][0:1, :], w["b_dn"][l]), (ln_gb[l][:, :], w["ln"][l])]

        def zero_keys_and_values(eng, i):
            blank = blanked[i]
            eng.memset(v2[i][:, :, :, :, :], 0.0).then_inc(blank.sem, 1)
            for j in range(2):
                eng.wait_ge(blank.sem, 1 + j)
                eng.memset(v2[i][j * S:(j + 1) * S, :, :, j, HD:VC], 1.0).then_inc(blank.sem, 1)
            eng.wait_ge(blank.sem, 3)
            eng.memset(kblk[i][:, :, :], 0.0).then_inc(blank.sem, 1)

        with nc.Block() as block:
            @block.sync
            def _(sp):
                for dst, src in loads:
                    sp.dma_start(dst, src).then_inc(loaded.sem, 16)
                sp.wait_ge(zeroed.sem, len(row_bias) + 3 + DEPTH)
                for dst, src in late_loads:
                    sp.dma_start(dst, src).then_inc(loaded_late.sem, 16)
                sp.wait_ge(loaded.sem, 16 * len(loads))

            @block.vector
            def _(dve):
                for n in row_bias:
                    dve.memset(row_bias[n][:, :], 0.0).then_inc(zeroed.sem, 1)
                dve.memset(ones[:, :], 1.0).then_inc(zeroed.sem, 1)
                dve.memset(minus_half[:, :], -0.5).then_inc(marked.sem, 1)
                dve.memset(w_up[:, :], 0.0).then_inc(zeroed.sem, 1)
                dve.memset(gates[:, :, :], 0.0).then_inc(zeroed.sem, 1)
                for l in range(DEPTH):
                    dve.memset(b_dn[l][:, :], 0.0).then_inc(zeroed.sem, 1)
                zero_keys_and_values(dve, 0)
                dve.wait_ge(loaded.sem, 16 * len(loads))
                dve.tensor_scalar(masks["L3"][:, :], mask_l3_in[:, :], -NEG, NEG, ALU.mult, ALU.add)\
                   .then_inc(marked.sem, 1)
                dve.wait_ge(drawn.sem, 14)
                for to, of in ((ident_16, ident), (masks["L1"], mask_l1_sb), (masks["causal"], causal)):
                    dve.tensor_copy(to[:, :], of[:, :]).then_inc(marked.sem, 1)
                dve.tensor_copy(pick_expert[:, :, :].rearrange("p c i -> p (c i)"), picks_32).then_inc(marked.sem, 1)

            @block.gpsimd
            def _(pool):
                zero_keys_and_values(pool, 1)
                pool.wait_ge(blanked[1].sem, 4)
                for n in GROUP_SIGNALS:
                    pool.sem_inc(signals[n].sem, 1)
                pool.memset(ident[:, :], 0.0).then_inc(drawn.sem, 1)
                pool.wait_ge(drawn.sem, 1)
                pool.affine_select(out=ident[:, :], in_=ident[:, :], compare_op=ALU.not_equal, fill=1.0,
                                   base=0, pattern=[[-1, P]], channel_multiplier=1).then_inc(drawn.sem, 1)
                pool.wait_ge(drawn.sem, 2)
                pool.memset(mask_l1_sb[:, :], 0.0).then_inc(drawn.sem, 1)
                for b in range(2):
                    rows = mask_l1_sb[b * S:(b + 1) * S, :]
                    pool.wait_ge(drawn.sem, 3 + 2 * b)
                    pool.affine_select(out=rows, in_=rows, compare_op=ALU.is_gt, fill=NEG,
                                       base=0, pattern=[[-1, S]], channel_multiplier=1)\
                        .then_inc(drawn.sem, 1)
                    pool.wait_ge(drawn.sem, 4 + 2 * b)
                    pool.memset(rows[0:1, 0:1], 0.0).then_inc(drawn.sem, 1)
                pool.wait_ge(drawn.sem, 7)
                pool.memset(causal[:, :], 0.0).then_inc(drawn.sem, 1)
                for b in range(2):
                    rows = causal[b * S:(b + 1) * S, :]
                    pool.wait_ge(drawn.sem, 8 + b)
                    pool.affine_select(out=rows, in_=rows, compare_op=ALU.is_ge, fill=NEG,
                                       base=0, pattern=[[-1, S]], channel_multiplier=1)\
                        .then_inc(drawn.sem, 1)
                pool.wait_ge(drawn.sem, 10)
                pool.memset(picks_32, 0.0).then_inc(drawn.sem, 1)
                pool.wait_ge(drawn.sem, 11)
                picks = picks_32.rearrange("p (c j i) -> p c j i", c=EC, j=2)
                for k in range(3):
                    pool.affine_select(out=picks, in_=picks, compare_op=ALU.not_equal, fill=1.0, base=-EXPERTS * k,
                                       pattern=[[-2, EC], [-1, 2], [0, INTER]], channel_multiplier=1)\
                        .then_inc(drawn.sem, 1)
                    pool.wait_ge(drawn.sem, 12 + k)

        sp_turn = signal("sp_turn")
        pool_turn = signal("pool_turn")
        dve_turn = signal("dve_turn")
        bn_done = signal("bn_done")
        var_ready = signal("var_ready")
        ln_ready = signal("ln_ready")
        r0_ready = signal("r0_ready")
        newton = signal("newton")
        x_norm_ready = signal("x_norm_ready")
        xt_in_psum = signal("xt_in_psum")
        xt_ready = signal("xt_ready")
        added = signal("added")

        def open_front(added_per, norm=True, root_on_pool=False):
            for s, per in ((xt_in_psum, 1), (xt_ready, 1), (added, added_per)):
                s.opens(per)
            if norm:
                for s, per in ((bn_done, GT + 6), (var_ready, 1), (ln_ready, 0 if root_on_pool else 1),
                               (r0_ready, 1), (newton, 4), (x_norm_ready, GT)):
                    s.opens(per)

        def tile_of(g, u):
            return x[:, bass.ds(g * GT + u, 1), :].rearrange("p a c -> p (a c)")

        def window_of(g):
            return x[:, bass.ds(g * GT, GT), :].rearrange("p u c -> p (u c)")

        def norm_stats(dve, g, shifted=None):
            for u in range(GT):
                rows = tile_of(g, u) if shifted is None else shifted[:, u, :]
                dve.bn_stats(bn[:, u, :], rows).then_inc(bn_done.sem, 1)
            dve.wait_ge(bn_done.sem, bn_done.at(g, GT))
            dve.tensor_tensor(mean[:, :], bn[:, :, 1], bn[:, :, 4], ALU.add).then_inc(bn_done.sem, 1)
            dve.tensor_tensor(mean_gap[:, :], bn[:, :, 1], bn[:, :, 4], ALU.subtract)\
               .then_inc(bn_done.sem, 1)
            dve.tensor_tensor(dev[:, :], bn[:, :, 2], bn[:, :, 5], ALU.add).then_inc(bn_done.sem, 1)
            dve.wait_ge(bn_done.sem, bn_done.at(g, GT + 3))
            dve.tensor_scalar(mean[:, :], mean[:, :], 0.5, None, ALU.mult).then_inc(bn_done.sem, 1)
            dve.tensor_tensor(mean_gap[:, :], mean_gap[:, :], mean_gap[:, :], ALU.mult)\
               .then_inc(bn_done.sem, 1)
            dve.tensor_scalar(dev[:, :], dev[:, :], 1.0 / P, LN_EPS, ALU.mult, ALU.add)\
               .then_inc(bn_done.sem, 1)
            dve.wait_ge(bn_done.sem, bn_done.at(g, GT + 6))
            dve.scalar_tensor_tensor(out=var_eps[:, :], in0=mean_gap[:, :], scalar=0.25,
                                     in1=dev[:, :], op0=ALU.mult, op1=ALU.add)\
               .then_inc(var_ready.sem, 1)

        def normalise(dve, g, shifted=None):
            dve.wait_ge(r0_ready.sem, r0_ready.at(g, 1))
            dve.tensor_tensor(r_sq[:, :], r0[:, :], r0[:, :], ALU.mult).then_inc(newton.sem, 1)
            dve.wait_ge(newton.sem, newton.at(g, 1))
            dve.tensor_tensor(r_sq[:, :], r_sq[:, :], var_eps[:, :], ALU.mult).then_inc(newton.sem, 1)
            dve.wait_ge(newton.sem, newton.at(g, 2))
            dve.tensor_scalar(r_sq[:, :], r_sq[:, :], -0.5, 1.5, ALU.mult, ALU.add)\
               .then_inc(newton.sem, 1)
            dve.wait_ge(newton.sem, newton.at(g, 3))
            dve.tensor_tensor(rstd[:, :], r0[:, :], r_sq[:, :], ALU.mult).then_inc(newton.sem, 1)
            dve.wait_ge(newton.sem, newton.at(g, 4))
            dve.wait_ge(xt_in_psum.sem, xt_in_psum.at(g, 0))
            for u in range(GT):
                rows = tile_of(g, u) if shifted is None else shifted[:, u, :]
                dve.tensor_scalar(x_norm[:, u, :], rows, mean[:, u:u + 1],
                                  rstd[:, u:u + 1], ALU.subtract, ALU.mult)\
                   .then_inc(x_norm_ready.sem, 1)

        def root_act(act, g):
            act.wait_ge(var_ready.sem, var_ready.at(g, 1))
            act.activation(var_log[:, :], var_eps[:, :], ACT.Ln).then_inc(ln_ready.sem, 1)
            act.wait_ge(ln_ready.sem, ln_ready.at(g, 1))
            act.wait_ge(newton.sem, newton.at(g, 0))
            act.activation(r0[:, :], var_log[:, :], ACT.Exp, scale=-0.5).then_inc(r0_ready.sem, 1)

        def root(pool, g):
            pool.wait_ge(var_ready.sem, var_ready.at(g, 1))
            pool.wait_ge(newton.sem, newton.at(g, 0))
            pool.tensor_tensor(r0[:, :], var_eps[:, :], minus_half[:, 0:GT], ALU.pow).then_inc(r0_ready.sem, 1)

        def transpose_x(pe, g):
            pe.wait_ge(x_norm_ready.sem, x_norm_ready.at(g, GT))
            for u in range(GT):
                last = pe.transpose(ps_pj[:, u * P:(u + 1) * P], x_norm[:, u, :], ident[:, :])
            last.then_inc(xt_in_psum.sem, 1)

        def run_groups_2(eng, body):
            with eng.Fori(0, GROUPS // 2 - 1) as pair:
                body(pair * 2, 0, True, True)
                body(pair * 2 + 1, 1, True, True)
            body(GROUPS - 2, 0, True, False)
            body(GROUPS - 1, 1, False, False)

        def cross_attention(name, scale, mask=None, mask_per_seq=None, project=True, relu=False):
            wq, wk, wv, wo = (attn_w.get(f"{name}_{n}", ident) for n in "qkvo")
            bv, bo = col_bias.get(name + "_v"), row_bias.get(name + "_o")
            bq, bk = col_bias.get(name + "_q"), col_bias.get(name + "_k")
            masked = mask_per_seq is not None

            open_front(GT)
            c_loaded = signal("c_loaded", 32)
            m_loaded = signal("m_loaded", 16 if mask_per_seq is not None else 0)
            k_placed = signal("k_placed", 16 * HEADS)
            k_in_psum = signal("k_in_psum", 1 if project else 0)
            kt_ready = signal("kt_ready", 1 if project else 0)
            v_in_psum = signal("v_in_psum", 2)
            v_even = signal("v_even", 2)
            v_odd = signal("v_odd", 2)
            q_in_psum = signal("q_in_psum", 1 if project else 0)
            qt_ready = signal("qt_ready", 1 if project else 0)
            scored = signal("scored", GT)
            max_ready = signal("max_ready", GT)
            mask_added = signal("mask_added", GT if masked else 0)
            shifted = signal("shifted", GT)
            exp_ready = signal("exp_ready", GT)
            turned = signal("turned", GT, 2)
            pt_ready = signal("pt_ready", GT)
            summed = signal("summed", GT)
            rec_ready = signal("rec_ready", 2 * GT)
            o_ready = signal("o_ready", 2 * GT)
            ot_in_psum = signal("ot_in_psum", GT)
            ot_ready = signal("ot_ready", GT)
            last_y = signal("last_y", 1)

            bias_added = signal("bias_added", 1 if bv is not None else 0)
            bias_made = signal("bias_made_" + name)

            q_signal = qt_ready if project else xt_ready
            accumulated = ps_o[:, 0:PAIRS * 2 * 2 * VC].rearrange("p (r b j c) -> p r b j c", b=2, j=2, c=VC)
            projected = ps_o[:, 384:384 + P]

            with nc.Block() as block:
                @block.sync
                def _(sp):
                    def load(g, par, first):
                        if not first:
                            sp.wait_ge(v_in_psum.sem, v_in_psum.at(g - 1, 1))
                            sp.sem_inc(sp_turn.sem, 1)
                        src = ctx_t[:, bass.ds(g * GTOK, GTOK)].rearrange("p (b k) -> p b k", k=S)
                        for j in range(2):
                            sp.dma_start(ci[par][:, :, j, :], src).then_inc(c_loaded.sem, 16)

                    def load_mask(g, par, first):
                        if mask_per_seq is None:
                            return
                        if not first:
                            sp.wait_ge(mask_added.sem, mask_added.at(g - 1, 1))
                            sp.sem_inc(sp_turn.sem, 1)
                        sp.dma_start(mask2[par][:, :, :], mask_per_seq[:, bass.ds(g * GT, GT), :])\
                          .then_inc(m_loaded.sem, 16)

                    def place_keys(g, par, first):
                        if project:
                            sp.wait_ge(kt_ready.sem, kt_ready.at(g, 1))
                        else:
                            sp.wait_ge(c_loaded.sem, c_loaded.at(g, 32))
                        sp.sem_inc(sp_turn.sem, 1)
                        if not first:
                            sp.wait_ge(scored.sem, scored.at(g - 1, 1))
                            sp.sem_inc(sp_turn.sem, 1)
                        src = k_t[:, :] if project else ci[par][:, :, 0, :]
                        for h in range(HEADS):
                            rows = slice(h * HD, (h + 1) * HD)
                            dst = kblk[par][rows, h, :]
                            if not project:
                                dst = dst.rearrange("p (b k) -> p b k", k=S)
                            sp.dma_start(dst, src[rows]).then_inc(k_placed.sem, 16)

                    def body(g, par, ahead, ahead2):
                        if ahead2:
                            load(g + 2, par, False)
                            load_mask(g + 2, par, False)
                            place_keys(g + 2, par, False)

                    load(0, 0, True)
                    load_mask(0, 0, True)
                    place_keys(0, 0, True)
                    load(1, 1, False)
                    load_mask(1, 1, False)
                    place_keys(1, 1, False)
                    run_groups_2(sp, body)

                @block.gpsimd
                def _(pool):
                    if bv is None:
                        return

                    def body(g, par, ahead, ahead2):
                        pool.wait_ge(x_norm_ready.sem, x_norm_ready.at(g, GT))
                        pool.sem_inc(pool_turn.sem, 1)
                        rows = x[:, bass.ds(g * GT, GT), :]
                        pool.tensor_tensor(rows, rows, out_bias[name][:, :].unsqueeze(1).broadcast_to([P, GT, P]),
                                           ALU.add).then_inc(bias_added.sem, 1)

                    pool.wait_ge(bias_made.sem, 3)
                    run_groups_2(pool, body)

                @block.vector
                def _(dve):
                    def values_even(g, par, c, first):
                        if not first:
                            dve.wait_ge(summed.sem, summed.at(g - 1, 0))
                        dve.wait_ge(v_in_psum.sem, v_in_psum.at(g, c + 1))
                        src = ps_pj[0:S, :].rearrange("p (b r j d) -> p b r j d", b=4, r=PAIRS, j=2)
                        dve.tensor_copy(v2[par][0:S, 4 * c:4 * c + 4, :, 0, 0:HD], src[:, :, :, 0, :])\
                           .then_inc(v_even.sem, 1)

                    def softmax(g, u, par):
                        s = u % 2
                        scores = ps_scores[s][:, :, :].rearrange("p a (h k) -> p (a h) k", k=S)
                        if u == 0 and mask_per_seq is not None:
                            dve.wait_ge(m_loaded.sem, m_loaded.at(g, 16))
                        dve.wait_ge(scored.sem, scored.at(g, u + 1))
                        dve.wait_ge(turned.sem, turned.at(g, u))
                        if masked:
                            m = mask2[par][:, u, :].unsqueeze(1).broadcast_to([P, HEADS, S])
                            dve.tensor_tensor(probs[s][:, :, :], scores, m, ALU.add).then_inc(mask_added.sem, 1)
                            scores = probs[s][:, :, :]
                            dve.wait_ge(mask_added.sem, mask_added.at(g, u + 1))
                        dve.tensor_reduce(row_max[s][:, :], scores, AX, ALU.max).then_inc(max_ready.sem, 1)
                        dve.wait_ge(max_ready.sem, max_ready.at(g, u + 1))
                        dve.tensor_tensor(probs[s][:, :, :], scores,
                                          row_max[s][:, :].unsqueeze(2).broadcast_to([P, HEADS, S]),
                                          ALU.subtract).then_inc(shifted.sem, 1)

                    def divide(g, u):
                        dve.wait_ge(summed.sem, summed.at(g, u + 1))
                        dve.wait_ge(ot_in_psum.sem, ot_in_psum.at(g, u))
                        for b in range(2):
                            rows = slice(b * S, (b + 1) * S)
                            dve.reciprocal(rec[rows, :, :], accumulated[rows, :, b, :, HD]).then_inc(rec_ready.sem, 1)
                        for b in range(2):
                            rows = slice(b * S, (b + 1) * S)
                            dve.wait_ge(rec_ready.sem, rec_ready.at(g, 2 * u + b + 1))
                            dve.tensor_tensor(o[rows, :, :].rearrange("p (r j) d -> p r j d", j=2),
                                              accumulated[rows, :, b, :, 0:HD],
                                              rec[rows, :, :].unsqueeze(3).broadcast_to([S, PAIRS, 2, HD]),
                                              ALU.mult).then_inc(o_ready.sem, 1)

                    def add_residual(g, u):
                        if u == 0 and bv is not None:
                            dve.wait_ge(bias_added.sem, bias_added.at(g, 1))
                            dve.sem_inc(dve_turn.sem, 1)
                        if u == GT - 1:
                            dve.wait_ge(last_y.sem, last_y.at(g, 1))
                        else:
                            dve.wait_ge(summed.sem, summed.at(g, u + 2))
                        rows = tile_of(g, u)
                        if relu:
                            dve.scalar_tensor_tensor(out=rows, in0=projected, scalar=0.0, in1=rows, op0=ALU.max,
                                                     op1=ALU.add).then_inc(added.sem, 1)
                        else:
                            dve.tensor_tensor(rows, projected, rows, ALU.add).then_inc(added.sem, 1)

                    def body(g, par, ahead, ahead2):
                        other = 1 - par
                        softmax(g, 1, par)
                        divide(g, 0)
                        softmax(g, 2, par)
                        divide(g, 1)
                        add_residual(g, 0)
                        softmax(g, 3, par)
                        if ahead:
                            values_even(g + 1, other, 0, False)
                        if ahead2:
                            norm_stats(dve, g + 2)
                        divide(g, 2)
                        add_residual(g, 1)
                        if ahead:
                            softmax(g + 1, 0, other)
                        divide(g, 3)
                        add_residual(g, 2)
                        if ahead:
                            values_even(g + 1, other, 1, False)
                        if ahead2:
                            normalise(dve, g + 2)
                        add_residual(g, 3)

                    norm_stats(dve, 0)
                    normalise(dve, 0)
                    if bv is not None:
                        dve.tensor_copy(o[:, :, :].rearrange("p h d -> p (h d)"), bv[:, 0:1].broadcast_to([P, P]))\
                           .then_inc(bias_made.sem, 1)
                    for c in range(2):
                        values_even(0, 0, c, True)
                    norm_stats(dve, 1)
                    normalise(dve, 1)
                    softmax(0, 0, 0)
                    run_groups_2(dve, body)

                @block.scalar
                def _(act):
                    act.preload_act_table_set(LN_EXP)

                    def keys(g):
                        if not project:
                            return
                        act.wait_ge(k_in_psum.sem, k_in_psum.at(g, 1))
                        act.wait_ge(k_placed.sem, k_placed.at(g, 0))
                        if bk is None:
                            act.activation(k_t[:, :], ps_pj[:, :], ACT.Copy).then_inc(kt_ready.sem, 1)
                        else:
                            act.activation(k_t[:, :], ps_pj[:, :], ACT.Identity, bias=bk[:, 0:1])\
                               .then_inc(kt_ready.sem, 1)

                    def values_odd(g, par, c, first):
                        if not first:
                            act.wait_ge(summed.sem, summed.at(g - 1, 0))
                        act.wait_ge(v_in_psum.sem, v_in_psum.at(g, c + 1))
                        src = ps_pj[S:P, :].rearrange("p (b r j d) -> p b r j d", b=4, r=PAIRS, j=2)
                        act.activation(v2[par][S:P, 4 * c:4 * c + 4, :, 1, 0:HD], src[:, :, :, 1, :], ACT.Copy)\
                           .then_inc(v_odd.sem, 1)

                    def x_transposed(g, par, first):
                        act.wait_ge(xt_in_psum.sem, xt_in_psum.at(g, 1))
                        if project:
                            act.wait_ge(q_in_psum.sem, q_in_psum.at(g, 0))
                            act.activation(x_norm_t[:, :], ps_pj[:, :], ACT.Copy).then_inc(xt_ready.sem, 1)
                        else:
                            if not first:
                                act.wait_ge(scored.sem, scored.at(g - 1, 0))
                            act.activation(q_t[par][:, :], ps_pj[:, :], ACT.Copy).then_inc(xt_ready.sem, 1)

                    def queries(g, par, first):
                        if not project:
                            return
                        act.wait_ge(q_in_psum.sem, q_in_psum.at(g, 1))
                        if not first:
                            act.wait_ge(scored.sem, scored.at(g - 1, 0))
                        if bq is None:
                            act.activation(q_t[par][:, :], ps_pj[:, :], ACT.Copy).then_inc(qt_ready.sem, 1)
                        else:
                            act.activation(q_t[par][:, :], ps_pj[:, :], ACT.Identity, bias=bq[:, 0:1])\
                               .then_inc(qt_ready.sem, 1)

                    def exponentials(g, u):
                        act.wait_ge(shifted.sem, shifted.at(g, u + 1))
                        p = probs[u % 2][:, :, :]
                        act.activation(p, p, ACT.Exp, scale=scale).then_inc(exp_ready.sem, 1)

                    def copy_turned(g, u):
                        act.wait_ge(turned.sem, turned.at(g, 2 + u + 1))
                        act.wait_ge(summed.sem, summed.at(g, u))
                        act.activation(probs_t[:, :, :], ps_pt[:, :, :].rearrange("p a (r t) -> p (a r) t", t=P),
                                       ACT.Copy).then_inc(pt_ready.sem, 1)

                    def o_transposed(g, u):
                        act.wait_ge(ot_in_psum.sem, ot_in_psum.at(g, u + 1))
                        act.activation(o_t[:, :], ps_pt[:, 0, 0:P], ACT.Copy).then_inc(ot_ready.sem, 1)

                    def body(g, par, ahead, ahead2):
                        other = 1 - par
                        copy_turned(g, 0)
                        exponentials(g, 1)
                        if ahead:
                            x_transposed(g + 1, other, False)
                        copy_turned(g, 1)
                        o_transposed(g, 0)
                        exponentials(g, 2)
                        if ahead:
                            queries(g + 1, other, False)
                            values_odd(g + 1, other, 0, False)
                        copy_turned(g, 2)
                        o_transposed(g, 1)
                        exponentials(g, 3)
                        if ahead2:
                            root_act(act, g + 2)
                        copy_turned(g, 3)
                        o_transposed(g, 2)
                        if ahead:
                            exponentials(g + 1, 0)
                            values_odd(g + 1, other, 1, False)
                        o_transposed(g, 3)
                        if ahead2:
                            keys(g + 2)

                    keys(0)
                    root_act(act, 0)
                    x_transposed(0, 0, True)
                    queries(0, 0, True)
                    for c in range(2):
                        values_odd(0, 0, c, True)
                    keys(1)
                    root_act(act, 1)
                    if bv is not None:
                        act.wait_ge(bias_made.sem, 2)
                        act.activation(out_bias[name][:, :], projected, ACT.Copy).then_inc(bias_made.sem, 1)
                    exponentials(0, 0)
                    run_groups_2(act, body)

                @block.tensor
                def _(pe):
                    pe.sem_inc(turned.sem, 2)

                    def project_k(g, par, first):
                        if not first:
                            pe.wait_ge(v_even.sem, v_even.at(g - 1, 2))
                            pe.wait_ge(v_odd.sem, v_odd.at(g - 1, 2))
                        if project:
                            pe.wait_ge(c_loaded.sem, c_loaded.at(g, 32))
                            pe.matmul(ps_pj[:, :], wk[:, :], ci[par][:, :, 0, :], start=True, stop=True)\
                              .then_inc(k_in_psum.sem, 1)

                    def turn_x(g):
                        if project:
                            pe.wait_ge(kt_ready.sem, kt_ready.at(g, 1))
                        transpose_x(pe, g)

                    def project_q(g):
                        if not project:
                            return
                        pe.wait_ge(xt_ready.sem, xt_ready.at(g, 1))
                        pe.matmul(ps_pj[:, :], wq[:, :], x_norm_t[:, :], start=True, stop=True)\
                          .then_inc(q_in_psum.sem, 1)

                    def project_v(g, par, c):
                        if c == 0:
                            pe.wait_ge(c_loaded.sem, c_loaded.at(g, 32))
                            pe.wait_ge(q_signal.sem, q_signal.at(g, 1))
                        else:
                            pe.wait_ge(v_even.sem, v_even.at(g, 1))
                            pe.wait_ge(v_odd.sem, v_odd.at(g, 1))
                        for b in range(4):
                            twice = ci[par][:, 4 * c + b, :, :].rearrange("p j k -> p (j k)")
                            dst = ps_pj[:, b * P:(b + 1) * P]
                            last = pe.matmul(dst, twice, wv[:, :], start=True, stop=True)
                        last.then_inc(v_in_psum.sem, 1)

                    def scores(g, u, par, reuse=True):
                        if u == 0:
                            pe.wait_ge(q_signal.sem, q_signal.at(g, 1))
                            pe.wait_ge(k_placed.sem, k_placed.at(g, 16 * HEADS))
                        if reuse:
                            free = mask_added if masked else shifted
                            pe.wait_ge(free.sem, free.at(g, u - 1))
                        for half in range(2):
                            if mask is not None:
                                pe.matmul(ps_scores[u % 2][:, half, :].rearrange("p (h k) -> p h k", k=S),
                                          ident_16[:, :], mask[:, :].unsqueeze(1).broadcast_to([P, PAIRS, S]),
                                          start=True, stop=False, skip_group_check=True)
                            for b in range(2):
                                tok = slice((2 * u + b) * S, (2 * u + b + 1) * S)
                                last = pe.matmul(
                                    ps_scores[u % 2][b * S:(b + 1) * S, half, :], q_t[par][:, tok],
                                    kblk[par][:, half * 8:half * 8 + 8, tok], start=mask is None, stop=True,
                                    skip_group_check=mask is not None)
                        last.then_inc(scored.sem, 1)

                    def turn_probs(g, u):
                        pe.wait_ge(exp_ready.sem, exp_ready.at(g, u + 1))
                        flat = probs[u % 2][:, :, :].rearrange("p h k -> p (h k)")
                        for r in range(PAIRS):
                            last = pe.transpose(ps_pt[:, r // 4, (r % 4) * P:(r % 4 + 1) * P],
                                                flat[:, r * P:(r + 1) * P], ident[:, :])
                        last.then_inc(turned.sem, 1)

                    def turn_o(g, u, last_turned):
                        pe.wait_ge(pt_ready.sem, pt_ready.at(g, last_turned + 1))
                        pe.wait_ge(o_ready.sem, o_ready.at(g, 2 * u + 2))
                        pe.transpose(ps_pt[:, 0, 0:P], o[:, :, :].rearrange("p h d -> p (h d)"), ident[:, :])\
                          .then_inc(ot_in_psum.sem, 1)

                    def weigh_values(g, u, par):
                        pe.wait_ge(pt_ready.sem, pt_ready.at(g, u + 1))
                        if u == 0:
                            pe.wait_ge(v_even.sem, v_even.at(g, 2))
                            pe.wait_ge(v_odd.sem, v_odd.at(g, 2))
                        pe.wait_ge(o_ready.sem, o_ready.at(g, 2 * u))
                        pe.wait_ge(added.sem, added.at(g, max(u - 1, 0)))
                        for r in range(PAIRS):
                            n = 4 * VC
                            last = pe.matmul(ps_o[:, r * n:(r + 1) * n], probs_t[:, r, :],
                                             v2[par][:, 2 * u:2 * u + 2, r, :, :], start=True, stop=True)
                        if u:
                            last = project_o(g, u - 1)
                        last.then_inc(summed.sem, 1)

                    def project_o(g, u):
                        pe.wait_ge(ot_ready.sem, ot_ready.at(g, u + 1))
                        last = pe.matmul(projected, o_t[:, :], wo[:, :], start=True, stop=not relu)
                        if relu:
                            last = pe.matmul(projected, ones[:, :], bo[:, :], start=False, stop=True)
                        return last

                    def body(g, par, ahead, ahead2):
                        other = 1 - par
                        turn_probs(g, 0)
                        if ahead:
                            turn_x(g + 1)
                        scores(g, 2, par)
                        weigh_values(g, 0, par)
                        turn_probs(g, 1)
                        scores(g, 3, par)
                        turn_o(g, 0, 1)
                        if ahead:
                            project_q(g + 1)
                        weigh_values(g, 1, par)
                        if ahead:
                            project_v(g + 1, other, 0)
                        turn_probs(g, 2)
                        if ahead:
                            scores(g + 1, 0, other)
                        turn_o(g, 1, 2)
                        weigh_values(g, 2, par)
                        turn_probs(g, 3)
                        if ahead:
                            scores(g + 1, 1, other)
                        turn_o(g, 2, 3)
                        weigh_values(g, 3, par)
                        if ahead:
                            project_v(g + 1, other, 1)
                        turn_o(g, 3, 3)
                        if ahead2:
                            project_k(g + 2, par, False)
                        pe.wait_ge(added.sem, added.at(g, GT - 1))
                        project_o(g, GT - 1).then_inc(last_y.sem, 1)

                    project_k(0, 0, True)
                    turn_x(0)
                    project_q(0)
                    for c in range(2):
                        project_v(0, 0, c)
                    project_k(1, 1, False)
                    if bv is not None:
                        pe.wait_ge(bias_made.sem, 1)
                        pe.matmul(projected, o[:, :, :].rearrange("p h d -> p (h d)"), wo[:, :], start=True, stop=False)
                        pe.matmul(projected, ones[:, :], bo[:, :], start=False, stop=True).then_inc(bias_made.sem, 1)
                    scores(0, 0, 0, False)
                    scores(0, 1, 0, False)
                    if bv is not None:
                        pe.wait_ge(bias_made.sem, 3)
                    run_groups_2(pe, body)
            close_stage()

        def run_groups(eng, body):
            with eng.Fori(0, GROUPS - 2, 2) as g:
                body(g, 0, True)
                body(g + 1, 1, True)
            body(GROUPS - 2, 0, True)
            body(GROUPS - 1, 1, False)

        class Steps:

            def __init__(self, eng, sig, g, k=0):
                self.eng, self.sig, self.g, self.k = eng, sig, g, k

            def __call__(self, ins):
                self.k += 1
                ins.then_inc(self.sig.sem, 1)
                self.eng.wait_ge(self.sig.sem, self.sig.at(self.g, self.k))

        def copy_x_transposed(act, g, par, used, used_value):
            act.wait_ge(xt_in_psum.sem, xt_in_psum.at(g, 1))
            if used is not None:
                act.wait_ge(used.sem, used_value)
            act.activation(q_t[par][:, :], ps_pj[:, :], ACT.Copy).then_inc(xt_ready.sem, 1)

        def prepare_low_rank():
            prep = signal("prep_dve")
            prep_pe, prep_act = signal("prep_pe"), signal("prep_act")
            sim, sq, nrm = w_low["sim"], small["a"][:, 0, 0:NLR], small["b"][:, 0, 0:NLR]
            root_, work = small["c"][:, 0, 0:NLR], small["d"][:, 0, 0:NLR]
            temp = w_low["temp"]
            with nc.Block() as block:
                @block.vector
                def _(dve):
                    step = Steps(dve, prep, 0)
                    step(dve.tensor_tensor(sq[0:PROJ, :], sim[:, :], sim[:, :], ALU.mult))
                    step(dve.tensor_scalar(temp[:, :], temp[:, :], float(np.log(100.0)), None, ALU.min))
                    step(dve.memset(wide[0][:, 0:P], 0.0))
                    step(dve.tensor_scalar(wide[0][0:PROJ, 0:P], ones[0:PROJ, :], w_low["bp"][:, 0:1], None, ALU.mult))
                    dve.wait_ge(prep_pe.sem, 1)
                    step(dve.tensor_scalar(nrm, ps_pj[:, 0:NLR], 1e-24, float(2 ** LOG_SCALE), ALU.max, ALU.mult))
                    dve.wait_ge(prep_act.sem, 3)
                    step(dve.tensor_tensor(work, root_, root_, ALU.mult))
                    step(dve.tensor_tensor(work, work, nrm, ALU.mult))
                    step(dve.tensor_scalar(work, work, -0.5, 1.5, ALU.mult, ALU.add))
                    step(dve.tensor_tensor(root_, root_, work, ALU.mult))
                    step(dve.tensor_scalar(root_, root_, float(2 ** LOG_SCALE), None, ALU.mult))
                    step(dve.tensor_scalar(root_, root_, temp[:, 0:1], None, ALU.mult))
                    step(dve.tensor_tensor(sim[:, :], sim[:, :], root_[0:PROJ, :], ALU.mult))
                    dve.wait_ge(prep_pe.sem, 3)
                    step(dve.tensor_copy(w_route[:, PROJ:PROJ + NLR], ps_pj[:, 0:NLR]))
                    step(dve.tensor_copy(b_route[:, 0:PROJ + NLR], ps_o[:, 0:PROJ + NLR]))
                    step(dve.memset(b_route[:, PROJ + NLR:ROUTE], 0.0))

                @block.scalar
                def _(act):
                    act.preload_act_table_set(LN_EXP)
                    act.wait_ge(prep.sem, prep.at(0, 2))
                    act.activation(temp[:, :], temp[:, :], ACT.Exp).then_inc(prep_act.sem, 1)
                    act.wait_ge(prep.sem, prep.at(0, 5))
                    act.activation(work, nrm, ACT.Ln).then_inc(prep_act.sem, 1)
                    act.wait_ge(prep_act.sem, 2)
                    act.activation(root_, work, ACT.Exp, scale=-0.5).then_inc(prep_act.sem, 1)

                @block.tensor
                def _(pe):
                    pe.wait_ge(prep.sem, prep.at(0, 4))
                    pe.matmul(ps_pj[:, 0:NLR], ones[0:PROJ, :], sq[0:PROJ, :], start=True, stop=True)\
                      .then_inc(prep_pe.sem, 1)
                    pe.wait_ge(prep.sem, prep.at(0, 12))
                    pe.matmul(ps_pj[:, 0:NLR], w_low["Wp"][:, :], sim[:, :], start=True, stop=True)\
                      .then_inc(prep_pe.sem, 1)
                    pe.matmul(ps_o[:, 0:PROJ], wide[0][0:PROJ, 0:P], ident[0:PROJ, 0:PROJ], start=True, stop=True)
                    pe.matmul(ps_o[:, PROJ:PROJ + NLR], wide[0][0:PROJ, 0:P], sim[:, :], start=True, stop=True)\
                      .then_inc(prep_pe.sem, 1)

        def low_rank_experts():
            open_front(1, root_on_pool=True)
            route_in_psum = signal("route_in_psum", 1)
            chain = signal("chain", 25)
            norm_ready = signal("norm_ready", 1)
            root_steps = signal("root_steps", 2)
            logit_ready = signal("logit_ready", 1)
            expo_ready = signal("expo_ready", 1)
            gates_ready = signal("gates_ready", NLR)
            gates_in_psum = signal("gates_in_psum", 1)
            gates_t_ready = signal("gates_t_ready", 1)
            y_done = signal("y_done", 1)

            with nc.Block() as block:
                @block.tensor
                def _(pe):
                    def turn_and_route(g, par, first=False):
                        if not first:
                            pe.wait_ge(xt_ready.sem, xt_ready.at(g - 1, 1))
                        transpose_x(pe, g)
                        pe.wait_ge(xt_ready.sem, xt_ready.at(g, 1))
                        if not first:
                            pe.wait_ge(chain.sem, chain.at(g - 1, 1))
                        for u in range(GT):
                            last = pe.matmul(ps_pt[:, 0, u * ROUTE:(u + 1) * ROUTE],
                                             q_t[par][:, u * P:(u + 1) * P], w_route[:, :],
                                             start=True, stop=True)
                        last.then_inc(route_in_psum.sem, 1)

                    def base(g, par):
                        pe.wait_ge(added.sem, added.at(g, 0))
                        for u in range(GT):
                            pe.matmul(ps_o[:, u * P:(u + 1) * P], q_t[par][:, u * P:(u + 1) * P],
                                      w_low["W"][:, :], start=u == 0, stop=False, skip_group_check=True)

                    def up(g):
                        pe.wait_ge(gates_ready.sem, gates_ready.at(g, NLR))
                        pe.wait_ge(gates_t_ready.sem, gates_t_ready.at(g, 0))
                        for u in range(GT):
                            last = pe.transpose(ps_pt[:, 1, u * P:(u + 1) * P], gates[:, u, :], ident[:, :])
                        last.then_inc(gates_in_psum.sem, 1)
                        pe.wait_ge(gates_t_ready.sem, gates_t_ready.at(g, 1))
                        for u in range(GT):
                            last = pe.matmul(ps_o[:, u * P:(u + 1) * P], gates_t[:, u * P:(u + 1) * P],
                                             w_up[:, :], start=False, stop=True, skip_group_check=True)
                        last.then_inc(y_done.sem, 1)

                    def body(g, par, ahead, ahead2):
                        base(g, par)
                        up(g)
                        if ahead2:
                            turn_and_route(g + 2, par)

                    turn_and_route(0, 0, True)
                    turn_and_route(1, 1)
                    run_groups_2(pe, body)

                @block.scalar
                def _(act):
                    act.preload_act_table_set(LN_EXP)

                    def route_exps(g):
                        act.wait_ge(norm_ready.sem, norm_ready.at(g, 1))
                        act.activation(tiny["b"][:, :], tiny["a"][:, :], ACT.Ln).then_inc(root_steps.sem, 1)
                        act.wait_ge(root_steps.sem, root_steps.at(g, 1))
                        act.activation(tiny["c"][:, :], tiny["b"][:, :], ACT.Exp, scale=-0.5)\
                           .then_inc(root_steps.sem, 1)
                        act.wait_ge(logit_ready.sem, logit_ready.at(g, 1))
                        act.activation(small["b"][:, :, 0:NLR], small["a"][:, :, 0:NLR], ACT.Exp)\
                           .then_inc(expo_ready.sem, 1)

                    def body(g, par, ahead, ahead2):
                        act.wait_ge(gates_in_psum.sem, gates_in_psum.at(g, 1))
                        act.wait_ge(y_done.sem, y_done.at(g, 0))
                        act.activation(gates_t[:, :], ps_pt[:, 1, :], ACT.Copy).then_inc(gates_t_ready.sem, 1)
                        if ahead:
                            route_exps(g + 1)
                        if ahead2:
                            copy_x_transposed(act, g + 2, par, y_done, y_done.at(g, 1))

                    copy_x_transposed(act, 0, 0, None, 0)
                    copy_x_transposed(act, 1, 1, None, 0)
                    route_exps(0)
                    run_groups_2(act, body)

                @block.gpsimd
                def _(pool):
                    root(pool, 0)
                    root(pool, 1)
                    run_groups_2(pool, lambda g, par, ahead, ahead2: root(pool, g + 2) if ahead2 else None)

                @block.vector
                def _(dve):
                    def col(t, i):
                        return small[t][:, :, i]

                    def choose(g, more):
                        step = Steps(dve, chain, g)
                        if more:
                            norm_stats(dve, g + 1)
                        dve.wait_ge(gates_ready.sem, gates_ready.at(g, 0))
                        dve.wait_ge(route_in_psum.sem, route_in_psum.at(g, 1))
                        rs = route[:, :, :]
                        step(dve.tensor_tensor(rs, ps_pt[:, 0, 0:GT * ROUTE].rearrange("p (u c) -> p u c", u=GT),
                                               b_route[:, :].unsqueeze(1).broadcast_to([P, GT, ROUTE]), ALU.add))
                        sq = wide[1][:, 0:GT * PROJ].rearrange("p (u c) -> p u c", u=GT)
                        step(dve.tensor_tensor(sq, rs[:, :, 0:PROJ], rs[:, :, 0:PROJ], ALU.mult))
                        step(dve.tensor_reduce(tiny["d"][:, :], sq, AX, ALU.add))
                        dve.tensor_scalar(tiny["a"][:, :], tiny["d"][:, :], 1e-24, float(2 ** LOG_SCALE),
                                          ALU.max, ALU.mult).then_inc(norm_ready.sem, 1)
                        if more:
                            normalise(dve, g + 1)
                        dve.wait_ge(norm_ready.sem, norm_ready.at(g, 1))
                        dve.wait_ge(root_steps.sem, root_steps.at(g, 2))
                        a, b, c, d = (tiny[n][:, :] for n in "abcd")
                        step(dve.tensor_tensor(d, c, c, ALU.mult))
                        step(dve.tensor_tensor(d, d, a, ALU.mult))
                        step(dve.tensor_scalar(d, d, -0.5, 1.5, ALU.mult, ALU.add))
                        step(dve.tensor_tensor(d, d, c, ALU.mult))
                        lg = small["a"][:, :, 0:NLR]
                        step(dve.tensor_tensor(lg, rs[:, :, PROJ:PROJ + NLR],
                                               d.unsqueeze(2).broadcast_to([P, GT, NLR]), ALU.mult))
                        step(dve.tensor_reduce(tiny["e"][:, :], lg, AX, ALU.max))
                        dve.tensor_tensor(lg, lg, tiny["e"][:, :].unsqueeze(2).broadcast_to([P, GT, NLR]),
                                          ALU.subtract).then_inc(logit_ready.sem, 1)
                        dve.wait_ge(logit_ready.sem, logit_ready.at(g, 1))
                        step(dve.tensor_scalar(small["c"][:, :, 0:NLR], lg, 0.0, None, ALU.is_equal))
                        step(dve.tensor_copy(col("d", 0), col("c", 0)))
                        for i in range(1, NLR):
                            step(dve.tensor_tensor(col("e", i), col("c", i), col("d", i - 1), ALU.is_gt))
                            if i < NLR - 1:
                                step(dve.tensor_tensor(col("d", i), col("d", i - 1), col("c", i), ALU.max))
                        step(dve.tensor_copy(col("e", 0), col("c", 0)))
                        dve.wait_ge(expo_ready.sem, expo_ready.at(g, 1))
                        step(dve.tensor_reduce(tiny["f"][:, :], small["b"][:, :, 0:NLR], AX, ALU.add))
                        step(dve.reciprocal(tiny["f"][:, :], tiny["f"][:, :]))
                        step(dve.tensor_tensor(small["e"][:, :, 0:NLR], small["e"][:, :, 0:NLR],
                                               small["b"][:, :, 0:NLR], ALU.mult))
                        step(dve.tensor_tensor(small["e"][:, :, 0:NLR], small["e"][:, :, 0:NLR],
                                               tiny["f"][:, :].unsqueeze(2).broadcast_to([P, GT, NLR]), ALU.mult))
                        dve.wait_ge(gates_in_psum.sem, gates_in_psum.at(g, 0))
                        at = 0
                        for i, r in enumerate(RANKS):
                            dve.tensor_tensor(gates[:, :, at:at + r], rs[:, :, PROJ + NLR + at:PROJ + NLR + at + r],
                                              small["e"][:, :, i:i + 1].broadcast_to([P, GT, r]), ALU.mult)\
                               .then_inc(gates_ready.sem, 1)
                            at += r
                        while step.k < 25:
                            step.k += 1
                            dve.sem_inc(chain.sem, 1)

                    def body(g, par, ahead, ahead2):
                        if ahead:
                            choose(g + 1, ahead2)
                        dve.wait_ge(y_done.sem, y_done.at(g, 1))
                        flat = window_of(g)
                        dve.tensor_tensor(flat, ps_o[:, :], flat, ALU.add).then_inc(added.sem, 1)

                    norm_stats(dve, 0)
                    normalise(dve, 0)
                    choose(0, True)
                    run_groups_2(dve, body)
            close_stage()

        def mixture():
            open_front(1, root_on_pool=True)
            CH = 20
            SLOTS = 4
            router_in_psum = signal("route_in_psum", 1)
            router_copied = signal("router_copied", 1)
            chain = signal("chain", CH)
            picked = signal("picked", 1)
            top_ready = signal("top_ready", GT)
            logit_ready = signal("logit_ready", 1)
            expo_ready = signal("expo_ready", 1)
            gates_ready = signal("gates_ready", 3)
            gates_in_psum = signal("gates_in_psum", 1)
            gates_t_ready = signal("gates_t_ready", 1)
            hidden_in_psum = signal("hidden_in_psum", EC)
            silu_done = signal("silu_done", EC, 2)
            times_up = signal("times_up", EC, 2)
            weighted = signal("weighted", EC, 2)
            mixed = signal("mixed", EC, SLOTS)
            bank_g = [ps_scores[i][:, 0, :] for i in range(2)]
            bank_u = [ps_scores[i][:, 1, :] for i in range(2)]
            bank_s = [ps_pt[:, i, :] for i in range(2)]
            hid = wide[0:SLOTS]

            with nc.Block() as block:
                @block.tensor
                def _(pe):
                    pe.sem_inc(mixed.sem, SLOTS)

                    def router(g, par):
                        pe.wait_ge(xt_ready.sem, xt_ready.at(g, 1))
                        for u in range(GT):
                            last = pe.matmul(ps_pj[:, u * EXPERTS:(u + 1) * EXPERTS],
                                             q_t[par][:, u * P:(u + 1) * P], w_gate[:, :], start=True, stop=True)
                        last.then_inc(router_in_psum.sem, 1)

                    def transpose_gates(g):
                        pe.wait_ge(gates_ready.sem, gates_ready.at(g, 3))
                        for u in range(GT):
                            last = pe.transpose(ps_pj[:, u * P:(u + 1) * P], gates[:, u, :], ident[:, :])
                        last.then_inc(gates_in_psum.sem, 1)

                    def hidden(g, c, par):
                        s = c % 2
                        pe.wait_ge(silu_done.sem, silu_done.at(g, c + 1))
                        pe.matmul(bank_g[s], w_1[:, 2 * c:2 * c + 2, :].rearrange("p e i -> p (e i)"),
                                  q_t[par][:, :], start=True, stop=True)
                        pe.wait_ge(times_up.sem, times_up.at(g, c + 1))
                        pe.matmul(bank_u[s], w_3[:, 2 * c:2 * c + 2, :].rearrange("p e i -> p (e i)"),
                                  q_t[par][:, :], start=True, stop=True)
                        pe.wait_ge(weighted.sem, weighted.at(g, c + 1))
                        if c == 0:
                            pe.wait_ge(gates_t_ready.sem, gates_t_ready.at(g, 1))
                        pe.matmul(bank_s[s], pick_expert[:, c, :], gates_t16[par][:, :], start=True, stop=True)\
                          .then_inc(hidden_in_psum.sem, 1)

                    def mix(g, c):
                        pe.wait_ge(weighted.sem, weighted.at(g, c + 3))
                        if c == 0:
                            pe.wait_ge(added.sem, added.at(g, 0))
                        for u in range(GT):
                            last = pe.matmul(ps_o[:, u * P:(u + 1) * P], hid[c % SLOTS][:, u * P:(u + 1) * P],
                                             w_2[:, c, :], start=c == 0 and u == 0, stop=c == EC - 1,
                                             skip_group_check=True)
                        last.then_inc(mixed.sem, 1)

                    def body(g, par, ahead, ahead2):
                        for c in range(2, EC):
                            hidden(g, c, par)
                            mix(g, c - 2)
                            if ahead and c == 2:
                                transpose_x(pe, g + 1)
                            if ahead and c == 3:
                                router(g + 1, 1 - par)
                            if ahead and c == 7:
                                transpose_gates(g + 1)
                        for c in range(2):
                            if ahead:
                                hidden(g + 1, c, 1 - par)
                            mix(g, EC - 2 + c)

                    transpose_x(pe, 0)
                    router(0, 0)
                    transpose_gates(0)
                    for c in range(2):
                        hidden(0, c, 0)
                    run_groups_2(pe, body)

                @block.scalar
                def _(act):
                    act.preload_act_table_set(LN_EXP)
                    act.sem_inc(silu_done.sem, 2)

                    def exps(g):
                        act.wait_ge(logit_ready.sem, logit_ready.at(g, 1))
                        act.activation(small["b"][:, :, :], small["a"][:, :, :], ACT.Exp).then_inc(expo_ready.sem, 1)

                    def copy_gates(g, par):
                        act.wait_ge(gates_in_psum.sem, gates_in_psum.at(g, 1))
                        act.activation(gates_t16[par][:, :], ps_pj[:, :], ACT.Copy).then_inc(gates_t_ready.sem, 1)

                    def silu(g, c):
                        act.wait_ge(hidden_in_psum.sem, hidden_in_psum.at(g, c + 1))
                        act.wait_ge(mixed.sem, mixed.at(g, c + 1))
                        act.activation(hid[c % SLOTS][:, :], bank_g[c % 2], ACT.Silu).then_inc(silu_done.sem, 1)

                    def body(g, par, ahead, ahead2):
                        for c in range(2, EC):
                            silu(g, c)
                            if ahead and c == 2:
                                copy_x_transposed(act, g + 1, 1 - par, hidden_in_psum, hidden_in_psum.at(g, 0))
                            if ahead and c == 4:
                                exps(g + 1)
                        if ahead:
                            copy_gates(g + 1, 1 - par)
                            for c in range(2):
                                silu(g + 1, c)

                    copy_x_transposed(act, 0, 0, None, 0)
                    exps(0)
                    copy_gates(0, 0)
                    for c in range(2):
                        silu(0, c)
                    run_groups_2(act, body)

                @block.gpsimd
                def _(pool):
                    root(pool, 0)
                    root(pool, 1)
                    run_groups_2(pool, lambda g, par, ahead, ahead2: root(pool, g + 2) if ahead2 else None)

                @block.vector
                def _(dve):
                    dve.sem_inc(times_up.sem, 2)
                    dve.sem_inc(weighted.sem, 2)

                    lg, pick, eq = small["c"][:, :, :], small["d"][:, :, :], small["e"][:, :, :]

                    def compare(g):
                        step = Steps(dve, chain, g)
                        dve.wait_ge(router_in_psum.sem, router_in_psum.at(g, 1))
                        dve.tensor_copy(lg, ps_pj[:, 0:GT * EXPERTS].rearrange("p (u e) -> p u e", u=GT))\
                           .then_inc(router_copied.sem, 1)
                        dve.wait_ge(router_copied.sem, router_copied.at(g, 1))
                        dve.sem_inc(dve_turn.sem, 1)
                        for u in range(GT):
                            dve.max(top8[:, u, :], small["c"][:, u, :]).then_inc(top_ready.sem, 1)
                        dve.wait_ge(top_ready.sem, top_ready.at(g, GT))
                        dve.tensor_tensor(small["a"][:, :, :], lg, top8[:, :, 0:1].broadcast_to([P, GT, EXPERTS]),
                                          ALU.subtract).then_inc(logit_ready.sem, 1)
                        fourth = top8[:, :, TOPK - 1:TOPK].broadcast_to([P, GT, EXPERTS])
                        step(dve.tensor_tensor(pick, lg, fourth, ALU.is_gt))
                        step(dve.tensor_tensor(eq, lg, fourth, ALU.is_equal))
                        step(dve.tensor_reduce(tiny["a"][:, :], pick, AX, ALU.add))

                    def choose(g):
                        step = Steps(dve, chain, g, 3)
                        src, at = "e", 1
                        for dst in ("f", "g", "f", "g"):
                            step(dve.tensor_copy(small[dst][:, :, 0:at], small[src][:, :, 0:at]))
                            step(dve.tensor_tensor(small[dst][:, :, at:], small[src][:, :, at:],
                                                   small[src][:, :, 0:EXPERTS - at], ALU.add))
                            src, at = dst, 2 * at
                        cnt = small[src][:, :, :]
                        step(dve.tensor_tensor(cnt, cnt, tiny["a"][:, :].unsqueeze(2).broadcast_to([P, GT, EXPERTS]),
                                               ALU.add))
                        step(dve.scalar_tensor_tensor(out=eq, in0=cnt, scalar=float(TOPK), in1=eq,
                                                      op0=ALU.is_le, op1=ALU.mult))
                        step(dve.tensor_tensor(pick, pick, eq, ALU.add))

                    def weigh(g):
                        step = Steps(dve, chain, g, CH - 6)
                        dve.wait_ge(expo_ready.sem, expo_ready.at(g, 1))
                        kept = small["h"][:, :, :]
                        dve.wait_ge(chain.sem, chain.at(g, CH - 6))
                        dve.tensor_tensor(kept, small["b"][:, :, :], small["d"][:, :, :], ALU.mult)\
                           .then_inc(picked.sem, 1)
                        dve.wait_ge(picked.sem, picked.at(g, 1))
                        step(dve.tensor_reduce(tiny["b"][:, :], kept, AX, ALU.add))
                        step(dve.reciprocal(tiny["b"][:, :], tiny["b"][:, :]))
                        full, rest = small["b"][:, :, :], small["f"][:, :, :]
                        high, mid = gate_high[:, :, :], gate_mid[:, :, :]
                        step(dve.tensor_tensor(full, kept, tiny["b"][:, :].unsqueeze(2).broadcast_to([P, GT, EXPERTS]),
                                               ALU.mult))
                        step(dve.tensor_copy(high, full))
                        step(dve.tensor_tensor(rest, full, high, ALU.subtract))
                        step(dve.tensor_copy(mid, rest))
                        dve.wait_ge(gates_in_psum.sem, gates_in_psum.at(g, 0))
                        dve.tensor_copy(gates[:, :, 0:EXPERTS], high).then_inc(gates_ready.sem, 1)
                        dve.tensor_copy(gates[:, :, EXPERTS:2 * EXPERTS], mid).then_inc(gates_ready.sem, 1)
                        dve.tensor_tensor(gates[:, :, 2 * EXPERTS:3 * EXPERTS], rest, mid, ALU.subtract)\
                           .then_inc(gates_ready.sem, 1)

                    def combine(g, c):
                        h = hid[c % SLOTS][:, :]
                        dve.wait_ge(silu_done.sem, silu_done.at(g, c + 3))
                        dve.tensor_tensor(h, h, bank_u[c % 2], ALU.mult).then_inc(times_up.sem, 1)
                        dve.wait_ge(times_up.sem, times_up.at(g, c + 3))
                        dve.tensor_tensor(h, h, bank_s[c % 2], ALU.mult).then_inc(weighted.sem, 1)

                    def body(g, par, ahead, ahead2):
                        for c in range(2, EC):
                            combine(g, c)
                            if ahead2 and c == 2:
                                norm_stats(dve, g + 2)
                            if ahead and c == 3:
                                compare(g + 1)
                            if ahead and c == 4:
                                choose(g + 1)
                            if ahead and c == 5:
                                weigh(g + 1)
                            if ahead2 and c == 6:
                                normalise(dve, g + 2)
                        if ahead:
                            for c in range(2):
                                combine(g + 1, c)
                        dve.wait_ge(mixed.sem, mixed.at(g, EC + SLOTS))
                        flat = window_of(g)
                        dve.tensor_tensor(flat, ps_o[:, :], flat, ALU.add).then_inc(added.sem, 1)

                    norm_stats(dve, 0)
                    normalise(dve, 0)
                    compare(0)
                    choose(0)
                    weigh(0)
                    norm_stats(dve, 1)
                    normalise(dve, 1)
                    for c in range(2):
                        combine(0, c)
                    run_groups_2(dve, body)
            close_stage()

        def channel_mix():
            open_front(1, root_on_pool=True)
            damped = signal("damped", 2)
            blended = signal("blended", 4)
            rk_in_psum = signal("rk_in_psum", 2)
            relu_done = signal("relu_done", 1)
            squared = signal("squared", 1)
            v_done = signal("v_done", 1)
            sig = signal("sig", 1)
            gated_v = signal("gated_v", 1)
            bank_r, bank_k, bank_v = ps_scores[0][:, 0, :], ps_scores[1][:, 0, :], ps_o[:, :]
            blend = {"r": wide[0], "k": wide[1]}
            k_act, gate, damp = wide[2], wide[3], {"r": wide[4], "k": wide[5]}

            with nc.Block() as block:
                @block.tensor
                def _(pe):
                    def body(g, par, ahead):
                        pe.wait_ge(blended.sem, blended.at(g, 4))
                        pe.wait_ge(relu_done.sem, relu_done.at(g, 0))
                        pe.matmul(bank_k, w_mix["k"][:, :], blend["k"][:, :], start=True, stop=True)\
                          .then_inc(rk_in_psum.sem, 1)
                        pe.wait_ge(sig.sem, sig.at(g, 0))
                        for u in range(GT):
                            last = pe.matmul(bank_r[:, u * P:(u + 1) * P], blend["r"][:, u * P:(u + 1) * P],
                                             w_mix["r"][:, :], start=True, stop=True)
                        last.then_inc(rk_in_psum.sem, 1)
                        pe.wait_ge(squared.sem, squared.at(g, 1))
                        pe.wait_ge(gated_v.sem, gated_v.at(g, 0))
                        for u in range(GT):
                            last = pe.matmul(bank_v[:, u * P:(u + 1) * P], k_act[:, u * P:(u + 1) * P],
                                             w_mix["v"][:, :], start=True, stop=True)
                        last.then_inc(v_done.sem, 1)
                        if ahead:
                            transpose_x(pe, g + 1)

                    transpose_x(pe, 0)
                    run_groups(pe, body)

                @block.scalar
                def _(act):
                    act.preload_act_table_set("sigmoid_and_others")

                    def body(g, par, ahead):
                        act.wait_ge(rk_in_psum.sem, rk_in_psum.at(g, 2))
                        act.wait_ge(added.sem, added.at(g, 0))
                        act.activation(gate[:, :], bank_r, ACT.Sigmoid).then_inc(sig.sem, 1)
                        if ahead:
                            copy_x_transposed(act, g + 1, 1 - par, blended, blended.at(g, 4))

                    copy_x_transposed(act, 0, 0, None, 0)
                    run_groups(act, body)

                @block.gpsimd
                def _(pool):
                    def body(g, par, ahead):
                        if ahead:
                            root(pool, g + 1)
                        pool.wait_ge(relu_done.sem, relu_done.at(g, 1))
                        pool.tensor_tensor(k_act[:, :], k_act[:, :], k_act[:, :], ALU.mult).then_inc(squared.sem, 1)

                    root(pool, 0)
                    run_groups(pool, body)

                @block.vector
                def _(dve):
                    def blend_rows(g, par):
                        dve.wait_ge(xt_ready.sem, xt_ready.at(g, 1))
                        dve.wait_ge(rk_in_psum.sem, rk_in_psum.at(g, 0))
                        n = q_t[par][:, :].rearrange("p (b t) -> p b t", t=S)
                        for c in "kr":
                            dve.tensor_scalar(damp[c][:, :], q_t[par][:, :], one_less_mu[c][:, 0:1], None, ALU.mult)\
                               .then_inc(damped.sem, 1)
                        dve.wait_ge(damped.sem, damped.at(g, 2))
                        for c in "kr":
                            b_ = blend[c][:, :].rearrange("p (b t) -> p b t", t=S)
                            d_ = damp[c][:, :].rearrange("p (b t) -> p b t", t=S)
                            dve.scalar_tensor_tensor(out=b_[:, :, 1:S], in0=n[:, :, 1:S], scalar=mu[c][:, 0:1],
                                                     in1=d_[:, :, 0:S - 1], op0=ALU.mult, op1=ALU.add)\
                               .then_inc(blended.sem, 1)
                            dve.tensor_scalar(b_[:, :, 0], n[:, :, 0], mu[c][:, 0:1], None, ALU.mult)\
                               .then_inc(blended.sem, 1)

                    def body(g, par, ahead):
                        if ahead:
                            norm_stats(dve, g + 1)
                        dve.wait_ge(rk_in_psum.sem, rk_in_psum.at(g, 1))
                        dve.wait_ge(v_done.sem, v_done.at(g, 0))
                        dve.tensor_scalar(k_act[:, :], bank_k, 0.0, None, ALU.max).then_inc(relu_done.sem, 1)
                        if ahead:
                            normalise(dve, g + 1)
                        dve.wait_ge(v_done.sem, v_done.at(g, 1))
                        dve.wait_ge(sig.sem, sig.at(g, 1))
                        dve.tensor_tensor(gate[:, :], gate[:, :], bank_v, ALU.mult).then_inc(gated_v.sem, 1)
                        dve.wait_ge(gated_v.sem, gated_v.at(g, 1))
                        flat = window_of(g)
                        dve.tensor_tensor(flat, gate[:, :], flat, ALU.add).then_inc(added.sem, 1)
                        if ahead:
                            blend_rows(g + 1, 1 - par)

                    for c in "rk":
                        dve.tensor_scalar(one_less_mu[c][:, :], mu[c][:, :], -1.0, 1.0, ALU.mult, ALU.add)\
                           .then_inc(mu_ready.sem, 1)
                    dve.wait_ge(mu_ready.sem, 2)
                    norm_stats(dve, 0)
                    normalise(dve, 0)
                    blend_rows(0, 0)
                    run_groups(dve, body)
            close_stage()

        shift_loaded = signal("shift_loaded")

        def move_shifted(sp, last=False):
            half = P // 2

            def load(g, par):
                rows = bass.ds(g * GT, GT)
                sp.dma_start(hi[par][:, :, 0:half], x[:, rows, 0:half]).then_inc(shift_loaded.sem, 16)
                for b in range(2):
                    sp.dma_start(hi[par][b * S + 1:(b + 1) * S, :, half:P],
                                 x[b * S:(b + 1) * S - 1, rows, half:P]).then_inc(shift_loaded.sem, 16)
                if last:
                    sp.dma_start(parked[par], out[:, rows, :]).then_inc(shift_loaded.sem, 16)

            def body(g, par, ahead):
                if ahead:
                    sp.wait_ge(xt_in_psum.sem, xt_in_psum.at(g, 1))
                    sp.sem_inc(sp_turn.sem, 1)
                    load(g + 1, 1 - par)

            sp.wait_ge(first_rows.sem, 4)
            load(0, 0)
            run_groups(sp, body)

        result_out = signal("result_out")
        first_rows = signal("first_rows")
        tables = signal("tables")

        def prepare_layers():
            with nc.Block() as block:
                @block.gpsimd
                def _(pool):
                    for i in range(2):
                        for b in range(2):
                            pool.memset(hi[i][b * S:b * S + 1, :, P // 2:P], 0.0).then_inc(first_rows.sem, 1)

                @block.vector
                def _(dve):
                    for i in range(2):
                        dve.memset(v_pair[i], 0.0).then_inc(tables.sem, 1)
                    dve.memset(k_pair, 0.0).then_inc(tables.sem, 1)
                    for l in range(DEPTH):
                        for a in range(2):
                            sc = rot_scale[:, l, a, :]
                            dve.tensor_tensor(rot[l][:, 2 * a, :], rot_base[:, 2 * a, :], sc, ALU.mult)\
                               .then_inc(tables.sem, 1)
                            for lo, hi_ in ((0, HALF), (HALF, 0)):
                                dve.tensor_tensor(rot[l][:, 2 * a + 1, lo:lo + HALF],
                                                  rot_base[:, 2 * a + 1, lo:lo + HALF],
                                                  sc[:, hi_:hi_ + HALF], ALU.mult).then_inc(tables.sem, 1)

        parked = [t[:, :].rearrange("p (u c) -> p u c", u=GT) for t in (k_t, x_norm_t)]

        def normalise_residual():
            in_out = signal("in_out")
            all_stats = signal("all_stats")
            all_chain = signal("all_chain")
            all_root = signal("all_root")
            centred = signal("centred")
            scaled = signal("scaled")
            bn_all = wide[0][:, 0:TILES * 6].rearrange("p (t s) -> p t s", s=6)
            mean_, gap_, dev_, log_, root_, work_ = (wide[1][:, i * TILES:(i + 1) * TILES] for i in range(6))
            front, back = slice(0, TILES * 5 // 8), slice(TILES * 5 // 8, TILES)

            with nc.Block() as block:
                @block.sync
                def _(sp):
                    sp.dma_start(out, x[:, :, :]).then_inc(in_out.sem, 16)
                    sp.wait_ge(in_out.sem, 16)

                @block.scalar
                def _(act):
                    act.preload_act_table_set(LN_EXP)
                    act.wait_ge(all_chain.sem, 7)
                    act.activation(log_, dev_, ACT.Ln).then_inc(all_root.sem, 1)
                    act.wait_ge(all_root.sem, 1)
                    act.activation(root_, log_, ACT.Exp, scale=-0.5).then_inc(all_root.sem, 1)

                @block.gpsimd
                def _(pool):
                    tiles = x[:, back, :]
                    shape = [P, back.stop - back.start, P]
                    pool.wait_ge(in_out.sem, 16)
                    pool.wait_ge(all_chain.sem, 4)
                    pool.tensor_tensor(tiles, tiles, mean_[:, back].unsqueeze(2).broadcast_to(shape), ALU.subtract)\
                        .then_inc(centred.sem, 1)
                    pool.wait_ge(centred.sem, 1)
                    pool.wait_ge(all_chain.sem, 11)
                    pool.tensor_tensor(tiles, tiles, root_[:, back].unsqueeze(2).broadcast_to(shape), ALU.mult)\
                        .then_inc(centred.sem, 1)

                @block.vector
                def _(dve):
                    with dve.Fori(0, GROUPS) as g:
                        for i in range(GT):
                            dve.bn_stats(bn_all[:, bass.ds(g * GT + i, 1), :].rearrange("p a s -> p (a s)"),
                                         x[:, bass.ds(g * GT + i, 1), :].rearrange("p a c -> p (a c)"))\
                               .then_inc(all_stats.sem, 1)
                    step = Steps(dve, all_chain, 0)
                    dve.wait_ge(all_stats.sem, TILES)
                    step(dve.tensor_tensor(mean_, bn_all[:, :, 1], bn_all[:, :, 4], ALU.add))
                    step(dve.tensor_tensor(gap_, bn_all[:, :, 1], bn_all[:, :, 4], ALU.subtract))
                    step(dve.tensor_tensor(dev_, bn_all[:, :, 2], bn_all[:, :, 5], ALU.add))
                    step(dve.tensor_scalar(mean_, mean_, 0.5, None, ALU.mult))
                    step(dve.tensor_tensor(gap_, gap_, gap_, ALU.mult))
                    step(dve.tensor_scalar(dev_, dev_, 1.0 / P, LN_EPS, ALU.mult, ALU.add))
                    step(dve.scalar_tensor_tensor(out=dev_, in0=gap_, scalar=0.25, in1=dev_, op0=ALU.mult,
                                                  op1=ALU.add))
                    tiles = x[:, front, :]
                    shape = [P, front.stop, P]
                    dve.wait_ge(in_out.sem, 16)
                    dve.tensor_tensor(tiles, tiles, mean_[:, front].unsqueeze(2).broadcast_to(shape), ALU.subtract)\
                       .then_inc(scaled.sem, 1)
                    dve.wait_ge(all_root.sem, 2)
                    step(dve.tensor_tensor(work_, root_, root_, ALU.mult))
                    step(dve.tensor_tensor(work_, work_, dev_, ALU.mult))
                    step(dve.tensor_scalar(work_, work_, -0.5, 1.5, ALU.mult, ALU.add))
                    step(dve.tensor_tensor(root_, root_, work_, ALU.mult))
                    dve.wait_ge(scaled.sem, 1)
                    dve.tensor_tensor(tiles, tiles, root_[:, front].unsqueeze(2).broadcast_to(shape), ALU.mult)\
                       .then_inc(scaled.sem, 1)
            close_stage()

        def local_attention(l):
            open_front(GT, norm=False)
            shift_loaded.opens(3 * 16)
            qk_in_psum = signal("qk_in_psum", 2 * GT)
            v_in_psum = signal("lv_in_psum", GT)
            squared = signal("l_squared", 2 * GT)
            norms = signal("norms", 3 * GT)
            l_root = signal("l_root", 2 * GT)
            l_newton = signal("l_newton", 4 * GT)
            products = signal("products", 6 * GT)
            rotated = signal("rotated", 2 * GT)
            unit = signal("unit", 2 * GT)
            qk_turned = signal("qk_turned", 2 * GT)
            q_copied = signal("q_copied", GT)
            k_copied = signal("k_copied", 2 * GT)
            v_copied = signal("v_copied", 4 * GT)
            scored = signal("scored", GT)
            max_ready = signal("max_ready", GT)
            shifted = signal("shifted", GT)
            exp_ready = signal("exp_ready", GT)
            sums_ready = signal("sums_ready", GT)
            rec_ready = signal("rec_ready", GT)
            turned = signal("turned", GT)
            pt_copied = signal("pt_ready", GT)
            summed = signal("summed", GT)
            o_ready = signal("o_ready", GT)
            ot_in_psum = signal("ot_in_psum", GT)
            ot_copied = signal("ot_ready", GT)
            y_ready = signal("y_ready", GT)

            bank_qk = [ps_scores[0][:, i, :] for i in range(2)]
            bank_v = ps_scores[1]
            bank_s, bank_t = ps_pt[:, 0, :], ps_pt[:, 1, :]
            sq = [wide[0], wide[1]]
            qt, kp = big["qt"], k_pair
            pl, pt, o_, ot = big["pl"], big["pt"], big["o"], big["ot"]
            nrm, nlog, nroot, nwork, nstep = (norm8[n] for n in "abcde")

            with nc.Block() as block:
                @block.sync
                def _(sp):
                    move_shifted(sp)

                @block.tensor
                def _(pe):
                    def transpose_window(g, par):
                        pe.wait_ge(shift_loaded.sem, shift_loaded.at(g, 48))
                        for u in range(GT):
                            last = pe.transpose(ps_pj[:, u * P:(u + 1) * P], hi[par][:, u, :], ident[:, :])
                        last.then_inc(xt_in_psum.sem, 1)

                    def project_qk(g, n, par):
                        h = q_t[(par + n // GT) % 2][:, n % GT * P:(n % GT + 1) * P]
                        if n % GT == 0:
                            pe.wait_ge(xt_ready.sem, xt_ready.at(g + n // GT, 1))
                        pe.wait_ge(products.sem, products.at(g, 6 * n))
                        for i in range(2):
                            pe.matmul(bank_qk[i], h, w_qkv[l][:, i * INNER:(i + 1) * INNER],
                                      start=True, stop=True).then_inc(qk_in_psum.sem, 1)

                    def project_v(g, n, par, first=False):
                        h = q_t[(par + n // GT) % 2][:, n % GT * P:(n % GT + 1) * P]
                        if not first:
                            pe.wait_ge(v_copied.sem, v_copied.at(g, 4 * n - 4))
                        pe.matmul(bank_v[:, n % 2, :], h, w_qkv[l][:, 2 * INNER:3 * INNER], start=True, stop=True)\
                          .then_inc(v_in_psum.sem, 1)

                    def turn_qk(g, n):
                        pe.wait_ge(unit.sem, unit.at(g, 2 * n + 1))
                        for r in range(LPAIRS):
                            last = pe.transpose(ps_pj[:, r * P:(r + 1) * P], part[n % 2][0][0][:, r * P:(r + 1) * P],
                                                ident[:, :])
                        last.then_inc(qk_turned.sem, 1)
                        pe.wait_ge(unit.sem, unit.at(g, 2 * n + 2))
                        for r in range(LPAIRS):
                            last = pe.transpose(bank_s[:, r * P:(r + 1) * P], part[n % 2][1][0][:, r * P:(r + 1) * P],
                                                ident[:, :])
                        last.then_inc(qk_turned.sem, 1)

                    def scores(g, n):
                        pe.wait_ge(q_copied.sem, q_copied.at(g, n + 1))
                        pe.wait_ge(k_copied.sem, k_copied.at(g, 2 * n + 2))
                        pe.matmul(bank_s.rearrange("p (h k) -> p h k", k=S), ident_16[:, :],
                                  masks["causal"][:, :].unsqueeze(1).broadcast_to([P, LHEADS, S]),
                                  start=True, stop=False, skip_group_check=True)
                        for r in range(LPAIRS):
                            for b in range(2):
                                last = pe.matmul(bank_s[b * S:(b + 1) * S, r * P:(r + 1) * P],
                                                 qt[:, r * P + b * S:r * P + (b + 1) * S],
                                                 kp[:, r, b, :, :].rearrange("p j k -> p (j k)"),
                                                 start=False, stop=True, skip_group_check=True)
                        last.then_inc(scored.sem, 1)

                    def turn_probs(g, u):
                        pe.wait_ge(exp_ready.sem, exp_ready.at(g, u + 1))
                        pe.wait_ge(ot_copied.sem, ot_copied.at(g, u))
                        for r in range(LPAIRS):
                            last = pe.transpose(bank_t[:, r * P:(r + 1) * P], pl[:, r * P:(r + 1) * P], ident[:, :])
                        last.then_inc(turned.sem, 1)

                    def weigh_values(g, u):
                        pe.wait_ge(pt_copied.sem, pt_copied.at(g, u + 1))
                        pe.wait_ge(v_copied.sem, v_copied.at(g, 4 * u + 4))
                        pe.wait_ge(o_ready.sem, o_ready.at(g, u))
                        for r in range(LPAIRS):
                            for b in range(2):
                                last = pe.matmul(ps_o[b * S:(b + 1) * S, r * P:(r + 1) * P],
                                                 pt[:, r * P + b * S:r * P + (b + 1) * S],
                                                 v_pair[u % 2][:, b, r, :, :].rearrange("p j d -> p (j d)"),
                                                 start=True, stop=True)
                        last.then_inc(summed.sem, 1)

                    def turn_o(g, u):
                        pe.wait_ge(o_ready.sem, o_ready.at(g, u + 1))
                        for r in range(LPAIRS):
                            last = pe.transpose(bank_t[:, r * P:(r + 1) * P], o_[:, r * P:(r + 1) * P], ident[:, :])
                        last.then_inc(ot_in_psum.sem, 1)

                    def project_o(g, u):
                        pe.wait_ge(ot_copied.sem, ot_copied.at(g, u + 1))
                        pe.wait_ge(added.sem, added.at(g, u))
                        for r in range(LPAIRS):
                            last = pe.matmul(ps_pj[:, 0:P], ot[:, r * P:(r + 1) * P], w_lo[l][:, r, :],
                                             start=r == 0, stop=r == LPAIRS - 1)
                        last.then_inc(y_ready.sem, 1)

                    def body(g, par, ahead):
                        for u in range(GT):
                            if ahead or u + 2 < GT:
                                project_qk(g, u + 2, par)
                            pe.wait_ge(added.sem, added.at(g, u))
                            if ahead and u == 1:
                                transpose_window(g + 1, 1 - par)
                            turn_probs(g, u)
                            if ahead and u == 1:
                                pe.wait_ge(xt_ready.sem, xt_ready.at(g + 1, 1))
                            if ahead or u + 1 < GT:
                                turn_qk(g, u + 1)
                            weigh_values(g, u)
                            if ahead or u + 2 < GT:
                                project_v(g, u + 2, par)
                            turn_o(g, u)
                            if ahead or u + 1 < GT:
                                scores(g, u + 1)
                            project_o(g, u)

                    pe.wait_ge(tables.sem, 3 + 6 * DEPTH)
                    transpose_window(0, 0)
                    for n in range(2):
                        project_qk(0, n, 0)
                        project_v(0, n, 0, True)
                    turn_qk(0, 0)
                    scores(0, 0)
                    run_groups(pe, body)

                @block.scalar
                def _(act):
                    act.preload_act_table_set(LN_EXP)

                    def copy_window(g, par, first):
                        act.wait_ge(xt_in_psum.sem, xt_in_psum.at(g, 1))
                        if not first:
                            act.wait_ge(v_in_psum.sem, v_in_psum.at(g - 1, 0))
                        act.activation(q_t[par][:, :], ps_pj[:, :], ACT.Copy).then_inc(xt_ready.sem, 1)

                    def squares(g, n, i):
                        act.wait_ge(qk_in_psum.sem, qk_in_psum.at(g, 2 * n + i + 1))
                        act.wait_ge(norms.sem, norms.at(g, 3 * n))
                        act.activation(sq[i][:, :], bank_qk[i], ACT.Square).then_inc(squared.sem, 1)

                    def roots(g, n):
                        act.wait_ge(norms.sem, norms.at(g, 3 * n + 3))
                        act.activation(nlog, nrm, ACT.Ln).then_inc(l_root.sem, 1)
                        act.wait_ge(l_root.sem, l_root.at(g, 2 * n + 1))
                        act.wait_ge(unit.sem, unit.at(g, 2 * n))
                        act.activation(nroot, nlog, ACT.Exp, scale=-0.5).then_inc(l_root.sem, 1)

                    def copy_v(g, n, first):
                        act.wait_ge(v_in_psum.sem, v_in_psum.at(g, n + 1))
                        if not first:
                            act.wait_ge(summed.sem, summed.at(g, n - 1))
                        for b in range(2):
                            src = bank_v[b * S:(b + 1) * S, n % 2, :].rearrange("p (r j d) -> p r j d", r=LPAIRS, j=2)
                            for j in range(2):
                                act.activation(v_pair[n % 2][j * S:(j + 1) * S, b, :, j, :], src[:, :, j, :], ACT.Copy)\
                                   .then_inc(v_copied.sem, 1)

                    def copy_qk(g, n):
                        act.wait_ge(qk_turned.sem, qk_turned.at(g, 2 * n + 1))
                        act.wait_ge(scored.sem, scored.at(g, n))
                        act.activation(qt[:, :], ps_pj[:, :], ACT.Copy).then_inc(q_copied.sem, 1)
                        act.wait_ge(qk_turned.sem, qk_turned.at(g, 2 * n + 2))
                        for j in range(2):
                            rows = slice(j * S, (j + 1) * S)
                            act.activation(kp[rows, :, :, j, :],
                                           bank_s[rows, :].rearrange("p (r b k) -> p r b k", r=LPAIRS, b=2),
                                           ACT.Copy).then_inc(k_copied.sem, 1)

                    def exponentials(g, u):
                        act.wait_ge(shifted.sem, shifted.at(g, u + 1))
                        act.activation(pl[:, :], pl[:, :], ACT.Exp, scale=8.0).then_inc(exp_ready.sem, 1)

                    def copy_pt(g, u):
                        act.wait_ge(turned.sem, turned.at(g, u + 1))
                        act.wait_ge(summed.sem, summed.at(g, u))
                        act.activation(pt[:, :], bank_t[:, :], ACT.Copy).then_inc(pt_copied.sem, 1)

                    def copy_ot(g, u):
                        act.wait_ge(ot_in_psum.sem, ot_in_psum.at(g, u + 1))
                        act.wait_ge(y_ready.sem, y_ready.at(g, u))
                        act.activation(ot[:, :], bank_t[:, :], ACT.Copy).then_inc(ot_copied.sem, 1)

                    def body(g, par, ahead):
                        for u in range(GT):
                            two = ahead or u + 2 < GT
                            if two:
                                squares(g, u + 2, 0)
                            exponentials(g, u)
                            if two:
                                squares(g, u + 2, 1)
                            if ahead and u == 1:
                                copy_window(g + 1, 1 - par, False)
                            copy_pt(g, u)
                            if ahead or u + 1 < GT:
                                copy_qk(g, u + 1)
                            if two:
                                roots(g, u + 2)
                            copy_ot(g, u)
                            if two:
                                copy_v(g, u + 2, False)

                    copy_window(0, 0, True)
                    for n in range(2):
                        for i in range(2):
                            squares(0, n, i)
                        copy_v(0, n, True)
                        roots(0, n)
                    copy_qk(0, 0)
                    run_groups(act, body)

                @block.gpsimd
                def _(pool):
                    def unite(g, n):
                        def add(i):
                            a, b_ = part[n % 2][i][0][:, :], part[n % 2][i][1][:, :]
                            pool.wait_ge(products.sem, products.at(g, 6 * n + 3 * i + 3))
                            pool.tensor_tensor(a, a, b_, ALU.add).then_inc(rotated.sem, 1)

                        add(0)
                        step = Steps(pool, l_newton, g, 4 * n)
                        pool.wait_ge(l_root.sem, l_root.at(g, 2 * n + 2))
                        step(pool.tensor_tensor(nstep, nroot, nroot, ALU.mult))
                        step(pool.tensor_tensor(nstep, nstep, nrm, ALU.mult))
                        pool.sem_inc(pool_turn.sem, 1)
                        step(pool.tensor_scalar(nstep, nstep, -0.5, 1.5, ALU.mult, ALU.add))
                        step(pool.tensor_tensor(nroot, nroot, nstep, ALU.mult))
                        for i in range(2):
                            if i:
                                add(1)
                            pool.wait_ge(rotated.sem, rotated.at(g, 2 * n + i + 1))
                            a = part[n % 2][i][0][:, :].rearrange("p (h d) -> p h d", d=LD)
                            pool.tensor_tensor(a, a, nroot[:, i, :].unsqueeze(2).broadcast_to([P, LHEADS, LD]),
                                               ALU.mult).then_inc(unit.sem, 1)

                    def body(g, par, ahead):
                        for u in range(GT):
                            if ahead or u + 2 < GT:
                                unite(g, u + 2)

                    unite(0, 0)
                    unite(0, 1)
                    run_groups(pool, body)

                @block.vector
                def _(dve):
                    def rotate(g, n, i, first):
                        src = bank_qk[i].rearrange("p (h d) -> p h d", d=LD)
                        a, b_ = (part[n % 2][i][m][:, :].rearrange("p (h d) -> p h d", d=LD) for m in range(2))

                        def table(m, lo, width):
                            return rot[l][:, m, lo:lo + width].unsqueeze(1).broadcast_to([P, LHEADS, width])

                        dve.wait_ge(squared.sem, squared.at(g, 2 * n + i + 1))
                        if not first:
                            dve.wait_ge(qk_turned.sem, qk_turned.at(g, 2 * n - 2))
                        dve.tensor_tensor(a, src, table(2 * i, 0, LD), ALU.mult).then_inc(products.sem, 1)
                        dve.tensor_tensor(b_[:, :, 0:HALF], src[:, :, HALF:LD], table(2 * i + 1, 0, HALF),
                                          ALU.mult).then_inc(products.sem, 1)
                        dve.tensor_tensor(b_[:, :, HALF:LD], src[:, :, 0:HALF], table(2 * i + 1, HALF, HALF),
                                          ALU.mult).then_inc(products.sem, 1)

                    def sum_squares(g, n, i):
                        dve.wait_ge(squared.sem, squared.at(g, 2 * n + i + 1))
                        dve.tensor_reduce(nwork[:, i, :], sq[i][:, :].rearrange("p (h d) -> p h d", d=LD),
                                          AX, ALU.add).then_inc(norms.sem, 1)

                    def clip(g, n):
                        dve.wait_ge(norms.sem, norms.at(g, 3 * n + 2))
                        dve.wait_ge(l_newton.sem, l_newton.at(g, 4 * n))
                        dve.tensor_scalar(nrm, nwork, 1e-24, float(2 ** LOG_SCALE), ALU.max, ALU.mult)\
                           .then_inc(norms.sem, 1)

                    def softmax(g, u):
                        p3 = pl[:, :].rearrange("p (h k) -> p h k", k=S)
                        s3 = bank_s.rearrange("p (h k) -> p h k", k=S)
                        dve.wait_ge(scored.sem, scored.at(g, u + 1))
                        dve.tensor_reduce(row_max[0][:, 0:LHEADS], s3, AX, ALU.max).then_inc(max_ready.sem, 1)
                        dve.wait_ge(max_ready.sem, max_ready.at(g, u + 1))
                        dve.wait_ge(turned.sem, turned.at(g, u))
                        dve.tensor_tensor(p3, s3, row_max[0][:, 0:LHEADS].unsqueeze(2).broadcast_to([P, LHEADS, S]),
                                          ALU.subtract).then_inc(shifted.sem, 1)

                    def sums(g, u):
                        dve.wait_ge(exp_ready.sem, exp_ready.at(g, u + 1))
                        dve.tensor_reduce(row_max[1][:, 0:LHEADS], pl[:, :].rearrange("p (h k) -> p h k", k=S),
                                          AX, ALU.add).then_inc(sums_ready.sem, 1)
                        dve.wait_ge(sums_ready.sem, sums_ready.at(g, u + 1))
                        dve.reciprocal(row_max[1][:, 0:LHEADS], row_max[1][:, 0:LHEADS]).then_inc(rec_ready.sem, 1)

                    def divide(g, u):
                        dve.wait_ge(summed.sem, summed.at(g, u + 1))
                        dve.wait_ge(rec_ready.sem, rec_ready.at(g, u + 1))
                        dve.wait_ge(ot_in_psum.sem, ot_in_psum.at(g, u))
                        dve.tensor_tensor(o_[:, :].rearrange("p (h d) -> p h d", d=LD),
                                          ps_o[:, :].rearrange("p (h d) -> p h d", d=LD),
                                          row_max[1][:, 0:LHEADS].unsqueeze(2).broadcast_to([P, LHEADS, LD]),
                                          ALU.mult).then_inc(o_ready.sem, 1)

                    def residual(g, u):
                        dve.wait_ge(y_ready.sem, y_ready.at(g, u + 1))
                        dve.tensor_tensor(tile_of(g, u), tile_of(g, u), ps_pj[:, 0:P], ALU.add)\
                           .then_inc(added.sem, 1)

                    def body(g, par, ahead):
                        for u in range(GT):
                            two = ahead or u + 2 < GT
                            softmax(g, u)
                            if u:
                                residual(g, u - 1)
                            if two:
                                rotate(g, u + 2, 0, False)
                            sums(g, u)
                            if two:
                                sum_squares(g, u + 2, 0)
                                sum_squares(g, u + 2, 1)
                                clip(g, u + 2)
                            divide(g, u)
                            if two:
                                rotate(g, u + 2, 1, False)
                        residual(g, GT - 1)

                    for n in range(2):
                        for i in range(2):
                            rotate(0, n, i, True)
                            sum_squares(0, n, i)
                        clip(0, n)
                    run_groups(dve, body)
            close_stage()

        def gated_mlp(l):
            NC = len(HC)
            open_front(1, root_on_pool=True)
            last = l == DEPTH - 1
            shift_loaded.opens(4 * 16 if last else 3 * 16)
            g_in_psum = signal("g_in_psum", NC)
            a_in_psum = signal("a_in_psum", NC)
            gelu_done = signal("gelu_done", NC)
            gated = signal("gated", NC)
            y_done = signal("y_done", 1)
            unparked = signal("unparked", 1 if last else 0)
            bank_g = [ps_scores[i][:, 0, :] for i in range(2)]
            bank_a = [ps_scores[i][:, 1, :] for i in range(2)]

            with nc.Block() as block:
                @block.sync
                def _(sp):
                    move_shifted(sp, last)

                @block.tensor
                def _(pe):
                    def body(g, par, ahead):
                        pe.wait_ge(xt_ready.sem, xt_ready.at(g, 1))
                        for c, (at, m) in enumerate(HC):
                            pe.wait_ge(gated.sem, gated.at(g, max(c - 1, 0)))
                            pe.matmul(bank_g[c % 2][0:m, :], w_up1[l][:, HID + at:HID + at + m], q_t[par][:, :],
                                      start=True, stop=True).then_inc(g_in_psum.sem, 1)
                            pe.matmul(bank_a[c % 2][0:m, :], w_up1[l][:, at:at + m], q_t[par][:, :],
                                      start=True, stop=True).then_inc(a_in_psum.sem, 1)
                        if ahead:
                            transpose_x(pe, g + 1)
                        pe.wait_ge(added.sem, added.at(g, 0))
                        for c, (at, m) in enumerate(HC):
                            pe.wait_ge(gated.sem, gated.at(g, c + 1))
                            for u in range(GT):
                                pe.matmul(ps_o[:, u * P:(u + 1) * P], wide[c][0:m, u * P:(u + 1) * P],
                                          w_dn[l][0:m, c, :], start=c == 0 and u == 0, stop=False,
                                          skip_group_check=True)
                        for u in range(GT):
                            last = pe.matmul(ps_o[:, u * P:(u + 1) * P], ones[:, :], b_dn[l][:, :], start=False,
                                             stop=True, skip_group_check=True)
                        last.then_inc(y_done.sem, 1)

                    transpose_x(pe, 0)
                    run_groups(pe, body)

                @block.scalar
                def _(act):
                    act.preload_act_table_set("gelu_and_others")

                    def copy_normed(g, par, wait_use):
                        act.wait_ge(xt_in_psum.sem, xt_in_psum.at(g, 1))
                        if wait_use:
                            act.wait_ge(a_in_psum.sem, a_in_psum.at(g - 1, 0))
                        act.activation(q_t[par][:, :], ps_pj[:, :], ACT.Identity, scale=ln_gb[l][:, 0:1],
                                       bias=ln_gb[l][:, 1:2]).then_inc(xt_ready.sem, 1)

                    def body(g, par, ahead):
                        for c, (at, m) in enumerate(HC):
                            act.wait_ge(g_in_psum.sem, g_in_psum.at(g, c + 1))
                            act.wait_ge(y_done.sem, y_done.at(g, 0))
                            act.activation(wide[3 + c][0:m, :], bank_g[c % 2][0:m, :], ACT.Gelu,
                                           bias=b_up1[l][0:m, NC + c:NC + c + 1]).then_inc(gelu_done.sem, 1)
                        if ahead:
                            copy_normed(g + 1, 1 - par, True)

                    copy_normed(0, 0, False)
                    run_groups(act, body)

                @block.gpsimd
                def _(pool):
                    def body(g, par, ahead):
                        if ahead:
                            root(pool, g + 1)
                        if last:
                            pool.wait_ge(added.sem, added.at(g, 1))
                            pool.sem_inc(pool_turn.sem, 1)
                            rows = bass.ds(g * GT, GT)
                            pool.dma_start(out[:, rows, :], x[:, rows, :]).then_inc(result_out.sem, 16)

                    root(pool, 0)
                    run_groups(pool, body)
                    if last:
                        pool.wait_ge(result_out.sem, 16 * GROUPS)

                @block.vector
                def _(dve):
                    def body(g, par, ahead):
                        if ahead:
                            dve.wait_ge(shift_loaded.sem, shift_loaded.at(g + 1, shift_loaded.per))
                            norm_stats(dve, g + 1, hi[1 - par])
                        flat = window_of(g)
                        if last:
                            dve.tensor_tensor(flat, flat, parked[par].rearrange("p u c -> p (u c)"), ALU.add)\
                               .then_inc(unparked.sem, 1)
                        for c, (at, m) in enumerate(HC):
                            dve.wait_ge(a_in_psum.sem, a_in_psum.at(g, c + 1))
                            dve.wait_ge(gelu_done.sem, gelu_done.at(g, c + 1))
                            dve.wait_ge(y_done.sem, y_done.at(g, 0))
                            dve.scalar_tensor_tensor(out=wide[c][0:m, :], in0=bank_a[c % 2][0:m, :],
                                                     scalar=b_up1[l][0:m, c:c + 1], in1=wide[3 + c][0:m, :],
                                                     op0=ALU.add, op1=ALU.mult).then_inc(gated.sem, 1)
                            if ahead and c == 0:
                                normalise(dve, g + 1, hi[1 - par])
                        dve.wait_ge(y_done.sem, y_done.at(g, 1))
                        if last:
                            dve.wait_ge(unparked.sem, unparked.at(g, 1))
                        dve.tensor_tensor(flat, ps_o[:, :], flat, ALU.add).then_inc(added.sem, 1)

                    dve.wait_ge(shift_loaded.sem, shift_loaded.at(0, shift_loaded.per))
                    norm_stats(dve, 0, hi[0])
                    normalise(dve, 0, hi[0])
                    run_groups(dve, body)
            close_stage()

        flat_big = kblk[0][:, :, :].rearrange("p h t -> p (h t)")
        big = {n: flat_big[:, i * 512:(i + 1) * 512] for i, n in enumerate(("qt", "pl", "pt", "o", "ot"))}
        k_pair = flat_big[:, 2560:2560 + 1024].rearrange("p (r b j k) -> p r b j k", r=LPAIRS, b=2, j=2)
        v_pair = [flat_big[:, 3584 + i * 1024:3584 + (i + 1) * 1024]
                  .rearrange("p (b r j d) -> p b r j d", r=LPAIRS, b=2, j=2) for i in range(2)]
        flat_parts = kblk[1][:, :, :].rearrange("p h t -> p (h t)")
        part = [[[flat_parts[:, k * 512:(k + 1) * 512] for k in (4 * m + 2 * i, 4 * m + 2 * i + 1)]
                 for i in range(2)] for m in range(2)]
        norm8 = {n: small[n][:, 0, :].rearrange("p (i h) -> p i h", i=2) for n in "abcde"}

        mu_ready = signal("mu_ready")

        def wait_for_late_loads():
            with nc.Block() as block:
                @block.sync
                def _(sp):
                    sp.wait_ge(loaded_late.sem, 16 * len(late_loads))

        cross_attention("L0", 1.0 / np.sqrt(HD))
        wait_for_late_loads()
        prepare_low_rank()
        low_rank_experts()
        cross_attention("L1", 1.0 / np.sqrt(HD), mask=masks["L1"])
        mixture()
        cross_attention("L2", 1.0, mask_per_seq=mask_l2, project=False, relu=True)
        channel_mix()
        cross_attention("L3", 1.0 / np.sqrt(HD), mask=masks["L3"])
        prepare_layers()
        normalise_residual()
        for l in range(DEPTH):
            local_attention(l)
            gated_mlp(l)


def rotary_tables():
    half = np.arange(0, LD, 2, dtype=np.float32)
    t = np.arange(S, dtype=np.float32)
    freqs = t[:, None] * (np.float32(1) / np.float32(10000) ** (half / np.float32(LD)))[None, :]
    freqs = np.concatenate([freqs, freqs], axis=1)
    base = (half + np.float32(0.4 * LD)) / np.float32(1.4 * LD)
    scale = base[None, :] ** ((t - S // 2) / np.float32(S // 2))[:, None]
    scale = np.concatenate([scale, scale], axis=1)
    sign = np.where(np.arange(LD) < HALF, -1.0, 1.0).astype(np.float32)
    cos, sin, up = np.cos(freqs), np.sin(freqs) * sign, np.float32(2 ** (LOG_SCALE // 2))
    t4 = np.stack([cos * scale * up, sin * scale * up, cos / scale * up, sin / scale * up], axis=1)
    return np.concatenate([t4, t4]).astype(np.float32)


def columns(b):
    out = np.zeros((DEPTH, P, 2 * len(HC)), b.dtype)
    for i in range(2):
        for c, (at, m) in enumerate(HC):
            out[:, :m, i * len(HC) + c] = b[:, i, at:at + m]
    return out


def chunks(w2):
    out = np.zeros((DEPTH, P, len(HC), P), w2.dtype)
    for c, (at, m) in enumerate(HC):
        out[:, :m, c, :] = w2[:, at:at + m, :]
    return out


def kernel(**inputs):
    import concourse.bacc as bacc
    from concourse.bass_utils import run_bass_kernel_spmd

    a = {k: np.asarray(v) for k, v in inputs.items()}

    def row(v):
        return v.reshape(1, -1)

    arrays = {
        "x_in": a["x"].reshape(TILES, P, P).transpose(1, 0, 2),
        "ctx_t": a["ctx_1024"].reshape(TILES * P, P).T,
        "mask_l2": a["mask_Bx1xSxS2_ff0"].reshape(TILES, P, S).transpose(1, 0, 2),
        "mask_l3": a["mask_SxS2_bk1"],
        "L0_q": a["L0_xattn_w_q"].T, "L0_k": a["L0_xattn_w_k"].T,
        "L0_v": a["L0_xattn_w_v"].T, "L0_o": a["L0_xattn_w_o"].T,
        "L1_q": a["L1_xattn_Wq"].T, "L1_k": a["L1_xattn_Wk"].T,
        "L1_v": a["L1_xattn_Wv"].T, "L1_o": a["L1_xattn_Wo"].T,
        "L2_o": a["L2_xattn_wo_w"].T,
        "L3_q": a["L3_xattn_Wq"], "L3_k": a["L3_xattn_Wk"],
        "L3_v": a["L3_xattn_Wv"], "L3_o": a["L3_xattn_Wo"],
        "bL1_v": a["L1_xattn_bv"].reshape(P, 1), "bL1_o": row(a["L1_xattn_bo"]), "bL2_o": row(a["L2_xattn_wo_b"]),
        "bL3_v": a["L3_xattn_bv"].reshape(P, 1), "bL3_o": row(a["L3_xattn_bo"]),
        "low_W": a["L0_ffn_W"].T, "low_Wp": a["L0_ffn_Wp"], "low_WpT": a["L0_ffn_Wp"].T,
        "low_sim": a["L0_ffn_sim"], "low_bp": a["L0_ffn_bp"].reshape(-1, 1),
        "low_temp": np.broadcast_to(a["L0_ffn_temp"].reshape(1, 1), (P, 1)),
        "low_Wd": np.concatenate([a[f"L0_ffn_Wd{i}"] for i in range(NLR)]).T,
        "low_Wu": np.concatenate([a[f"L0_ffn_Wu{i}"] for i in range(NLR)], axis=1).T,
        "moe_gate": a["L1_ffn_gate_w"].T,
        "moe_1": a["L1_ffn_w1"].transpose(1, 0, 2), "moe_3": a["L1_ffn_w3"].transpose(1, 0, 2),
        "moe_2": a["L1_ffn_w2"].reshape(EC, P, P).transpose(1, 0, 2),
        "mix_r": a["L2_ffn_W_r"].T, "mix_k": a["L2_ffn_W_k"].T, "mix_v": a["L2_ffn_W_v"].T,
        "mu_r": a["L2_ffn_mu_r"].reshape(P, 1), "mu_k": a["L2_ffn_mu_k"].reshape(P, 1),
        "rot": rotary_tables(), "rot_scale": np.broadcast_to(
            np.stack([a["L3_ffn_q_scale"], a["L3_ffn_k_scale"]], axis=1), (P, DEPTH, 2, LD)),
        "wqkv": a["L3_ffn_wqkv"], "lo": a["L3_ffn_wo"].reshape(DEPTH, LPAIRS, P, P).transpose(0, 2, 1, 3),
        "up1": a["L3_ffn_w1"], "b_up1": columns(a["L3_ffn_b1"].reshape(DEPTH, 2, HID)),
        "dn": chunks(a["L3_ffn_w2"]), "b_dn": a["L3_ffn_b2"].reshape(DEPTH, 1, P),
        "ln": np.stack([a["L3_ffn_ln_g"], a["L3_ffn_ln_b"]], axis=2),
        "bL3_q": a["L3_xattn_bq"].reshape(P, 1), "bL3_k": a["L3_xattn_bk"].reshape(P, 1),
    }
    nc = bacc.Bacc("TRN2", target_bir_lowering=False, num_devices=1)
    feed, args = {}, {}
    for name, v in arrays.items():
        v = np.ascontiguousarray(v)
        feed["in_" + name] = v
        args[name] = nc.dram_tensor("in_" + name, v.shape, mybir.dt.from_np(v.dtype), kind="ExternalInput").ap()
    out = nc.dram_tensor("out", (P, TILES, P), F32, kind="ExternalOutput").ap()
    main = {n: args.pop(n) for n in ("x_in", "ctx_t", "mask_l2", "mask_l3")}
    build_program(nc, args, main["x_in"], main["ctx_t"], main["mask_l2"], main["mask_l3"], out)
    r = run_bass_kernel_spmd(nc, [feed], core_ids=[0])
    return r.results[0]["out"].transpose(1, 0, 2).reshape(NSEQ, S, P)
```
